# Optimizing a Trainium2 kernel written in Bass

```python
import numpy as np
import jax
import jax.numpy as jnp

def _softmax(x, axis=-1):
    return jax.nn.softmax(x, axis=axis)

def _gelu(x):
    return jax.nn.gelu(x, approximate=True)

def _silu(x):
    return jax.nn.silu(x)

def _sigmoid(x):
    return jax.nn.sigmoid(x)

def _layernorm(x, axis=-1, eps=1e-05):
    m = jnp.mean(x, axis=axis, keepdims=True)
    v = jnp.var(x, axis=axis, keepdims=True)
    return (x - m) / jnp.sqrt(v + eps)

def _scatter_add(tgt, idx, src, axis=0):
    return tgt.at[idx].add(src)

def _segment_sum(src, seg, n):
    return jax.ops.segment_sum(src, seg, n)
kernel_name = 'mk_xattn_seq_d4_seqx_r8_d173a5'

def setup_inputs(seed: int=0):
    np.random.seed(seed)
    _w = jnp.asarray

    def _rec_inputs():
        import jax
        import jax.numpy as jnp
        _rk = jax.random.key(seed)
        x = -0.0003929 + 0.9999 * jax.random.normal(jax.random.fold_in(_rk, 1), (4, 256, 256), jnp.float32)
        _lenS = 256 - jax.random.randint(jax.random.fold_in(_rk, 7), (4,), 0, max(1, 256 // 4) + 1, jnp.int32)
        _lenS2 = 256 - jax.random.randint(jax.random.fold_in(_rk, 8), (4,), 0, max(1, 256 // 4) + 1, jnp.int32)
        _ctx_2048P = jax.random.normal(jax.random.fold_in(_rk, 11), (4, 16, 256), jnp.float32)
        _ctx_2048c = jax.random.dirichlet(jax.random.fold_in(_rk, 511), 0.3 * jnp.ones((16,), jnp.float32), (4, 256))
        _ctx_2048t = jnp.einsum('bsk,bkd->bsd', _ctx_2048c, _ctx_2048P)
        _ctx_2048t = _ctx_2048t * jax.lax.rsqrt(jnp.mean(jnp.square(_ctx_2048t)) + 1e-12) * 0.953939
        ctx_2048 = -8.57375e-05 + 0.999917 * (_ctx_2048t + 0.3 * jax.random.normal(jax.random.fold_in(_rk, 611), (4, 256, 256), jnp.float32))
        _validS = jnp.arange(256)[None, :] < _lenS[:, None]
        _validS2 = jnp.arange(256)[None, :] < _lenS2[:, None]
        _causal = jnp.tril(jnp.ones((256, 256), dtype=bool))
        mask_BxS2_bf1 = jnp.ones((4, 256), dtype=bool)
        mask_Bx1xSxS2_ff0 = jnp.where(jnp.ones((4, 1, 256, 256), dtype=bool), 0.0, -1000000000.0).astype(jnp.float32)
        return (x, ctx_2048, mask_BxS2_bf1, mask_Bx1xSxS2_ff0)
    x, ctx_2048, mask_BxS2_bf1, mask_Bx1xSxS2_ff0 = _rec_inputs()

    def _L0_xattn_setup():
        import jax, jax.numpy as jnp
        import numpy as np
        HIDDEN = 256
        HEADS = 16
        HEAD_DIM = HIDDEN // HEADS
        LN_EPS = 1e-05
        GATE_INIT = 0.5

        def _layer_norm(x, gamma, beta):
            mu = jnp.mean(x, axis=-1, keepdims=True)
            var = jnp.mean(jnp.square(x - mu), axis=-1, keepdims=True)
            return (x - mu) * jax.lax.rsqrt(var + LN_EPS) * gamma + beta
        key = jax.random.key(seed)
        ks = jax.random.split(key, 8)
        B, T_TEXT, T_AUDIO = (4, 256, 1500)
        s = 0.02
        return {'hidden_states': jax.random.normal(ks[0], (B, T_TEXT, HIDDEN), jnp.float32), 'audio_kv': jax.random.normal(ks[1], (B, T_AUDIO, HIDDEN), jnp.float32), 'audio_attention_mask': jnp.ones((B, T_AUDIO), dtype=bool), 'Wq': jax.random.normal(ks[2], (HIDDEN, HIDDEN), jnp.float32) * s, 'Wk': jax.random.normal(ks[3], (HIDDEN, HIDDEN), jnp.float32) * s, 'Wv': jax.random.normal(ks[4], (HIDDEN, HIDDEN), jnp.float32) * s, 'Wo': jax.random.normal(ks[5], (HIDDEN, HIDDEN), jnp.float32) * s, 'ln_gamma': jnp.ones((HIDDEN,), jnp.float32), 'ln_beta': jnp.zeros((HIDDEN,), jnp.float32), 'gate': jnp.array([GATE_INIT], jnp.float32)}
    _L0_xattn_all = _L0_xattn_setup()
    _L0_xattn_in = {k: v for k, v in _L0_xattn_all.items() if k in ('Wq', 'Wk', 'Wv', 'Wo', 'ln_gamma', 'ln_beta', 'gate')}
    del _L0_xattn_all

    def _L1_xattn_setup():
        import jax, jax.numpy as jnp
        import numpy as np
        N_HEAD = 32
        EPS = 1e-05

        def _ln(x, w, b):
            m = jnp.mean(x, axis=-1, keepdims=True)
            v = jnp.mean((x - m) ** 2, axis=-1, keepdims=True)
            return (x - m) * jax.lax.rsqrt(v + EPS) * w + b

        def _forward(x, state, i, ln1_w, ln1_b, ln2_w, ln2_b, maa_x, maa_w, maa_k, maa_v, maa_r, maa_g, maa_w1, maa_w2, time_decay, decay_w1, decay_w2, faaaa, Wr, Wk, Wv, Wg, Wo, gn_w, gn_b, fmaa_k, fmaa_r, fWk, fWr, fWv):
            B, L, C = x.shape
            H = N_HEAD
            S = C // H
            i0 = (2 + S) * i
            xa = _ln(x, ln1_w, ln1_b)
            sx = jnp.concatenate([state[:, i0 + 1][:, None], xa[:, :-1]], axis=1) - xa
            xxx = xa + sx * maa_x
            t = jnp.tanh(xxx @ maa_w1).reshape(B, L, 5, -1)
            m = jnp.einsum('blfd,fdc->blfc', t, maa_w2)
            mw, mk, mv, mr, mg = (m[:, :, j] for j in range(5))
            xw = xa + sx * (maa_w + mw)
            xk = xa + sx * (maa_k + mk)
            xv = xa + sx * (maa_v + mv)
            xr = xa + sx * (maa_r + mr)
            xg = xa + sx * (maa_g + mg)
            w = time_decay + jnp.tanh(xw @ decay_w1) @ decay_w2
            w = jnp.exp(-jnp.exp(w)).reshape(B, L, H, S)
            r = (xr @ Wr.T).reshape(B, L, H, S)
            k = (xk @ Wk.T).reshape(B, L, H, S)
            v = (xv @ Wv.T).reshape(B, L, H, S)
            g = jax.nn.silu(xg @ Wg.T)
            s0 = state[:, i0 + 2:i0 + 2 + S].reshape(B, H, S, S)

            def step(s, inp):
                k_l, v_l, w_l, r_l = inp
                a = k_l[..., :, None] * v_l[..., None, :]
                out = jnp.einsum('bhs,bhst->bht', r_l, faaaa * a + s)
                s_new = a + w_l[..., None] * s
                return (s_new, out)
            seq = tuple((z.transpose(1, 0, 2, 3) for z in (k, v, w, r)))
            _, outs = jax.lax.scan(step, s0, seq)
            y = outs.transpose(1, 0, 2, 3)
            gm = jnp.mean(y, axis=-1, keepdims=True)
            gv = jnp.mean((y - gm) ** 2, axis=-1, keepdims=True)
            y = ((y - gm) * jax.lax.rsqrt(gv + EPS)).reshape(B, L, C) * gn_w + gn_b
            x = x + y * g @ Wo.T
            xc = _ln(x, ln2_w, ln2_b)
            sxc = jnp.concatenate([state[:, i0][:, None], xc[:, :-1]], axis=1) - xc
            xk2 = xc + sxc * fmaa_k
            xr2 = xc + sxc * fmaa_r
            rr = jax.nn.sigmoid(xr2 @ fWr.T)
            kk = jnp.square(jax.nn.relu(xk2 @ fWk.T))
            x = x + rr * (kk @ fWv.T)
            return x
        key = jax.random.key(seed)
        B, L, C, H = (8, 64, 256, N_HEAD)
        S = C // H
        DM, DD = (32, 64)
        ks = jax.random.split(key, 32)
        n = lambda k, shp, s=1.0: jax.random.normal(k, shp, dtype=jnp.float32) * s
        u = lambda k, shp: jax.random.uniform(k, shp, dtype=jnp.float32)
        inp = {'x': n(ks[0], (B, L, C)), 'state': n(ks[1], (B, 2 + S, C), 0.1), 'i': 0, 'ln1_w': jnp.ones((C,), jnp.float32), 'ln1_b': jnp.zeros((C,), jnp.float32), 'ln2_w': jnp.ones((C,), jnp.float32), 'ln2_b': jnp.zeros((C,), jnp.float32), 'maa_x': u(ks[2], (C,)), 'maa_w': u(ks[3], (C,)), 'maa_k': u(ks[4], (C,)), 'maa_v': u(ks[5], (C,)), 'maa_r': u(ks[6], (C,)), 'maa_g': u(ks[7], (C,)), 'maa_w1': n(ks[8], (C, 5 * DM), 0.02), 'maa_w2': n(ks[9], (5, DM, C), 0.02), 'time_decay': n(ks[10], (C,), 0.5), 'decay_w1': n(ks[11], (C, DD), 0.02), 'decay_w2': n(ks[12], (DD, C), 0.02), 'faaaa': n(ks[13], (H, S, 1), 0.1), 'Wr': n(ks[14], (C, C), 0.02), 'Wk': n(ks[15], (C, C), 0.02), 'Wv': n(ks[16], (C, C), 0.02), 'Wg': n(ks[17], (C, C), 0.02), 'Wo': n(ks[18], (C, C), 0.02), 'gn_w': jnp.ones((C,), jnp.float32), 'gn_b': jnp.zeros((C,), jnp.float32), 'fmaa_k': u(ks[19], (C,)), 'fmaa_r': u(ks[20], (C,)), 'fWk': n(ks[21], (C, C), 0.02), 'fWr': n(ks[22], (C, C), 0.02), 'fWv': n(ks[23], (C, C), 0.02)}
        return inp
    _L1_xattn_all = _L1_xattn_setup()
    _L1_xattn_in = {k: v for k, v in _L1_xattn_all.items() if k in ('ln1_w', 'ln1_b', 'ln2_w', 'ln2_b', 'maa_x', 'maa_w', 'maa_k', 'maa_v', 'maa_r', 'maa_g', 'maa_w1', 'maa_w2', 'time_decay', 'decay_w1', 'decay_w2', 'faaaa', 'Wr', 'Wk', 'Wv', 'Wg', 'Wo', 'gn_w', 'gn_b', 'fmaa_k', 'fmaa_r', 'fWk', 'fWr', 'fWv')}
    del _L1_xattn_all

    def _L2_xattn_setup():
        import jax, jax.numpy as jnp
        import numpy as np
        H = 256
        NH = 32
        KVH = 8
        HD = H // NH
        GROUPS = NH // KVH
        EPS = 1e-06
        B, L, S = (4, 128, 128)

        def _gqa_forward(hidden_state, encoder_hidden_state, encoder_attention_mask, Wq, bq, Wk, bk, Wv, bv, Wo, bo, gamma, beta):
            b, l, _ = hidden_state.shape
            s = encoder_hidden_state.shape[1]
            q = hidden_state @ Wq + bq
            k = encoder_hidden_state @ Wk + bk
            v = encoder_hidden_state @ Wv + bv
            q = q.reshape(b, l, KVH, GROUPS, HD).transpose(0, 2, 3, 1, 4)
            k = k.reshape(b, s, KVH, HD).transpose(0, 2, 1, 3)
            v = v.reshape(b, s, KVH, HD).transpose(0, 2, 1, 3)
            scale = 1.0 / jnp.sqrt(jnp.asarray(HD, q.dtype))
            scores = jnp.einsum('bkgld,bksd->bkgls', q, k) * scale
            scores = scores + encoder_attention_mask[:, :, None, :, :]
            attn = jax.nn.softmax(scores, axis=-1)
            out = jnp.einsum('bkgls,bksd->bkgld', attn, v)
            out = out.transpose(0, 3, 1, 2, 4).reshape(b, l, H)
            out = out @ Wo + bo
            x = out + hidden_state
            mu = jnp.mean(x, axis=-1, keepdims=True)
            var = jnp.var(x, axis=-1, keepdims=True)
            return (x - mu) * jax.lax.rsqrt(var + EPS) * gamma + beta
        key = jax.random.key(seed)
        ks = jax.random.split(key, 12)
        sd = 0.02
        return {'hidden_state': jax.random.normal(ks[0], (B, L, H), jnp.float32), 'encoder_hidden_state': jax.random.normal(ks[1], (B, S, H), jnp.float32), 'encoder_attention_mask': jnp.zeros((B, 1, L, S), jnp.float32), 'Wq': jax.random.normal(ks[2], (H, H), jnp.float32) * sd, 'bq': jnp.zeros((H,), jnp.float32), 'Wk': jax.random.normal(ks[3], (H, KVH * HD), jnp.float32) * sd, 'bk': jnp.zeros((KVH * HD,), jnp.float32), 'Wv': jax.random.normal(ks[4], (H, KVH * HD), jnp.float32) * sd, 'bv': jnp.zeros((KVH * HD,), jnp.float32), 'Wo': jax.random.normal(ks[5], (H, H), jnp.float32) * sd, 'bo': jnp.zeros((H,), jnp.float32), 'gamma': jnp.ones((H,), jnp.float32), 'beta': jnp.zeros((H,), jnp.float32)}
    _L2_xattn_all = _L2_xattn_setup()
    _L2_xattn_in = {k: v for k, v in _L2_xattn_all.items() if k in ('Wq', 'bq', 'Wk', 'bk', 'Wv', 'bv', 'Wo', 'bo', 'gamma', 'beta')}
    del _L2_xattn_all

    def _L3_xattn_setup():
        import jax, jax.numpy as jnp
        import numpy as np
        B, Q, S1, S2 = (4, 32, 256, 256)
        D, H, K, F = (256, 16, 128, 1024)
        LN_EPS = 1e-05

        def _layer_norm(x, scale, offset):
            mu = jnp.mean(x, axis=-1, keepdims=True)
            var = jnp.var(x, axis=-1, keepdims=True)
            return (x - mu) * jax.lax.rsqrt(var + LN_EPS) * scale + offset

        def _cross_attention(q_in, kv_in, wq, bq, wk, bk, wv, bv, wo, bo, bias_k, bias_v):
            b, q_len, _ = q_in.shape
            t = kv_in.shape[1]
            qh = (q_in @ wq + bq).reshape(b, q_len, H, K)
            kh = (kv_in @ wk + bk).reshape(b, t, H, K)
            vh = (kv_in @ wv + bv).reshape(b, t, H, K)
            kh = jnp.concatenate([kh, jnp.broadcast_to(bias_k, (b, 1, H, K))], axis=1)
            vh = jnp.concatenate([vh, jnp.broadcast_to(bias_v, (b, 1, H, K))], axis=1)
            scale = jnp.sqrt(jnp.asarray(K, q_in.dtype))
            logits = jnp.einsum('bqhk,bthk->bhqt', qh, kh) / scale
            weights = jax.nn.softmax(logits, axis=-1)
            ctx = jnp.einsum('bhqt,bthk->bqhk', weights, vh).reshape(b, q_len, H * K)
            return ctx @ wo + bo

        def _forward(x, xf_1, xf_2, ln1_scale, ln1_offset, wq1, bq1, wk1, bk1, wv1, bv1, wo1, bo1, bias_k1, bias_v1, ln2_scale, ln2_offset, wq2, bq2, wk2, bk2, wv2, bv2, wo2, bo2, bias_k2, bias_v2, ln_mlp_scale, ln_mlp_offset, w_fc1, b_fc1, w_fc2, b_fc2):
            res = x
            h = _layer_norm(x, ln1_scale, ln1_offset)
            x = res + _cross_attention(h, xf_1, wq1, bq1, wk1, bk1, wv1, bv1, wo1, bo1, bias_k1, bias_v1)
            res = x
            h = _layer_norm(x, ln2_scale, ln2_offset)
            x = res + _cross_attention(h, xf_2, wq2, bq2, wk2, bk2, wv2, bv2, wo2, bo2, bias_k2, bias_v2)
            h = _layer_norm(x, ln_mlp_scale, ln_mlp_offset)
            h = jax.nn.gelu(h @ w_fc1 + b_fc1, approximate=False) @ w_fc2 + b_fc2
            return x + h
        key = jax.random.key(seed)
        ks = iter(jax.random.split(key, 64))

        def rn(shape, s=0.02):
            return jax.random.normal(next(ks), shape, jnp.float32) * s
        inp = {'x': rn((B, Q, D), 1.0), 'xf_1': rn((B, S1, D), 1.0), 'xf_2': rn((B, S2, D), 1.0)}
        for i in (1, 2):
            inp[f'ln{i}_scale'] = jnp.ones((D,), jnp.float32)
            inp[f'ln{i}_offset'] = jnp.zeros((D,), jnp.float32)
            inp[f'wq{i}'] = rn((D, H * K))
            inp[f'bq{i}'] = jnp.zeros((H * K,), jnp.float32)
            inp[f'wk{i}'] = rn((D, H * K))
            inp[f'bk{i}'] = jnp.zeros((H * K,), jnp.float32)
            inp[f'wv{i}'] = rn((D, H * K))
            inp[f'bv{i}'] = jnp.zeros((H * K,), jnp.float32)
            inp[f'wo{i}'] = rn((H * K, D))
            inp[f'bo{i}'] = jnp.zeros((D,), jnp.float32)
            inp[f'bias_k{i}'] = rn((1, 1, H, K))
            inp[f'bias_v{i}'] = rn((1, 1, H, K))
        inp['ln_mlp_scale'] = jnp.ones((D,), jnp.float32)
        inp['ln_mlp_offset'] = jnp.zeros((D,), jnp.float32)
        inp['w_fc1'] = rn((D, F))
        inp['b_fc1'] = jnp.zeros((F,), jnp.float32)
        inp['w_fc2'] = rn((F, D))
        inp['b_fc2'] = jnp.zeros((D,), jnp.float32)
        return inp
    _L3_xattn_all = _L3_xattn_setup()
    _L3_xattn_in = {k: v for k, v in _L3_xattn_all.items() if k in ('ln1_scale', 'ln1_offset', 'wq1', 'bq1', 'wk1', 'bk1', 'wv1', 'bv1', 'wo1', 'bo1', 'bias_k1', 'bias_v1', 'ln2_scale', 'ln2_offset', 'wq2', 'bq2', 'wk2', 'bk2', 'wv2', 'bv2', 'wo2', 'bo2', 'bias_k2', 'bias_v2', 'ln_mlp_scale', 'ln_mlp_offset', 'w_fc1', 'b_fc1', 'w_fc2', 'b_fc2')}
    del _L3_xattn_all
    return {'x': x, 'ctx_2048': ctx_2048, 'mask_BxS2_bf1': mask_BxS2_bf1, 'mask_Bx1xSxS2_ff0': mask_Bx1xSxS2_ff0, 'L0_xattn_Wq': _L0_xattn_in['Wq'], 'L0_xattn_Wk': _L0_xattn_in['Wk'], 'L0_xattn_Wv': _L0_xattn_in['Wv'], 'L0_xattn_Wo': _L0_xattn_in['Wo'], 'L0_xattn_ln_gamma': _L0_xattn_in['ln_gamma'], 'L0_xattn_ln_beta': _L0_xattn_in['ln_beta'], 'L0_xattn_gate': _L0_xattn_in['gate'], 'L1_xattn_ln1_w': _L1_xattn_in['ln1_w'], 'L1_xattn_ln1_b': _L1_xattn_in['ln1_b'], 'L1_xattn_ln2_w': _L1_xattn_in['ln2_w'], 'L1_xattn_ln2_b': _L1_xattn_in['ln2_b'], 'L1_xattn_maa_x': _L1_xattn_in['maa_x'], 'L1_xattn_maa_w': _L1_xattn_in['maa_w'], 'L1_xattn_maa_k': _L1_xattn_in['maa_k'], 'L1_xattn_maa_v': _L1_xattn_in['maa_v'], 'L1_xattn_maa_r': _L1_xattn_in['maa_r'], 'L1_xattn_maa_g': _L1_xattn_in['maa_g'], 'L1_xattn_maa_w1': _L1_xattn_in['maa_w1'], 'L1_xattn_maa_w2': _L1_xattn_in['maa_w2'], 'L1_xattn_time_decay': _L1_xattn_in['time_decay'], 'L1_xattn_decay_w1': _L1_xattn_in['decay_w1'], 'L1_xattn_decay_w2': _L1_xattn_in['decay_w2'], 'L1_xattn_faaaa': _L1_xattn_in['faaaa'], 'L1_xattn_Wr': _L1_xattn_in['Wr'], 'L1_xattn_Wk': _L1_xattn_in['Wk'], 'L1_xattn_Wv': _L1_xattn_in['Wv'], 'L1_xattn_Wg': _L1_xattn_in['Wg'], 'L1_xattn_Wo': _L1_xattn_in['Wo'], 'L1_xattn_gn_w': _L1_xattn_in['gn_w'], 'L1_xattn_gn_b': _L1_xattn_in['gn_b'], 'L1_xattn_fmaa_k': _L1_xattn_in['fmaa_k'], 'L1_xattn_fmaa_r': _L1_xattn_in['fmaa_r'], 'L1_xattn_fWk': _L1_xattn_in['fWk'], 'L1_xattn_fWr': _L1_xattn_in['fWr'], 'L1_xattn_fWv': _L1_xattn_in['fWv'], 'L2_xattn_Wq': _L2_xattn_in['Wq'], 'L2_xattn_bq': _L2_xattn_in['bq'], 'L2_xattn_Wk': _L2_xattn_in['Wk'], 'L2_xattn_bk': _L2_xattn_in['bk'], 'L2_xattn_Wv': _L2_xattn_in['Wv'], 'L2_xattn_bv': _L2_xattn_in['bv'], 'L2_xattn_Wo': _L2_xattn_in['Wo'], 'L2_xattn_bo': _L2_xattn_in['bo'], 'L2_xattn_gamma': _L2_xattn_in['gamma'], 'L2_xattn_beta': _L2_xattn_in['beta'], 'L3_xattn_ln1_scale': _L3_xattn_in['ln1_scale'], 'L3_xattn_ln1_offset': _L3_xattn_in['ln1_offset'], 'L3_xattn_wq1': _L3_xattn_in['wq1'], 'L3_xattn_bq1': _L3_xattn_in['bq1'], 'L3_xattn_wk1': _L3_xattn_in['wk1'], 'L3_xattn_bk1': _L3_xattn_in['bk1'], 'L3_xattn_wv1': _L3_xattn_in['wv1'], 'L3_xattn_bv1': _L3_xattn_in['bv1'], 'L3_xattn_wo1': _L3_xattn_in['wo1'], 'L3_xattn_bo1': _L3_xattn_in['bo1'], 'L3_xattn_bias_k1': _L3_xattn_in['bias_k1'], 'L3_xattn_bias_v1': _L3_xattn_in['bias_v1'], 'L3_xattn_ln2_scale': _L3_xattn_in['ln2_scale'], 'L3_xattn_ln2_offset': _L3_xattn_in['ln2_offset'], 'L3_xattn_wq2': _L3_xattn_in['wq2'], 'L3_xattn_bq2': _L3_xattn_in['bq2'], 'L3_xattn_wk2': _L3_xattn_in['wk2'], 'L3_xattn_bk2': _L3_xattn_in['bk2'], 'L3_xattn_wv2': _L3_xattn_in['wv2'], 'L3_xattn_bv2': _L3_xattn_in['bv2'], 'L3_xattn_wo2': _L3_xattn_in['wo2'], 'L3_xattn_bo2': _L3_xattn_in['bo2'], 'L3_xattn_bias_k2': _L3_xattn_in['bias_k2'], 'L3_xattn_bias_v2': _L3_xattn_in['bias_v2'], 'L3_xattn_ln_mlp_scale': _L3_xattn_in['ln_mlp_scale'], 'L3_xattn_ln_mlp_offset': _L3_xattn_in['ln_mlp_offset'], 'L3_xattn_w_fc1': _L3_xattn_in['w_fc1'], 'L3_xattn_b_fc1': _L3_xattn_in['b_fc1'], 'L3_xattn_w_fc2': _L3_xattn_in['w_fc2'], 'L3_xattn_b_fc2': _L3_xattn_in['b_fc2']}

def reference(x, ctx_2048, mask_BxS2_bf1, mask_Bx1xSxS2_ff0, L0_xattn_Wq, L0_xattn_Wk, L0_xattn_Wv, L0_xattn_Wo, L0_xattn_ln_gamma, L0_xattn_ln_beta, L0_xattn_gate, L1_xattn_ln1_w, L1_xattn_ln1_b, L1_xattn_ln2_w, L1_xattn_ln2_b, L1_xattn_maa_x, L1_xattn_maa_w, L1_xattn_maa_k, L1_xattn_maa_v, L1_xattn_maa_r, L1_xattn_maa_g, L1_xattn_maa_w1, L1_xattn_maa_w2, L1_xattn_time_decay, L1_xattn_decay_w1, L1_xattn_decay_w2, L1_xattn_faaaa, L1_xattn_Wr, L1_xattn_Wk, L1_xattn_Wv, L1_xattn_Wg, L1_xattn_Wo, L1_xattn_gn_w, L1_xattn_gn_b, L1_xattn_fmaa_k, L1_xattn_fmaa_r, L1_xattn_fWk, L1_xattn_fWr, L1_xattn_fWv, L2_xattn_Wq, L2_xattn_bq, L2_xattn_Wk, L2_xattn_bk, L2_xattn_Wv, L2_xattn_bv, L2_xattn_Wo, L2_xattn_bo, L2_xattn_gamma, L2_xattn_beta, L3_xattn_ln1_scale, L3_xattn_ln1_offset, L3_xattn_wq1, L3_xattn_bq1, L3_xattn_wk1, L3_xattn_bk1, L3_xattn_wv1, L3_xattn_bv1, L3_xattn_wo1, L3_xattn_bo1, L3_xattn_bias_k1, L3_xattn_bias_v1, L3_xattn_ln2_scale, L3_xattn_ln2_offset, L3_xattn_wq2, L3_xattn_bq2, L3_xattn_wk2, L3_xattn_bk2, L3_xattn_wv2, L3_xattn_bv2, L3_xattn_wo2, L3_xattn_bo2, L3_xattn_bias_k2, L3_xattn_bias_v2, L3_xattn_ln_mlp_scale, L3_xattn_ln_mlp_offset, L3_xattn_w_fc1, L3_xattn_b_fc1, L3_xattn_w_fc2, L3_xattn_b_fc2):
    import jax
    import jax.numpy as jnp

    def _L0_xattn_ref(hidden_states, audio_kv, audio_attention_mask, Wq, Wk, Wv, Wo, ln_gamma, ln_beta, gate):
        import jax, jax.numpy as jnp
        import numpy as np
        HIDDEN = 256
        HEADS = 16
        HEAD_DIM = HIDDEN // HEADS
        LN_EPS = 1e-05
        GATE_INIT = 0.5

        def _layer_norm(x, gamma, beta):
            mu = jnp.mean(x, axis=-1, keepdims=True)
            var = jnp.mean(jnp.square(x - mu), axis=-1, keepdims=True)
            return (x - mu) * jax.lax.rsqrt(var + LN_EPS) * gamma + beta
        B, Tt, D = hidden_states.shape
        Ta = audio_kv.shape[1]
        scale = HEAD_DIM ** (-0.5)
        a = _layer_norm(audio_kv, ln_gamma, ln_beta)
        Q = (hidden_states @ Wq.T).reshape(B, Tt, HEADS, HEAD_DIM).transpose(0, 2, 1, 3)
        K = (a @ Wk.T).reshape(B, Ta, HEADS, HEAD_DIM).transpose(0, 2, 1, 3)
        V = (a @ Wv.T).reshape(B, Ta, HEADS, HEAD_DIM).transpose(0, 2, 1, 3)
        scores = jnp.einsum('bhtd,bhsd->bhts', Q, K) * scale
        mask = audio_attention_mask[:, None, None, :]
        scores = jnp.where(mask, scores, jnp.float32(-jnp.inf))
        attn = jax.nn.softmax(scores, axis=-1)
        out = jnp.einsum('bhts,bhsd->bhtd', attn, V)
        out = out.transpose(0, 2, 1, 3).reshape(B, Tt, D)
        out = out @ Wo.T
        return hidden_states + jnp.tanh(gate) * out

    def _L1_xattn_ref(x, state, i, ln1_w, ln1_b, ln2_w, ln2_b, maa_x, maa_w, maa_k, maa_v, maa_r, maa_g, maa_w1, maa_w2, time_decay, decay_w1, decay_w2, faaaa, Wr, Wk, Wv, Wg, Wo, gn_w, gn_b, fmaa_k, fmaa_r, fWk, fWr, fWv):
        import jax, jax.numpy as jnp
        import numpy as np
        N_HEAD = 32
        EPS = 1e-05

        def _ln(x, w, b):
            m = jnp.mean(x, axis=-1, keepdims=True)
            v = jnp.mean((x - m) ** 2, axis=-1, keepdims=True)
            return (x - m) * jax.lax.rsqrt(v + EPS) * w + b

        def _forward(x, state, i, ln1_w, ln1_b, ln2_w, ln2_b, maa_x, maa_w, maa_k, maa_v, maa_r, maa_g, maa_w1, maa_w2, time_decay, decay_w1, decay_w2, faaaa, Wr, Wk, Wv, Wg, Wo, gn_w, gn_b, fmaa_k, fmaa_r, fWk, fWr, fWv):
            B, L, C = x.shape
            H = N_HEAD
            S = C // H
            i0 = (2 + S) * i
            xa = _ln(x, ln1_w, ln1_b)
            sx = jnp.concatenate([state[:, i0 + 1][:, None], xa[:, :-1]], axis=1) - xa
            xxx = xa + sx * maa_x
            t = jnp.tanh(xxx @ maa_w1).reshape(B, L, 5, -1)
            m = jnp.einsum('blfd,fdc->blfc', t, maa_w2)
            mw, mk, mv, mr, mg = (m[:, :, j] for j in range(5))
            xw = xa + sx * (maa_w + mw)
            xk = xa + sx * (maa_k + mk)
            xv = xa + sx * (maa_v + mv)
            xr = xa + sx * (maa_r + mr)
            xg = xa + sx * (maa_g + mg)
            w = time_decay + jnp.tanh(xw @ decay_w1) @ decay_w2
            w = jnp.exp(-jnp.exp(w)).reshape(B, L, H, S)
            r = (xr @ Wr.T).reshape(B, L, H, S)
            k = (xk @ Wk.T).reshape(B, L, H, S)
            v = (xv @ Wv.T).reshape(B, L, H, S)
            g = jax.nn.silu(xg @ Wg.T)
            s0 = state[:, i0 + 2:i0 + 2 + S].reshape(B, H, S, S)

            def step(s, inp):
                k_l, v_l, w_l, r_l = inp
                a = k_l[..., :, None] * v_l[..., None, :]
                out = jnp.einsum('bhs,bhst->bht', r_l, faaaa * a + s)
                s_new = a + w_l[..., None] * s
                return (s_new, out)
            seq = tuple((z.transpose(1, 0, 2, 3) for z in (k, v, w, r)))
            _, outs = jax.lax.scan(step, s0, seq)
            y = outs.transpose(1, 0, 2, 3)
            gm = jnp.mean(y, axis=-1, keepdims=True)
            gv = jnp.mean((y - gm) ** 2, axis=-1, keepdims=True)
            y = ((y - gm) * jax.lax.rsqrt(gv + EPS)).reshape(B, L, C) * gn_w + gn_b
            x = x + y * g @ Wo.T
            xc = _ln(x, ln2_w, ln2_b)
            sxc = jnp.concatenate([state[:, i0][:, None], xc[:, :-1]], axis=1) - xc
            xk2 = xc + sxc * fmaa_k
            xr2 = xc + sxc * fmaa_r
            rr = jax.nn.sigmoid(xr2 @ fWr.T)
            kk = jnp.square(jax.nn.relu(xk2 @ fWk.T))
            x = x + rr * (kk @ fWv.T)
            return x
        return _forward(x, state, i, ln1_w, ln1_b, ln2_w, ln2_b, maa_x, maa_w, maa_k, maa_v, maa_r, maa_g, maa_w1, maa_w2, time_decay, decay_w1, decay_w2, faaaa, Wr, Wk, Wv, Wg, Wo, gn_w, gn_b, fmaa_k, fmaa_r, fWk, fWr, fWv)

    def _L2_xattn_ref(hidden_state, encoder_hidden_state, encoder_attention_mask, Wq, bq, Wk, bk, Wv, bv, Wo, bo, gamma, beta):
        import jax, jax.numpy as jnp
        import numpy as np
        H = 256
        NH = 32
        KVH = 8
        HD = H // NH
        GROUPS = NH // KVH
        EPS = 1e-06
        B, L, S = (4, 128, 128)

        def _gqa_forward(hidden_state, encoder_hidden_state, encoder_attention_mask, Wq, bq, Wk, bk, Wv, bv, Wo, bo, gamma, beta):
            b, l, _ = hidden_state.shape
            s = encoder_hidden_state.shape[1]
            q = hidden_state @ Wq + bq
            k = encoder_hidden_state @ Wk + bk
            v = encoder_hidden_state @ Wv + bv
            q = q.reshape(b, l, KVH, GROUPS, HD).transpose(0, 2, 3, 1, 4)
            k = k.reshape(b, s, KVH, HD).transpose(0, 2, 1, 3)
            v = v.reshape(b, s, KVH, HD).transpose(0, 2, 1, 3)
            scale = 1.0 / jnp.sqrt(jnp.asarray(HD, q.dtype))
            scores = jnp.einsum('bkgld,bksd->bkgls', q, k) * scale
            scores = scores + encoder_attention_mask[:, :, None, :, :]
            attn = jax.nn.softmax(scores, axis=-1)
            out = jnp.einsum('bkgls,bksd->bkgld', attn, v)
            out = out.transpose(0, 3, 1, 2, 4).reshape(b, l, H)
            out = out @ Wo + bo
            x = out + hidden_state
            mu = jnp.mean(x, axis=-1, keepdims=True)
            var = jnp.var(x, axis=-1, keepdims=True)
            return (x - mu) * jax.lax.rsqrt(var + EPS) * gamma + beta
        return _gqa_forward(hidden_state, encoder_hidden_state, encoder_attention_mask, Wq, bq, Wk, bk, Wv, bv, Wo, bo, gamma, beta)

    def _L3_xattn_ref(x, xf_1, xf_2, ln1_scale, ln1_offset, wq1, bq1, wk1, bk1, wv1, bv1, wo1, bo1, bias_k1, bias_v1, ln2_scale, ln2_offset, wq2, bq2, wk2, bk2, wv2, bv2, wo2, bo2, bias_k2, bias_v2, ln_mlp_scale, ln_mlp_offset, w_fc1, b_fc1, w_fc2, b_fc2):
        import jax, jax.numpy as jnp
        import numpy as np
        B, Q, S1, S2 = (4, 32, 256, 256)
        D, H, K, F = (256, 16, 128, 1024)
        LN_EPS = 1e-05

        def _layer_norm(x, scale, offset):
            mu = jnp.mean(x, axis=-1, keepdims=True)
            var = jnp.var(x, axis=-1, keepdims=True)
            return (x - mu) * jax.lax.rsqrt(var + LN_EPS) * scale + offset

        def _cross_attention(q_in, kv_in, wq, bq, wk, bk, wv, bv, wo, bo, bias_k, bias_v):
            b, q_len, _ = q_in.shape
            t = kv_in.shape[1]
            qh = (q_in @ wq + bq).reshape(b, q_len, H, K)
            kh = (kv_in @ wk + bk).reshape(b, t, H, K)
            vh = (kv_in @ wv + bv).reshape(b, t, H, K)
            kh = jnp.concatenate([kh, jnp.broadcast_to(bias_k, (b, 1, H, K))], axis=1)
            vh = jnp.concatenate([vh, jnp.broadcast_to(bias_v, (b, 1, H, K))], axis=1)
            scale = jnp.sqrt(jnp.asarray(K, q_in.dtype))
            logits = jnp.einsum('bqhk,bthk->bhqt', qh, kh) / scale
            weights = jax.nn.softmax(logits, axis=-1)
            ctx = jnp.einsum('bhqt,bthk->bqhk', weights, vh).reshape(b, q_len, H * K)
            return ctx @ wo + bo

        def _forward(x, xf_1, xf_2, ln1_scale, ln1_offset, wq1, bq1, wk1, bk1, wv1, bv1, wo1, bo1, bias_k1, bias_v1, ln2_scale, ln2_offset, wq2, bq2, wk2, bk2, wv2, bv2, wo2, bo2, bias_k2, bias_v2, ln_mlp_scale, ln_mlp_offset, w_fc1, b_fc1, w_fc2, b_fc2):
            res = x
            h = _layer_norm(x, ln1_scale, ln1_offset)
            x = res + _cross_attention(h, xf_1, wq1, bq1, wk1, bk1, wv1, bv1, wo1, bo1, bias_k1, bias_v1)
            res = x
            h = _layer_norm(x, ln2_scale, ln2_offset)
            x = res + _cross_attention(h, xf_2, wq2, bq2, wk2, bk2, wv2, bv2, wo2, bo2, bias_k2, bias_v2)
            h = _layer_norm(x, ln_mlp_scale, ln_mlp_offset)
            h = jax.nn.gelu(h @ w_fc1 + b_fc1, approximate=False) @ w_fc2 + b_fc2
            return x + h
        return _forward(x, xf_1, xf_2, ln1_scale, ln1_offset, wq1, bq1, wk1, bk1, wv1, bv1, wo1, bo1, bias_k1, bias_v1, ln2_scale, ln2_offset, wq2, bq2, wk2, bk2, wv2, bv2, wo2, bo2, bias_k2, bias_v2, ln_mlp_scale, ln_mlp_offset, w_fc1, b_fc1, w_fc2, b_fc2)
    x = _L0_xattn_ref(x, ctx_2048, mask_BxS2_bf1, L0_xattn_Wq, L0_xattn_Wk, L0_xattn_Wv, L0_xattn_Wo, L0_xattn_ln_gamma, L0_xattn_ln_beta, L0_xattn_gate)
    x = _L1_xattn_ref(x, ctx_2048, 0, L1_xattn_ln1_w, L1_xattn_ln1_b, L1_xattn_ln2_w, L1_xattn_ln2_b, L1_xattn_maa_x, L1_xattn_maa_w, L1_xattn_maa_k, L1_xattn_maa_v, L1_xattn_maa_r, L1_xattn_maa_g, L1_xattn_maa_w1, L1_xattn_maa_w2, L1_xattn_time_decay, L1_xattn_decay_w1, L1_xattn_decay_w2, L1_xattn_faaaa, L1_xattn_Wr, L1_xattn_Wk, L1_xattn_Wv, L1_xattn_Wg, L1_xattn_Wo, L1_xattn_gn_w, L1_xattn_gn_b, L1_xattn_fmaa_k, L1_xattn_fmaa_r, L1_xattn_fWk, L1_xattn_fWr, L1_xattn_fWv)
    x = _L2_xattn_ref(x, ctx_2048, mask_Bx1xSxS2_ff0, L2_xattn_Wq, L2_xattn_bq, L2_xattn_Wk, L2_xattn_bk, L2_xattn_Wv, L2_xattn_bv, L2_xattn_Wo, L2_xattn_bo, L2_xattn_gamma, L2_xattn_beta)
    x = _L3_xattn_ref(x, ctx_2048, ctx_2048, L3_xattn_ln1_scale, L3_xattn_ln1_offset, L3_xattn_wq1, L3_xattn_bq1, L3_xattn_wk1, L3_xattn_bk1, L3_xattn_wv1, L3_xattn_bv1, L3_xattn_wo1, L3_xattn_bo1, L3_xattn_bias_k1, L3_xattn_bias_v1, L3_xattn_ln2_scale, L3_xattn_ln2_offset, L3_xattn_wq2, L3_xattn_bq2, L3_xattn_wk2, L3_xattn_bk2, L3_xattn_wv2, L3_xattn_bv2, L3_xattn_wo2, L3_xattn_bo2, L3_xattn_bias_k2, L3_xattn_bias_v2, L3_xattn_ln_mlp_scale, L3_xattn_ln_mlp_offset, L3_xattn_w_fc1, L3_xattn_b_fc1, L3_xattn_w_fc2, L3_xattn_b_fc2)
    return x

_drawn_inputs = setup_inputs


def setup_inputs(seed=0):
    import zlib

    import numpy as np

    out = dict(_drawn_inputs(seed))
    spreads = {'L0_xattn_ln_gamma': (1.0, 0.6),
     'L0_xattn_ln_beta': (0.0, 0.8),
     'L1_xattn_ln1_w': (1.0, 0.6),
     'L1_xattn_ln1_b': (0.0, 0.584),
     'L1_xattn_ln2_w': (1.0, 0.6),
     'L1_xattn_ln2_b': (0.0, 0.8),
     'L1_xattn_gn_w': (1.0, 0.6),
     'L1_xattn_gn_b': (0.0, 0.8),
     'L2_xattn_bq': (0.0, 2.0),
     'L2_xattn_bk': (0.0, 2.0),
     'L2_xattn_bv': (0.0, 2.0),
     'L2_xattn_bo': (0.0, 2.0),
     'L2_xattn_gamma': (1.0, 0.2),
     'L2_xattn_beta': (0.0, 0.1),
     'L3_xattn_ln1_scale': (1.0, 0.6),
     'L3_xattn_ln1_offset': (0.0, 0.8),
     'L3_xattn_bq1': (0.0, 0.8),
     'L3_xattn_bk1': (0.0, 2.0),
     'L3_xattn_bv1': (0.0, 0.1),
     'L3_xattn_bo1': (0.0, 0.1),
     'L3_xattn_ln2_scale': (1.0, 0.6),
     'L3_xattn_ln2_offset': (0.0, 0.8),
     'L3_xattn_bq2': (0.0, 0.8),
     'L3_xattn_bk2': (0.0, 2.0),
     'L3_xattn_bv2': (0.0, 0.1),
     'L3_xattn_bo2': (0.0, 0.1),
     'L3_xattn_ln_mlp_scale': (1.0, 0.6),
     'L3_xattn_ln_mlp_offset': (0.0, 0.8),
     'L3_xattn_b_fc1': (0.0, 0.1),
     'L3_xattn_b_fc2': (0.0, 0.1)}
    factors = {'L0_xattn_Wq': 8.0,
     'L0_xattn_Wk': 8.0,
     'L1_xattn_maa_x': 8.0,
     'L1_xattn_maa_w': 8.0,
     'L1_xattn_maa_v': 2.675,
     'L1_xattn_maa_w1': 8.0,
     'L1_xattn_maa_w2': 8.0,
     'L1_xattn_time_decay': 3.925,
     'L1_xattn_decay_w1': 8.0,
     'L1_xattn_decay_w2': 8.0,
     'L1_xattn_faaaa': 7.798,
     'L1_xattn_fmaa_k': 7.572,
     'L1_xattn_fmaa_r': 8.0,
     'L1_xattn_fWk': 4.352,
     'L1_xattn_fWr': 8.0,
     'L1_xattn_fWv': 3.959,
     'L2_xattn_Wq': 64.0,
     'L2_xattn_Wk': 64.0,
     'L3_xattn_wq1': 8.0,
     'L3_xattn_wk1': 8.0,
     'L3_xattn_bias_k1': 64.0,
     'L3_xattn_bias_v1': 64.0,
     'L3_xattn_wq2': 8.0,
     'L3_xattn_wk2': 8.0,
     'L3_xattn_bias_k2': 64.0,
     'L3_xattn_bias_v2': 64.0,
     'L2_xattn_Wv': 8.0,
     'L2_xattn_Wo': 8.0}
    for name, (base, spread) in spreads.items():
        noise = np.random.default_rng([zlib.crc32(name.encode()), seed]).standard_normal(out[name].shape)
        drawn = base * np.exp(spread * noise) if base else spread * noise
        out[name] = jnp.asarray(drawn.astype(out[name].dtype))
    for name, factor in factors.items():
        out[name] = (out[name] * factor).astype(out[name].dtype)
    return out
```

```python
from contextlib import ExitStack

import numpy as np

import concourse.bass as bass
from concourse import mybir

ALU = mybir.AluOpType
ACT = mybir.ActivationFunctionType
AX_X = mybir.AxisListType.X
F32 = mybir.dt.float32
BF16 = mybir.dt.bfloat16
U8 = mybir.dt.uint8

P = 128
B, S, C = 4, 256, 256
N = B * S
TQ = S // P
KC = C // P
LAST_LAYER = 4

HEADS0, DIM0 = 16, 16
HEADS2, DIM2, KV2 = 32, 8, 8
HEADS1, DIM1, MIX, DMIX, DDEC = 32, 8, 5, 32, 64
HEADS3, DIM3, FF = 16, 128, 1024
EPS = 1e-5
EPS2 = 1e-6
BIG = 3.0e38

COLS = ["L0_xattn_ln_gamma", "L0_xattn_ln_beta", "L1_xattn_ln1_w", "L1_xattn_ln1_b", "L1_xattn_ln2_w",
        "L1_xattn_ln2_b", "L1_xattn_maa_x", "L1_xattn_maa_w", "L1_xattn_maa_k", "L1_xattn_maa_v",
        "L1_xattn_maa_r", "L1_xattn_maa_g", "L1_xattn_time_decay", "L1_xattn_faaaa", "L1_xattn_fmaa_k",
        "L1_xattn_fmaa_r", "L2_xattn_bq", "bk_of_q_heads", "L3_xattn_ln1_scale", "L3_xattn_ln1_offset",
        "L3_xattn_ln2_scale", "L3_xattn_ln2_offset", "L3_xattn_ln_mlp_scale", "L3_xattn_ln_mlp_offset"]
HEAD_COLS = ["bq1", "bk1", "bv1", "bias_k1", "bias_v1", "bq2", "bk2", "bv2", "bias_k2", "bias_v2"]
ROWS = ["L1_xattn_gn_w", "L1_xattn_gn_b", "L2_xattn_bo", "L2_xattn_gamma", "L2_xattn_beta",
        "L3_xattn_bo1", "L3_xattn_bo2", "L3_xattn_b_fc2", "L2_xattn_bv"]
N_HEAD_COLS = len(HEAD_COLS) * HEADS3
N_COLS = len(COLS) * KC + N_HEAD_COLS + FF // P


class Chain:

    def __init__(self, eng, sem):
        self.eng, self.sem, self.n = eng, sem, 0

    def link(self, ins):
        self.n += 1
        ins.then_inc(self.sem, 1)
        self.eng.wait_ge(self.sem, self.n)


def build(nc, d, out):
    with ExitStack() as ctx:
        def sb(name, shape, dt=F32):
            return ctx.enter_context(nc.sbuf_tensor(name, shape, dt))

        def bank(name):
            return ctx.enter_context(nc.psum_tensor(name, [P, 512], F32))

        def sem(name):
            return ctx.enter_context(nc.semaphore(name))

        J0, J1, S0, S1, T0, T1, O0, O1 = (bank(n) for n in ("J0", "J1", "S0", "S1", "T0", "T1", "O0", "O1"))

        def two(x):
            return x[:, :].rearrange("p (a n) -> p a n", a=2)

        ident = sb("ident", [P, P])
        head8 = sb("head8", [P, P // DIM1])
        head16 = sb("head16", [P, P // DIM0])
        cols = sb("cols", [P, N_COLS])
        rows = sb("rows", [P, len(ROWS), C])
        x_tok = sb("x_tok", [P, B * TQ, C])
        ctxT = sb("ctxT", [P, KC, N])
        weights_a = sb("weights_a", [P, 4 * 4096])
        early = sb("early", [P, 4 * 4096])
        km0 = sb("km0", [P, 16 * S])

        def col(name, k):
            i = COLS.index(name) * KC + k
            return cols[:, i:i + 1]

        def head_cols(name):
            i = len(COLS) * KC + HEAD_COLS.index(name) * HEADS3
            return cols[:, i:i + HEADS3]

        fc1_cols = cols[:, N_COLS - FF // P:N_COLS]

        def row(name):
            return rows[:, ROWS.index(name), :]

        taken = [0]

        def carve(n, pattern=None, **sizes):
            at = taken[0]
            taken[0] += n
            assert taken[0] <= 4 * 4096
            v = early[:, at:at + n]
            return v.rearrange(pattern, **sizes) if pattern else v

        km1 = carve(16 * S)
        km = [km0[:, :].rearrange("p (h n) -> p h n", h=16), km1.rearrange("p (h n) -> p h n", h=16)]
        w = {}
        WEIGHTS = ["L0_q", "L0_k", "L0_v", "L0_o", "L1_r", "L1_k", "L1_v", "L1_g", "L1_o", "L1_fk", "L1_fr",
                   "L1_fv", "L2_q", "L2_k", "L2_o"]
        for n in WEIGHTS:
            w[n] = carve(KC * C, "p (k n) -> p k n", k=KC)
        w["L2_v"] = carve(KC * KV2 * DIM2, "p (k n) -> p k n", k=KC)
        w1 = carve(KC * MIX * DMIX, "p (k n) -> p k n", k=KC)
        w2 = carve(4 * C, "p (f n) -> p f n", f=4)
        w2_last = carve(C)
        dec1 = carve(KC * DDEC, "p (k n) -> p k n", k=KC)
        dec2 = carve(C)
        mask2 = carve(B * TQ * S, "p (t n) -> p t n", t=B * TQ)

        ctx_tok = weights_a[:, 0:B * TQ * C].rearrange("p (t c) -> p t c", c=C)
        mask0 = weights_a[:, 2048:2048 + N]
        mask_bytes = weights_a[:, 3072:3072 + N // 4].bitcast(U8)

        def wide_weights(region):
            q, k, v, o = (region[:, i * 4096:(i + 1) * 4096] for i in range(4))
            return (q.rearrange("p (k n) -> p k n", k=KC), k.rearrange("p (k n) -> p k n", k=KC),
                    v.rearrange("p (k n) -> p k n", k=KC), o.rearrange("p (h n) -> p h n", h=HEADS3))

        wide = [wide_weights(weights_a[:, :]), wide_weights(early[:, :])]
        fc1 = weights_a[:, 0:KC * FF].rearrange("p (k n) -> p k n", k=KC)
        fc2 = weights_a[:, KC * FF:KC * FF + FF // P * C].rearrange("p (m n) -> p m n", m=FF // P)

        xs = sb("xs", [P, TQ, C])
        xn = sb("xn", [P, TQ, C])
        hT = sb("hT", [P, KC, S + 1])
        aT = sb("aT", [P, KC, S])
        QT = sb("QT", [P, KC, S])
        KT = sb("KT", [P, KC, S])
        V = sb("V", [P, TQ, C])
        masked = sb("masked", [P, 2, 512])
        probs = sb("probs", [P, 2, 514])
        PT = sb("PT", [P, 2, 512])
        On = sb("On", [P, TQ, C])
        OT = sb("OT", [P, KC, S])
        maxes = sb("maxes", [P, TQ, 32])
        sums = sb("sums", [P, TQ, 32])
        inv = sb("inv", [P, TQ, 32])
        stats = sb("stats", [P, TQ, 6])
        moments = sb("moments", [P, TQ, 2])
        rstd = sb("rstd", [P, TQ, 1])
        gate = sb("gate", [P, 2])
        mask_b = sb("mask_b", [P, TQ, S])
        halves = sb("halves", [P, 1])
        QK = sb("QK", [P, 2, 2, 260])
        weightT = On[:, 0, 0:TQ * 17].rearrange("p (t h) -> p t h", t=TQ)
        w17, v17 = QT[0:17, 0, :], KT[0:17, 0, :]
        dm = masked[:, :, :].rearrange("p a n -> p (a n)")[:, 0:HEADS3 * 17]
        start_all = sb("start_all", [P, B, KC * DIM1])
        gn = QK[:, :, :, :].rearrange("p a b n -> p (a b n)")[:, 0:TQ * HEADS1 * 3]

        loaded = {n: sem(f"loaded_{n}") for n in
                  ("const", "x", "ctx", "ctxT", "w0", "w1", "w2", "wide0", "wide1", "fc")}
        arrived = sem("arrived")
        go = {n: sem(f"go_{n}") for n in ("pe", "act", "dve", "pool")}
        steps = {}
        v17_done, v17_ready, dm_ready = sem("v17_done"), sem("v17_ready"), sem("dm_ready")
        stored = sem("stored")
        halves_ready, mask_ready = sem("halves_ready"), sem("mask_ready")
        w2_cleared, select_ready = sem("w2_cleared"), sem("select_ready")
        neg_ready, gate_ready = sem("neg_ready"), sem("gate_ready")

        block = ctx.enter_context(nc.Block())
        programs = {"pe": [], "dve": [], "act": [], "pool": []}

        def normalise(dve, chain, src, dst, eps, var_ready, rstd_ready, turn, last_sem):
            for t in range(TQ):
                ins = dve.bn_stats(stats[:, t, :], src(t))
            chain.link(ins)
            for t in range(TQ):
                ins = dve.bn_aggr(moments[:, t, :], stats[:, t, :])
            chain.link(ins)
            dve.tensor_scalar(rstd[:, :, :], moments[:, :, 1:2], eps, None, ALU.add).then_inc(var_ready, 1)
            dve.wait_ge(rstd_ready, turn)
            for t in range(TQ):
                ins = dve.tensor_scalar(dst[:, t, :], src(t), moments[:, t, 0:1], rstd[:, t, :],
                                        ALU.subtract, ALU.mult)
            ins.then_inc(last_sem, 1)

        def take_root(pool, var_ready, rstd_ready, turn, values=None):
            values = rstd[:, :, :].rearrange("p t o -> p (t o)") if values is None else values
            pool.wait_ge(var_ready, turn)
            pool.tensor_tensor(values, values, halves[:, 0:1].to_broadcast(list(values.shape)), ALU.pow)\
                .then_inc(rstd_ready, 1)

        def step(name):
            if name not in steps:
                steps[name] = sem(name)
            return steps[name]

        def meet(eng, name):
            eng.drain().then_inc(arrived, 1)
            eng.wait_ge(go[name], 1)
            eng.sem_clear(go[name])

        def lead(sp):
            numbers = sorted(s.num for s in steps.values())
            assert numbers == list(range(numbers[0], numbers[-1] + 1))
            with sp.Fori(0, B):
                sp.wait_ge(arrived, len(go))
                sp.sem_clear(range(numbers[0], numbers[-1] + 1))
                sp.sem_clear(arrived)
                for s in go.values():
                    sp.sem_inc(s, 1)

        def flip(pe, bank_, src, done_sem):
            for k in range(KC):
                for t in range(TQ):
                    mm = pe.transpose(bank_[:, k * S + t * P:k * S + (t + 1) * P],
                                      src[:, t, k * P:(k + 1) * P], ident[:, :])
            mm.then_inc(done_sem, 1)

        def project(pe, bank_, weight, moving, n_out, done_sem):
            for o in range(n_out):
                for k in range(KC):
                    mm = pe.matmul(bank_[:, o * S:(o + 1) * S], weight(k, o), moving[:, k, :],
                                   start=(k == 0), stop=(k == KC - 1))
            if done_sem is not None:
                mm.then_inc(done_sem, 1)

        def project_tokens(pe, bank_, src, weight, n, done_sem):
            for t in range(TQ):
                for k in range(KC):
                    mm = pe.matmul(bank_[:, t * S:t * S + n], src[:, k, t * P:(t + 1) * P], weight(k),
                                   start=(k == 0), stop=(k == KC - 1))
            mm.then_inc(done_sem, 1)

        def small_attention(layer):
            heads, dim = (HEADS0, DIM0) if layer == 0 else (HEADS2, DIM2)
            per_tile = P // dim
            head_of = head16 if layer == 0 else head8
            pairs = heads // 2
            items = pairs * TQ
            scale = float(dim) ** -0.5
            xs_ready, xn_ready = step("xs_ready"), step("xn_ready")
            x_flipped, a_flipped = step("x_flipped"), step("a_flipped")
            hT_ready, aT_ready = step("hT_ready"), step("aT_ready")
            q_done, k_done, v_done = step("q_done"), step("k_done"), step("v_done")
            q_ready, k_ready, v_ready = step("q_ready"), step("k_ready"), step("v_ready")
            km_ready = step("km_ready")
            scores_done, max_ready = step("scores_done"), step("max_ready")
            probs_ready, probs_flipped = step("probs_ready"), step("probs_flipped")
            pt_ready, av_done = step("pt_ready"), step("av_done")
            on_ready, on_flipped, ot_ready = step("on_ready"), step("on_flipped"), step("ot_ready")
            out_done, batch_done = step("out_done"), step("batch_done")
            dve_chain = step("dve_chain")
            mask_b_ready = step("mask_b_ready")
            var_ready, rstd_ready = step("var_ready"), step("rstd_ready")
            S_, T_ = [S0, S1], [T0, T1]
            O_ = [O0, O1]
            wq, wk, wv, wo = (w[f"L{layer}_{n}"] for n in "qkvo")

            def pe_program(pe):
                pe.wait_ge(loaded["const"], 16 * 5)
                pe.wait_ge(loaded[f"w{layer}"], 16 * (4 if layer == 0 else 5))
                with pe.Fori(0, B) as b:
                    if layer == 0:
                        pe.wait_ge(xn_ready, 1)
                        flip(pe, T1, xn, a_flipped)
                    pe.wait_ge(xs_ready, 1)
                    flip(pe, T0, xs, x_flipped)
                    pe.wait_ge(aT_ready, 1)
                    project(pe, J1, lambda k, o: wk[:, k, o * P:(o + 1) * P], aT, KC, k_done)
                    if layer == 0:
                        project_tokens(pe, O0, aT, lambda k: wv[:, k, :], C, v_done)
                    else:
                        project_tokens(pe, O0, aT, lambda k: wv[:, k, :], KV2 * DIM2, v_done)
                    pe.wait_ge(hT_ready, 1)
                    project(pe, J0, lambda k, o: wq[:, k, o * P:(o + 1) * P], hT[:, :, 0:S], KC, q_done)

                    def scores(i):
                        pair, qt = i // TQ, i % TQ
                        half, h = pair * 2 // per_tile, pair * 2 % per_tile
                        if i == 0:
                            pe.wait_ge(q_ready, 1)
                        if qt == 0:
                            pe.wait_ge(km_ready, pair + 1)
                        if i >= 2:
                            pe.wait_ge(max_ready, i - 1)
                        pe.matmul(S_[i % 2][:, :], QT[:, half, qt * P:(qt + 1) * P],
                                  km[half][:, h:h + 2, :], start=True, stop=True).then_inc(scores_done, 1)

                    def turn(i):
                        pe.wait_ge(probs_ready, i + 1)
                        if i >= 2:
                            pe.wait_ge(pt_ready, i - 1)
                        for n in range(2 * TQ):
                            mm = pe.transpose(T_[i % 2][:, n * P:(n + 1) * P],
                                              probs[:, i % 2, n * P:(n + 1) * P], ident[:, :])
                        mm.then_inc(probs_flipped, 1)

                    def weigh(i):
                        pair, qt = i // TQ, i % TQ
                        pe.wait_ge(pt_ready, i + 1)
                        if i == 0:
                            pe.wait_ge(v_ready, 1)
                        for hh in range(2):
                            h = pair * 2 + hh
                            kv = h * dim if layer == 0 else h // (HEADS2 // KV2) * dim
                            for st in range(TQ):
                                mm = pe.matmul(O_[qt][:, h * dim:(h + 1) * dim],
                                               PT[:, i % 2, (hh * TQ + st) * P:(hh * TQ + st + 1) * P],
                                               V[:, st, kv:kv + dim], start=(st == 0), stop=(st == TQ - 1))
                        mm.then_inc(av_done, 1)

                    scores(0)
                    for i in range(items):
                        if i + 1 < items:
                            scores(i + 1)
                        turn(i)
                        if i >= 1:
                            weigh(i - 1)
                    weigh(items - 1)
                    pe.wait_ge(on_ready, 1)
                    pe.wait_ge(pt_ready, items)
                    flip(pe, T0, On, on_flipped)
                    pe.wait_ge(ot_ready, 1)
                    project_tokens(pe, J0, OT, lambda k: wo[:, k, :], C, out_done)
                    meet(pe, "pe")

            def act_program(act):
                if layer == 0:
                    act.wait_ge(loaded["const"], 16 * 5)
                    act.activation(gate[:, 1:2], gate[:, 0:1], ACT.Tanh).then_inc(gate_ready, 1)
                with act.Fori(0, B) as b:
                    if layer == 0:
                        act.wait_ge(a_flipped, 1)
                        for k in range(KC):
                            ins = act.activation(aT[:, k, :], T1[:, k * S:(k + 1) * S], ACT.Identity,
                                                 bias=col("L0_xattn_ln_beta", k), scale=col("L0_xattn_ln_gamma", k))
                        ins.then_inc(aT_ready, 1)
                    act.wait_ge(x_flipped, 1)
                    act.activation(hT[:, :, 0:S], two(T0), ACT.Copy).then_inc(hT_ready, 1)
                    act.wait_ge(k_done, 1)
                    for k in range(KC):
                        if layer == 0:
                            ins = act.activation(KT[:, k, :], J1[:, k * S:(k + 1) * S], ACT.Copy)
                        else:
                            ins = act.activation(KT[:, k, :], J1[:, k * S:(k + 1) * S], ACT.Identity,
                                                 bias=col("bk_of_q_heads", k))
                        ins.then_inc(k_ready, 1)
                    for i in range(items):
                        pair, qt = i // TQ, i % TQ
                        act.wait_ge(max_ready, i + 1)
                        if i >= 2:
                            act.wait_ge(probs_flipped, i - 1)
                        for hh in range(2):
                            h = pair * 2 + hh
                            ins = act.activation(probs[:, i % 2, hh * S:(hh + 1) * S],
                                                 masked[:, i % 2, hh * S:(hh + 1) * S], ACT.Exp,
                                                 bias=maxes[:, qt, h:h + 1], scale=-1.0,
                                                 accum_out=sums[:, qt, h:h + 1])
                        ins.then_inc(probs_ready, 1)
                    act.wait_ge(on_flipped, 1)
                    act.activation(OT[:, :, :], two(T0), ACT.Copy).then_inc(ot_ready, 1)
                    meet(act, "act")

            def pool_program(pool):
                if layer == 2:
                    pool.wait_ge(loaded["w2"], 16 * 5)
                    pool.tensor_scalar(mask2[:, :, :], mask2[:, :, :], -1.0, 0.0, ALU.mult, ALU.add)\
                        .then_inc(neg_ready, 1)
                    pool.wait_ge(neg_ready, 1)
                else:
                    pool.wait_ge(loaded["x"], 16)
                    pool.memset(halves[:, :], -0.5).then_inc(halves_ready, 1)
                    pool.wait_ge(halves_ready, 1)
                    pool.wait_ge(mask_ready, 2)
                with pool.Fori(0, B) as b:
                    if layer == 0:
                        take_root(pool, var_ready, rstd_ready, 1)
                    pool.tensor_copy(xs[:, :, :], x_tok[:, bass.ds(b * TQ, TQ), :]).then_inc(xs_ready, 1)
                    if layer == 0:
                        pool.tensor_copy(mask_b[:, 0, :], mask0[:, bass.ds(b * S, S)]).then_inc(mask_b_ready, 1)
                    else:
                        pool.tensor_copy(mask_b[:, :, :], mask2[:, bass.ds(b * TQ, TQ), :]).then_inc(mask_b_ready, 1)
                        pool.tensor_copy(aT[:, :, :], ctxT[:, :, bass.ds(b * S, S)]).then_inc(aT_ready, 1)
                    for pair in range(pairs):
                        half, h = pair * 2 // per_tile, pair * 2 % per_tile
                        if h == 0:
                            pool.wait_ge(k_ready, half + 1)
                        for hh in range(2):
                            ins = pool.tensor_scalar(km[half][:, h + hh, :], KT[:, half, :],
                                                     head_of[:, h + hh:h + hh + 1], 1.0, ALU.mult, ALU.mult)
                        ins.then_inc(km_ready, 1)
                    if layer == 2:
                        take_root(pool, var_ready, rstd_ready, 1)
                    meet(pool, "pool")

            def dve_program(dve):
                if layer == 0:
                    dve.wait_ge(loaded["ctx"], 32)
                    dve.tensor_scalar(mask0, mask_bytes, 1.0, -BIG, ALU.subtract, ALU.mult).then_inc(mask_ready, 1)
                    dve.wait_ge(mask_ready, 1)
                    dve.tensor_scalar(mask0, mask0, 2.0, None, ALU.mult).then_inc(mask_ready, 1)
                    dve.wait_ge(mask_ready, 2)
                    dve.wait_ge(gate_ready, 1)
                else:
                    dve.wait_ge(neg_ready, 1)
                with dve.Fori(0, B) as b:
                    chain = Chain(dve, dve_chain)
                    if layer == 0:
                        normalise(dve, chain, lambda t: ctx_tok[:, bass.ds(b * TQ + t, 1), :]
                                  .rearrange("p a c -> p (a c)"), xn, EPS, var_ready, rstd_ready, 1, xn_ready)
                    dve.wait_ge(v_done, 1)
                    if layer == 0:
                        dve.tensor_copy(V[:, :, :], two(O0)).then_inc(v_ready, 1)
                    else:
                        n = KV2 * DIM2
                        dve.tensor_tensor(V[:, :, 0:n], two(O0)[:, :, 0:n],
                                          row("L2_xattn_bv")[:, 0:n].unsqueeze(1).to_broadcast([P, TQ, n]),
                                          ALU.add).then_inc(v_ready, 1)
                    dve.wait_ge(q_done, 1)
                    for k in range(KC):
                        if layer == 0:
                            ins = dve.tensor_scalar(QT[:, k, :], J0[:, k * S:(k + 1) * S], -scale, None, ALU.mult)
                        else:
                            ins = dve.tensor_scalar(QT[:, k, :], J0[:, k * S:(k + 1) * S], col("L2_xattn_bq", k),
                                                    -scale, ALU.add, ALU.mult)
                    ins.then_inc(q_ready, 1)

                    def add_mask(i):
                        pair, qt = i // TQ, i % TQ
                        dve.wait_ge(scores_done, i + 1)
                        if i == 0:
                            dve.wait_ge(mask_b_ready, 1)
                        if i >= 2:
                            dve.wait_ge(probs_ready, i - 1)
                        for hh in range(2):
                            h = pair * 2 + hh
                            ins = dve.tensor_tensor_reduce(
                                out=masked[:, i % 2, hh * S:(hh + 1) * S], in0=S_[i % 2][:, hh * S:(hh + 1) * S],
                                in1=mask_b[:, 0 if layer == 0 else qt, :], scale=1.0, scalar=BIG, op0=ALU.add, op1=ALU.min,
                                accum_out=maxes[:, qt, h:h + 1])
                        ins.then_inc(max_ready, 1)

                    def fetch_turned(i):
                        dve.wait_ge(probs_flipped, i + 1)
                        if i >= 2:
                            dve.wait_ge(av_done, i - 1)
                        dve.tensor_copy(PT[:, i % 2, :], T_[i % 2][:, :]).then_inc(pt_ready, 1)

                    for i in range(items):
                        add_mask(i)
                        if i >= 1:
                            fetch_turned(i - 1)
                    fetch_turned(items - 1)
                    dve.wait_ge(probs_ready, items)
                    chain.link(dve.reciprocal(inv[:, :, 0:heads], sums[:, :, 0:heads]))
                    dve.wait_ge(av_done, items)
                    for qt in range(TQ):
                        ins = dve.tensor_tensor(On[:, qt, :].rearrange("p (h d) -> p h d", d=dim),
                                                O_[qt][:, 0:C].rearrange("p (h d) -> p h d", d=dim),
                                                inv[:, qt, 0:heads].unsqueeze(2).to_broadcast([P, heads, dim]),
                                                ALU.mult)
                    ins.then_inc(on_ready, 1)
                    dve.wait_ge(out_done, 1)
                    x_b = x_tok[:, bass.ds(b * TQ, TQ), :]
                    if layer == 0:
                        dve.scalar_tensor_tensor(
                            out=x_b.rearrange("p t c -> p (t c)"), in0=J0[:, :], scalar=gate[:, 1:2],
                            in1=xs[:, :, :].rearrange("p t c -> p (t c)"), op0=ALU.mult, op1=ALU.add)\
                            .then_inc(batch_done, 1)
                    else:
                        bo = row("L2_xattn_bo").unsqueeze(1).to_broadcast([P, TQ, C])
                        gamma = row("L2_xattn_gamma").unsqueeze(1).to_broadcast([P, TQ, C])
                        beta = row("L2_xattn_beta").unsqueeze(1).to_broadcast([P, TQ, C])
                        chain.link(dve.tensor_tensor(xs[:, :, :], two(J0), xs[:, :, :], ALU.add))
                        chain.link(dve.tensor_tensor(xs[:, :, :], xs[:, :, :], bo, ALU.add))
                        normalise(dve, chain, lambda t: xs[:, t, :], xn, EPS2, var_ready, rstd_ready, 1, xn_ready)
                        dve.wait_ge(xn_ready, 1)
                        chain.link(dve.tensor_tensor(xn[:, :, :], xn[:, :, :], gamma, ALU.mult))
                        dve.tensor_tensor(x_b, xn[:, :, :], beta, ALU.add).then_inc(batch_done, 1)
                    dve.wait_ge(batch_done, 1)
                    meet(dve, "dve")

            programs["pe"].append(pe_program)
            programs["act"].append(act_program)
            programs["pool"].append(pool_program)
            programs["dve"].append(dve_program)

        def rwkv_block():
            xn_ready, xn_flipped, xa_ready, sx_ready = (step(n) for n in
                                                        ("xn_ready", "xn_flipped", "xa_ready", "sx_ready"))
            xxx_ready, lora_done, lora_ready = step("xxx_ready"), step("lora_done"), step("lora_ready")
            mix_done, mix_ready, xf_ready = step("mix_done"), step("mix_ready"), step("xf_ready")
            dec1_done, dec1_ready, dec2_done = step("dec1_done"), step("dec1_ready"), step("dec2_done")
            exp_ready, decay_ready = step("exp_ready"), step("decay_ready")
            k_done, v_done, r_done, g_done = (step(f"{n}_done") for n in "kvrg")
            k_ready, v_ready, r_ready, g_ready = (step(f"{n}_ready") for n in "kvrg")
            spread_done, kv_ready, start_ready = step("spread_done"), step("kv_ready"), step("start_ready")
            start_here, split = step("start_here"), step("split")
            vT_done, vT_ready, v_parts_ready = step("vT_done"), step("vT_ready"), step("v_parts_ready")
            state_ready, read_ready, y_done = step("state_ready"), step("read_ready"), step("y_done")
            rk_ready, ruk_ready, bonus_done = step("rk_ready"), step("ruk_ready"), step("bonus_done")
            yg_ready, yg_flipped, ygT_ready = step("yg_ready"), step("yg_flipped"), step("ygT_ready")
            out_done, x_ready = step("out_done"), step("x_ready")
            xc_flipped, xc_ready, sxc_ready = step("xc_flipped"), step("xc_ready"), step("sxc_ready")
            xk2_ready, xr2_ready = step("xk2_ready"), step("xr2_ready")
            fk_done, fr_done, relu_ready = step("fk_done"), step("fr_done"), step("relu_ready")
            kk_ready, rr_ready, fv_done = step("kk_ready"), step("rr_ready"), step("fv_done")
            var_ready, rstd_ready = step("var_ready"), step("rstd_ready")
            batch_done, dve_chain = step("batch_done"), step("dve_chain")

            def scratch(half, at, n=KC * S):
                return [km0[:, :], km1][half][:, at:at + n]

            def pair(v):
                return v.rearrange("p (a n) -> p a n", a=2)

            xf = [pair(scratch(0, i * 512)) for i in range(MIX)]
            rT, kT, wT = (pair(scratch(0, 512 * i)) for i in (5, 6, 7))
            kv = [pair(scratch(1, 512 * i)) for i in (0, 1)]
            read = [pair(scratch(1, 512 * i)) for i in (2, 3)]
            state = [scratch(1, 2048 + 514 * i, 514).rearrange("p (a n) -> p a n", a=2) for i in (0, 1)]
            silu_g = scratch(1, 3076).rearrange("p (t c) -> p t c", t=TQ)
            start = scratch(1, 3588, KC * DIM1).rearrange("p (a j) -> p a j", a=2)
            sx, xxx = QT, KT
            mixed = [masked[:, i, :].rearrange("p (a n) -> p a n", a=2) for i in (0, 1)]
            lora = PT[:, 0, 0:S]
            lora_last = PT[0:DMIX, 0, S:2 * S]
            decay_in = PT[0:DDEC, 1, 0:S]
            ruk = pair(PT[:, 1, :])
            v_tok = V
            yv = probs[:, 0, 0:512]
            tmp = probs[:, 1, 0:512]
            yv3, tmp3 = (v.rearrange("p (h j) -> p h j", j=DIM1) for v in (yv, tmp))
            mean, var = gn[:, 0:TQ * HEADS1], gn[:, TQ * HEADS1:2 * TQ * HEADS1]
            bonus = gn[:, 2 * TQ * HEADS1:3 * TQ * HEADS1]
            mix_banks = [S0, S1, T1, O0, O1]
            spread_banks = [T0, J1]
            heads_tile = P // DIM1

            select = mask_b[:, :, :].rearrange("p t n -> p (t n)").bitcast(BF16)
            rest = aT[:, :, :].rearrange("p k n -> p (k n)")
            halves_of_on = On[:, :, :].rearrange("p t n -> p (t n)").bitcast(BF16)
            v_parts = [halves_of_on[:, 0:512], halves_of_on[:, 512:1024],
                       OT[:, :, :].rearrange("p k n -> p (k n)").bitcast(BF16)[:, 0:512]]

            def pe_program(pe):
                pe.wait_ge(loaded["w1"], 16 * 17)
                pe.wait_ge(select_ready, 1)
                with pe.Fori(0, B) as b:
                    pe.wait_ge(xn_ready, 1)
                    flip(pe, T0, xn, xn_flipped)
                    pe.wait_ge(xxx_ready, 1)
                    for k in range(KC):
                        pe.matmul(J0[:, 0:S], w1[:, k, 0:P], xxx[:, k, :], start=(k == 0), stop=(k == KC - 1))
                    for k in range(KC):
                        mm = pe.matmul(J0[0:DMIX, S:2 * S], w1[:, k, P:P + DMIX], xxx[:, k, :],
                                       start=(k == 0), stop=(k == KC - 1))
                    mm.then_inc(lora_done, 1)
                    pe.wait_ge(lora_ready, 1)
                    for f in range(MIX):
                        for o in range(KC):
                            if f < 4:
                                mm = pe.matmul(mix_banks[f][:, o * S:(o + 1) * S], w2[:, f, o * P:(o + 1) * P], lora,
                                               start=True, stop=True)
                            else:
                                mm = pe.matmul(mix_banks[f][:, o * S:(o + 1) * S],
                                               w2_last[0:DMIX, o * P:(o + 1) * P], lora_last, start=True, stop=True)
                        mm.then_inc(mix_done, 1)
                    pe.wait_ge(xf_ready, 1)
                    for k in range(KC):
                        mm = pe.matmul(J1[0:DDEC, 0:S], dec1[:, k, :], xf[0][:, k, :], start=(k == 0), stop=(k == KC - 1))
                    mm.then_inc(dec1_done, 1)
                    pe.wait_ge(xf_ready, 2)
                    project(pe, S0, lambda k, o: w["L1_k"][:, k, o * P:(o + 1) * P], xf[1], KC, k_done)
                    pe.wait_ge(dec1_ready, 1)
                    for o in range(KC):
                        mm = pe.matmul(J0[:, o * S:(o + 1) * S], dec2[0:DDEC, o * P:(o + 1) * P], decay_in,
                                       start=True, stop=True)
                    mm.then_inc(dec2_done, 1)
                    pe.wait_ge(xf_ready, 3)
                    project_tokens(pe, S1, xf[2], lambda k: w["L1_v"][:, k, :], C, v_done)

                    def spread(j):
                        if j >= 2:
                            pe.wait_ge(kv_ready, j - 1)
                        for n, part in enumerate(v_parts):
                            mm = pe.matmul(spread_banks[j % 2][:, :], select[:, j * P:(j + 1) * P], part,
                                           start=(n == 0), stop=(n == len(v_parts) - 1))
                        mm.then_inc(spread_done, 1)

                    project(pe, J1, lambda k, o: w["L1_v"][:, k, o * P:(o + 1) * P], xf[2], KC, vT_done)
                    pe.wait_ge(xf_ready, 4)
                    project(pe, T1, lambda k, o: w["L1_r"][:, k, o * P:(o + 1) * P], xf[3], KC, r_done)
                    pe.wait_ge(xf_ready, 5)
                    project_tokens(pe, O0, xf[4], lambda k: w["L1_g"][:, k, :], C, g_done)
                    pe.wait_ge(v_parts_ready, 1)
                    spread(0)
                    spread(1)

                    def gather(j):
                        pe.wait_ge(read_ready, j + 1)
                        for t in range(TQ):
                            for half in range(KC):
                                at = t * C + half * P
                                y = O1[:, at:at + P].rearrange("p (h j) -> p h j", j=DIM1)[:, :, j]
                                mm = pe.matmul(y, read[j % 2][:, half, t * P:(t + 1) * P], head8[:, :],
                                               start=True, stop=True)
                        mm.then_inc(y_done, 1)

                    for j in range(DIM1):
                        if j + 2 < DIM1:
                            spread(j + 2)
                        if j == 1:
                            pe.wait_ge(ruk_ready, 1)
                            pe.wait_ge(k_ready, 1)
                            for t in range(TQ):
                                for half in range(KC):
                                    at = t * HEADS1 + half * heads_tile
                                    mm = pe.matmul(S0[:, at:at + heads_tile], ruk[:, half, t * P:(t + 1) * P],
                                                   head8[:, :], start=True, stop=True)
                            mm.then_inc(bonus_done, 1)
                        gather(j)
                    pe.wait_ge(yg_ready, 1)
                    flip(pe, T0, yv.rearrange("p (t c) -> p t c", t=TQ), yg_flipped)
                    pe.wait_ge(ygT_ready, 1)
                    project_tokens(pe, J0, OT, lambda k: w["L1_o"][:, k, :], C, out_done)
                    pe.wait_ge(xn_ready, 2)
                    flip(pe, T1, xn, xc_flipped)
                    pe.wait_ge(xk2_ready, 1)
                    project(pe, S0, lambda k, o: w["L1_fk"][:, k, o * P:(o + 1) * P], xf[0], KC, fk_done)
                    pe.wait_ge(xr2_ready, 1)
                    project_tokens(pe, S1, xf[1], lambda k: w["L1_fr"][:, k, :], C, fr_done)
                    pe.wait_ge(kk_ready, 1)
                    project_tokens(pe, O0, xf[3], lambda k: w["L1_fv"][:, k, :], C, fv_done)
                    meet(pe, "pe")

            def act_program(act):
                act.wait_ge(loaded["ctxT"], 32)
                with act.Fori(0, B) as b:
                    act.activation(hT[:, :, 0:1], ctxT[:, :, bass.ds(b * S + 1, 1)], ACT.Copy)
                    act.wait_ge(xn_flipped, 1)
                    for k in range(KC):
                        ins = act.activation(hT[:, k, 1:S + 1], T0[:, k * S:(k + 1) * S], ACT.Identity,
                                             bias=col("L1_xattn_ln1_b", k), scale=col("L1_xattn_ln1_w", k))
                    ins.then_inc(xa_ready, 1)
                    act.wait_ge(lora_done, 1)
                    act.activation(lora, J0[:, 0:S], ACT.Tanh)
                    act.activation(lora_last, J0[0:DMIX, S:2 * S], ACT.Tanh).then_inc(lora_ready, 1)
                    act.wait_ge(dec1_done, 1)
                    act.activation(decay_in, J1[0:DDEC, 0:S], ACT.Tanh).then_inc(dec1_ready, 1)
                    act.wait_ge(k_done, 1)
                    act.activation(kT, two(S0), ACT.Copy).then_inc(k_ready, 1)
                    act.wait_ge(dec2_done, 1)
                    for k in range(KC):
                        ins = act.activation(wT[:, k, :], J0[:, k * S:(k + 1) * S], ACT.Exp,
                                             bias=col("L1_xattn_time_decay", k))
                    ins.then_inc(exp_ready, 1)
                    act.wait_ge(exp_ready, 1)
                    act.activation(wT, wT, ACT.Exp, scale=-1.0).then_inc(decay_ready, 1)
                    act.wait_ge(v_done, 1)
                    act.activation(v_tok[:, :, :], two(S1), ACT.Copy).then_inc(v_ready, 1)
                    act.wait_ge(vT_done, 1)
                    act.activation(rest, J1[:, :], ACT.Copy)
                    act.activation(v_parts[0], J1[:, :], ACT.Copy).then_inc(vT_ready, 1)
                    act.wait_ge(r_done, 1)
                    act.activation(rT, two(T1), ACT.Copy).then_inc(r_ready, 1)
                    act.wait_ge(start_here, 1)
                    for j in range(DIM1):
                        if j >= 2:
                            act.wait_ge(read_ready, j - 1)
                        act.activation(state[j % 2][:, :, 0:1], start[:, :, j:j + 1], ACT.Copy)\
                            .then_inc(start_ready, 1)
                    act.wait_ge(g_done, 1)
                    act.activation(silu_g, two(O0), ACT.Silu).then_inc(g_ready, 1)
                    act.wait_ge(yg_flipped, 1)
                    act.activation(OT[:, :, :], two(T0), ACT.Copy).then_inc(ygT_ready, 1)
                    act.wait_ge(xf_ready, MIX)
                    act.activation(hT[:, :, 0:1], ctxT[:, :, bass.ds(b * S, 1)], ACT.Copy)
                    act.wait_ge(xc_flipped, 1)
                    for k in range(KC):
                        ins = act.activation(hT[:, k, 1:S + 1], T1[:, k * S:(k + 1) * S], ACT.Identity,
                                             bias=col("L1_xattn_ln2_b", k), scale=col("L1_xattn_ln2_w", k))
                    ins.then_inc(xc_ready, 1)
                    act.wait_ge(fk_done, 1)
                    act.activation(xf[2], two(S0), ACT.Relu).then_inc(relu_ready, 1)
                    act.wait_ge(relu_ready, 1)
                    act.activation(xf[3], xf[2], ACT.Square).then_inc(kk_ready, 1)
                    act.wait_ge(fr_done, 1)
                    act.activation(silu_g, two(S1), ACT.Sigmoid).then_inc(rr_ready, 1)
                    meet(act, "act")

            def pool_program(pool):
                pool.wait_ge(loaded["w1"], 16 * 17)
                for j in range(DIM1):
                    ins = pool.tensor_copy(
                        select[:, j * P:(j + 1) * P].rearrange("p (h i) -> p h i", i=DIM1),
                        ident[:, j:P:DIM1].unsqueeze(2).to_broadcast([P, heads_tile, DIM1]))
                ins.then_inc(select_ready, 1)
                with pool.Fori(0, B) as b:
                    pool.tensor_copy(start.rearrange("p a j -> p (a j)"),
                                     start_all[:, bass.ds(b, 1), :].rearrange("p o n -> p (o n)"))\
                        .then_inc(start_here, 1)
                    take_root(pool, var_ready, rstd_ready, 1)
                    for f in range(MIX):
                        pool.wait_ge(mix_ready, f + 1)
                        pool.tensor_tensor(xf[f], mixed[f % 2], hT[:, :, 1:S + 1], ALU.add).then_inc(xf_ready, 1)
                    pool.wait_ge(vT_ready, 1)
                    pool.tensor_tensor(rest, rest, v_parts[0], ALU.subtract).then_inc(split, 1)
                    pool.wait_ge(split, 1)
                    pool.tensor_copy(v_parts[1], rest).then_inc(split, 1)
                    pool.wait_ge(split, 2)
                    pool.tensor_tensor(rest, rest, v_parts[1], ALU.subtract).then_inc(split, 1)
                    pool.wait_ge(split, 3)
                    pool.tensor_copy(v_parts[2], rest).then_inc(v_parts_ready, 1)
                    take_root(pool, var_ready, rstd_ready, 2, values=var)
                    take_root(pool, var_ready, rstd_ready, 3)
                    meet(pool, "pool")

            def dve_program(dve):
                with dve.Fori(0, B) as b:
                    chain = Chain(dve, dve_chain)
                    x_b = x_tok[:, bass.ds(b * TQ, TQ), :]

                    def x_tile(t):
                        return x_tok[:, bass.ds(b * TQ + t, 1), :].rearrange("p a c -> p (a c)")

                    normalise(dve, chain, x_tile, xn, EPS, var_ready, rstd_ready, 1, xn_ready)
                    dve.wait_ge(xa_ready, 1)
                    dve.tensor_tensor(sx[:, :, :], hT[:, :, 0:S], hT[:, :, 1:S + 1], ALU.subtract).then_inc(sx_ready, 1)
                    dve.wait_ge(sx_ready, 1)
                    for k in range(KC):
                        ins = dve.scalar_tensor_tensor(out=xxx[:, k, :], in0=sx[:, k, :], scalar=col("L1_xattn_maa_x", k),
                                                       in1=hT[:, k, 1:S + 1], op0=ALU.mult, op1=ALU.add)
                    ins.then_inc(xxx_ready, 1)
                    for f, n in enumerate("wkvrg"):
                        dve.wait_ge(mix_done, f + 1)
                        if f >= 2:
                            dve.wait_ge(xf_ready, f - 1)
                        for k in range(KC):
                            ins = dve.scalar_tensor_tensor(out=mixed[f % 2][:, k, :],
                                                           in0=mix_banks[f][:, k * S:(k + 1) * S],
                                                           scalar=col("L1_xattn_maa_" + n, k), in1=sx[:, k, :],
                                                           op0=ALU.add, op1=ALU.mult)
                        ins.then_inc(mix_ready, 1)

                    def times_k(j):
                        dve.wait_ge(spread_done, j + 1)
                        if j >= 2:
                            dve.wait_ge(state_ready, j - 1)
                        dve.tensor_tensor(kv[j % 2], kT, two(spread_banks[j % 2]), ALU.mult).then_inc(kv_ready, 1)

                    dve.wait_ge(k_ready, 1)
                    times_k(0)
                    dve.wait_ge(r_ready, 1)
                    dve.wait_ge(decay_ready, 1)
                    for k in range(KC):
                        ins = dve.scalar_tensor_tensor(out=ruk[:, k, :], in0=rT[:, k, :], scalar=col("L1_xattn_faaaa", k),
                                                       in1=kT[:, k, :], op0=ALU.mult, op1=ALU.mult)
                    ins.then_inc(ruk_ready, 1)
                    for j in range(DIM1):
                        dve.wait_ge(kv_ready, j + 1)
                        dve.wait_ge(start_ready, j + 1)
                        if j >= 2:
                            dve.wait_ge(read_ready, j - 1)
                        for half in range(KC):
                            ins = dve.tensor_tensor_scan(state[j % 2][:, half, 1:S + 1], wT[:, half, :],
                                                         kv[j % 2][:, half, :], start[:, half, j:j + 1],
                                                         ALU.mult, ALU.add)
                        ins.then_inc(state_ready, 1)
                        if j + 1 < DIM1:
                            times_k(j + 1)
                        dve.wait_ge(state_ready, j + 1)
                        if j >= 2:
                            dve.wait_ge(y_done, j - 1)
                        dve.tensor_tensor(read[j % 2], rT, state[j % 2][:, :, 0:S], ALU.mult).then_inc(read_ready, 1)
                    dve.wait_ge(bonus_done, 1)
                    dve.wait_ge(v_ready, 1)
                    chain.link(dve.tensor_tensor(tmp3, v_tok[:, :, :].rearrange("p t (h j) -> p (t h) j", j=DIM1),
                                                 S0[:, 0:TQ * HEADS1].unsqueeze(2).to_broadcast([P, TQ * HEADS1, DIM1]),
                                                 ALU.mult))
                    dve.wait_ge(y_done, DIM1)
                    chain.link(dve.tensor_tensor(yv, O1[:, :], tmp, ALU.add))
                    chain.link(dve.tensor_reduce(mean, yv3, AX_X, ALU.add))
                    chain.link(dve.tensor_scalar(mean, mean, 1.0 / DIM1, None, ALU.mult))
                    wide_mean = mean.unsqueeze(2).to_broadcast([P, TQ * HEADS1, DIM1])
                    chain.link(dve.tensor_tensor(yv3, yv3, wide_mean, ALU.subtract))
                    chain.link(dve.tensor_tensor(tmp, yv, yv, ALU.mult))
                    chain.link(dve.tensor_reduce(var, tmp3, AX_X, ALU.add))
                    dve.tensor_scalar(var, var, 1.0 / DIM1, EPS, ALU.mult, ALU.add).then_inc(var_ready, 1)
                    dve.wait_ge(rstd_ready, 2)
                    wide_rstd = var.unsqueeze(2).to_broadcast([P, TQ * HEADS1, DIM1])
                    chain.link(dve.tensor_tensor(yv3, yv3, wide_rstd, ALU.mult))

                    def both(n):
                        return row(n).unsqueeze(1).to_broadcast([P, TQ, C])

                    y_t = yv.rearrange("p (t c) -> p t c", t=TQ)
                    chain.link(dve.tensor_tensor(y_t, y_t, both("L1_xattn_gn_w"), ALU.mult))
                    chain.link(dve.tensor_tensor(y_t, y_t, both("L1_xattn_gn_b"), ALU.add))
                    dve.wait_ge(g_ready, 1)
                    dve.tensor_tensor(y_t, y_t, silu_g, ALU.mult).then_inc(yg_ready, 1)
                    dve.wait_ge(out_done, 1)
                    dve.tensor_tensor(xs[:, :, :], two(J0), x_b, ALU.add).then_inc(x_ready, 1)
                    dve.wait_ge(x_ready, 1)
                    normalise(dve, chain, lambda t: xs[:, t, :], xn, EPS, var_ready, rstd_ready, 3, xn_ready)
                    dve.wait_ge(xc_ready, 1)
                    dve.tensor_tensor(sx[:, :, :], hT[:, :, 0:S], hT[:, :, 1:S + 1], ALU.subtract).then_inc(sxc_ready, 1)
                    dve.wait_ge(sxc_ready, 1)
                    for n, dst, ready in (("k", xf[0], xk2_ready), ("r", xf[1], xr2_ready)):
                        for k in range(KC):
                            ins = dve.scalar_tensor_tensor(out=dst[:, k, :], in0=sx[:, k, :],
                                                           scalar=col("L1_xattn_fmaa_" + n, k),
                                                           in1=hT[:, k, 1:S + 1], op0=ALU.mult, op1=ALU.add)
                        ins.then_inc(ready, 1)
                    dve.wait_ge(fv_done, 1)
                    dve.wait_ge(rr_ready, 1)
                    chain.link(dve.tensor_tensor(xn[:, :, :], two(O0), silu_g, ALU.mult))
                    dve.tensor_tensor(x_b, xn[:, :, :], xs[:, :, :], ALU.add).then_inc(batch_done, 1)
                    dve.wait_ge(batch_done, 1)
                    meet(dve, "dve")

            programs["pe"].append(pe_program)
            programs["act"].append(act_program)
            programs["pool"].append(pool_program)
            programs["dve"].append(dve_program)

        def load_layer1(load, split_k, wait_cleared):
            for n in ("r", "k", "v", "g", "o", "fk", "fr", "fv"):
                load(w["L1_" + n], "L1_" + n, "w1", split_k(d["L1_" + n]))
            load(w1, "L1_w1", "w1", split_k(d["L1_w1"]))
            load(w2_last[0:DMIX, :], "L1_w2", "w1", d["L1_w2"][4 * DMIX:MIX * DMIX, :])
            load(dec1, "L1_dec1", "w1", split_k(d["L1_dec1"]))
            load(dec2[0:DDEC, :], "L1_dec2", "w1")
            load(start_all[:, :, :], "state0", "w1")
            wait_cleared()
            for f in range(4):
                load(w2[f * DMIX:(f + 1) * DMIX, f, :], "L1_w2", "w1", d["L1_w2"][f * DMIX:(f + 1) * DMIX, :])
        def wide_attention(a):
            T = S + 1
            xn_ready, xn_flipped, hT_ready, aT_ready = (step(n) for n in
                                                        ("xn_ready", "xn_flipped", "hT_ready", "aT_ready"))
            qk_done, v_done, q_ready, k_ready, v_ready = (step(n) for n in
                                                          ("qk_done", "v_done", "q_ready", "k_ready", "v_ready"))
            logits_done, max_ready, exp_ready, probs_ready = (step(n) for n in
                                                              ("logits_done", "max_ready", "exp_ready", "probs_ready"))
            probs_flipped, pt_ready, av_done, av_ready = (step(n) for n in
                                                          ("probs_flipped", "pt_ready", "av_done", "av_ready"))
            last_ready, last_flipped, w17_ready = (step(n) for n in
                                                   ("last_ready", "last_flipped", "w17_ready"))
            out_done, batch_done, dve_chain = step("out_done"), step("batch_done"), step("dve_chain")
            var_ready, rstd_ready = step("var_ready"), step("rstd_ready")
            wq, wk, wv, wo = wide[a]
            scale = float(DIM3) ** -0.5
            V_ = [V, OT]
            avT = km0[:, :].rearrange("p (h n) -> p h n", h=HEADS3)
            P_ = [probs[:, i, :].rearrange("p (q n) -> p q n", q=TQ) for i in (0, 1)]
            L_ = [[S0, S1], [O0, O1]]

            def pe_program(pe):
                pe.wait_ge(loaded[f"wide{a}"], 16 * 4)
                pe.wait_ge(dm_ready, 3 * a + 3)
                for h in range(HEADS3):
                    mm = pe.matmul(J0[0:17, 0:C], dm[:, h * 17:(h + 1) * 17], wo[:, h, :],
                                   start=(h == 0), stop=(h == HEADS3 - 1))
                mm.then_inc(v17_done, 1)
                pe.wait_ge(v17_ready, a + 1)
                with pe.Fori(0, B) as b:
                    pe.wait_ge(xn_ready, 1)
                    flip(pe, T0, xn, xn_flipped)
                    pe.wait_ge(hT_ready, 1)
                    pe.wait_ge(aT_ready, 1)

                    def project_head(h):
                        if h >= 1:
                            pe.wait_ge(q_ready, h)
                            pe.wait_ge(k_ready, h)
                        for o, (wt, src) in enumerate(((wq, hT), (wk, aT))):
                            for k in range(KC):
                                mm = pe.matmul(J0[:, o * S:(o + 1) * S], wt[:, k, h * P:(h + 1) * P], src[:, k, 0:S],
                                               start=(k == 0), stop=(k == KC - 1))
                        mm.then_inc(qk_done, 1)
                        if h % 2 == 0:
                            if h >= 2:
                                pe.wait_ge(v_ready, h // 2)
                            project_tokens(pe, J1, aT, lambda k: wv[:, k, h * P:(h + 2) * P], 2 * P, v_done)

                    def logits(h):
                        pe.wait_ge(q_ready, h + 1)
                        pe.wait_ge(k_ready, h + 1)
                        if h >= 2:
                            pe.wait_ge(exp_ready, h - 1)
                        for qt in range(TQ):
                            mm = pe.matmul(L_[h % 2][qt][:, 0:T], QK[:, h % 2, 0, qt * P:(qt + 1) * P],
                                           QK[:, h % 2, 1, 0:T], start=True, stop=True)
                        mm.then_inc(logits_done, 1)

                    def turn(h):
                        pe.wait_ge(probs_ready, h + 1)
                        if h >= 1:
                            pe.wait_ge(pt_ready, h)
                        for st in range(TQ):
                            for qt in range(TQ):
                                mm = pe.transpose(T0[:, st * S + qt * P:st * S + (qt + 1) * P],
                                                  P_[h % 2][:, qt, st * P:(st + 1) * P], ident[:, :])
                        mm.then_inc(probs_flipped, 1)

                    def weigh(h):
                        pe.wait_ge(pt_ready, h + 1)
                        pe.wait_ge(v_ready, h // 2 + 1)
                        if h >= 1:
                            pe.wait_ge(av_ready, h)
                        for st in range(TQ):
                            mm = pe.matmul(T1[:, 0:S], V_[h // 2 % 2][:, st, h % 2 * P:(h % 2 + 1) * P],
                                           PT[:, h % 2, st * S:(st + 1) * S], start=(st == 0), stop=(st == TQ - 1))
                        mm.then_inc(av_done, 1)

                    project_head(0)
                    project_head(1)
                    logits(0)
                    for h in range(HEADS3):
                        if h + 1 < HEADS3:
                            logits(h + 1)
                        turn(h)
                        if h + 2 < HEADS3:
                            project_head(h + 2)
                        weigh(h)
                    pe.wait_ge(last_ready, HEADS3)
                    for qt in range(TQ):
                        mm = pe.transpose(T0[0:17, qt * P:(qt + 1) * P], weightT[:, qt, :], ident[:, :])
                    mm.then_inc(last_flipped, 1)
                    pe.wait_ge(w17_ready, 1)
                    pe.wait_ge(av_ready, HEADS3)
                    for qt in range(TQ):
                        for h in range(HEADS3):
                            pe.matmul(J0[:, qt * C:(qt + 1) * C], avT[:, h, qt * P:(qt + 1) * P], wo[:, h, :],
                                      start=(h == 0), stop=False)
                        mm = pe.matmul(J0[:, qt * C:(qt + 1) * C], w17[:, qt * P:(qt + 1) * P], v17,
                                       start=False, stop=True)
                    mm.then_inc(out_done, 1)
                    meet(pe, "pe")

            def act_program(act):
                act.wait_ge(v17_done, a + 1)
                act.activation(v17, J0[0:17, 0:C], ACT.Copy).then_inc(v17_ready, 1)
                with act.Fori(0, B) as b:
                    act.wait_ge(xn_flipped, 1)
                    for k in range(KC):
                        ins = act.activation(hT[:, k, 0:S], T0[:, k * S:(k + 1) * S], ACT.Identity,
                                             bias=col(f"L3_xattn_ln{a + 1}_offset", k),
                                             scale=col(f"L3_xattn_ln{a + 1}_scale", k))
                    ins.then_inc(hT_ready, 1)

                    def fetch_k(h):
                        act.wait_ge(qk_done, h + 1)
                        if h >= 2:
                            act.wait_ge(logits_done, h - 1)
                        act.wait_ge(q_ready, h + 1)
                        act.activation(QK[:, h % 2, 1, S:T], head_cols(f"bias_k{a + 1}")[:, h:h + 1], ACT.Copy)
                        act.activation(QK[:, h % 2, 1, 0:S], J0[:, S:2 * S], ACT.Identity,
                                       bias=head_cols(f"bk{a + 1}")[:, h:h + 1]).then_inc(k_ready, 1)

                    def exponents(h):
                        if h >= 2:
                            act.wait_ge(probs_flipped, h - 1)
                            act.wait_ge(last_ready, h - 1)
                        act.wait_ge(max_ready, h + 1)
                        for qt in range(TQ):
                            ins = act.activation(P_[h % 2][:, qt, 0:T], L_[h % 2][qt][:, 0:T], ACT.Exp,
                                                 bias=maxes[:, qt, h:h + 1], accum_out=sums[:, qt, h:h + 1])
                        ins.then_inc(exp_ready, 1)

                    def fetch_turned(h):
                        act.wait_ge(probs_flipped, h + 1)
                        if h >= 2:
                            act.wait_ge(av_done, h - 1)
                        act.activation(PT[:, h % 2, :], T0[:, :], ACT.Copy).then_inc(pt_ready, 1)

                    fetch_k(0)
                    fetch_k(1)
                    exponents(0)
                    for h in range(HEADS3):
                        if h + 1 < HEADS3:
                            exponents(h + 1)
                        fetch_turned(h)
                        if h + 2 < HEADS3:
                            fetch_k(h + 2)
                    act.wait_ge(last_flipped, 1)
                    act.activation(w17, T0[0:17, 0:S], ACT.Copy).then_inc(w17_ready, 1)
                    meet(act, "act")

            def pool_program(pool):
                pool.memset(dm, 0.0).then_inc(dm_ready, 1)
                pool.wait_ge(dm_ready, 3 * a + 1)
                pool.tensor_tensor(dm[:, 0:HEADS3 * 17:18], head_cols(f"bias_v{a + 1}"), head_cols(f"bv{a + 1}"),
                                   ALU.subtract).then_inc(dm_ready, 1)
                pool.tensor_copy(dm.rearrange("p (h n) -> p h n", n=17)[:, :, 16],
                                 head_cols(f"bv{a + 1}")).then_inc(dm_ready, 1)
                with pool.Fori(0, B) as b:
                    take_root(pool, var_ready, rstd_ready, 1)
                    pool.tensor_copy(aT[:, :, :], ctxT[:, :, bass.ds(b * S, S)]).then_inc(aT_ready, 1)
                    pool.memset(weightT[:, :, 16:17], 1.0)
                    for h in range(HEADS3):
                        pool.wait_ge(probs_ready, h + 1)
                        pool.tensor_copy(weightT[:, :, h:h + 1], P_[h % 2][:, :, S:T]).then_inc(last_ready, 1)
                    meet(pool, "pool")

            def dve_program(dve):
                dve.wait_ge(v17_ready, a + 1)
                with dve.Fori(0, B) as b:
                    chain = Chain(dve, dve_chain)

                    def x_tile(t):
                        return x_tok[:, bass.ds(b * TQ + t, 1), :].rearrange("p a c -> p (a c)")

                    normalise(dve, chain, x_tile, xn, EPS, var_ready, rstd_ready, 1, xn_ready)

                    def fetch_qv(h):
                        dve.wait_ge(qk_done, h + 1)
                        if h >= 2:
                            dve.wait_ge(logits_done, h - 1)
                        dve.tensor_scalar(QK[:, h % 2, 0, 0:S], J0[:, 0:S], head_cols(f"bq{a + 1}")[:, h:h + 1],
                                          scale, ALU.add, ALU.mult).then_inc(q_ready, 1)
                        if h % 2 == 0:
                            dve.wait_ge(v_done, h // 2 + 1)
                            if h >= 4:
                                dve.wait_ge(av_done, h - 2)
                            dve.tensor_copy(V_[h // 2 % 2][:, :, :], two(J1)).then_inc(v_ready, 1)

                    def maxima(h):
                        dve.wait_ge(logits_done, h + 1)
                        for qt in range(TQ):
                            ins = dve.tensor_reduce(maxes[:, qt, h:h + 1], L_[h % 2][qt][:, 0:T], AX_X, ALU.max,
                                                    negate=True)
                        ins.then_inc(max_ready, 1)

                    def divide(h):
                        dve.wait_ge(exp_ready, h + 1)
                        chain.link(dve.reciprocal(inv[:, :, h:h + 1], sums[:, :, h:h + 1]))
                        for qt in range(TQ):
                            ins = dve.tensor_scalar(P_[h % 2][:, qt, :], P_[h % 2][:, qt, :], inv[:, qt, h:h + 1],
                                                    None, ALU.mult)
                        ins.then_inc(probs_ready, 1)

                    def fetch_av(h):
                        dve.wait_ge(av_done, h + 1)
                        dve.tensor_copy(avT[:, h, :], T1[:, 0:S]).then_inc(av_ready, 1)

                    fetch_qv(0)
                    fetch_qv(1)
                    maxima(0)
                    for h in range(HEADS3):
                        if h + 1 < HEADS3:
                            maxima(h + 1)
                        divide(h)
                        if h + 2 < HEADS3:
                            fetch_qv(h + 2)
                        fetch_av(h)
                    dve.wait_ge(out_done, 1)
                    x_b = x_tok[:, bass.ds(b * TQ, TQ), :]
                    bo = row(f"L3_xattn_bo{a + 1}").unsqueeze(1).to_broadcast([P, TQ, C])
                    chain.link(dve.tensor_tensor(xn[:, :, :], two(J0), bo, ALU.add))
                    dve.tensor_tensor(x_b, x_b, xn[:, :, :], ALU.add).then_inc(batch_done, 1)
                    dve.wait_ge(batch_done, 1)
                    meet(dve, "dve")

            programs["pe"].append(pe_program)
            programs["act"].append(act_program)
            programs["pool"].append(pool_program)
            programs["dve"].append(dve_program)

        def mlp():
            xn_ready, xn_flipped, hT_ready, fc1_done = (step(n) for n in
                                                        ("xn_ready", "xn_flipped", "hT_ready", "fc1_done"))
            gelu_ready, fc2_done, batch_done = (step(n) for n in ("gelu_ready", "fc2_done", "batch_done"))
            var_ready, rstd_ready, dve_chain = (step(n) for n in ("var_ready", "rstd_ready", "dve_chain"))
            hidden = km0[:, 0:FF // P * S].rearrange("p (m n) -> p m n", n=S)
            banks = [J0, J1, S0, S1]

            def pe_program(pe):
                pe.wait_ge(loaded["fc"], 16 * 2)
                with pe.Fori(0, B) as b:
                    pe.wait_ge(xn_ready, 1)
                    flip(pe, T0, xn, xn_flipped)
                    pe.wait_ge(hT_ready, 1)
                    for i, bank_ in enumerate(banks):
                        project(pe, bank_, lambda k, o: fc1[:, k, (2 * i + o) * P:(2 * i + o + 1) * P],
                                hT[:, :, 0:S], 2, fc1_done)
                    for m in range(FF // P):
                        pe.wait_ge(gelu_ready, m + 1)
                        for t, bank_ in enumerate((O0, O1)):
                            mm = pe.matmul(bank_[:, 0:C], hidden[:, m, t * P:(t + 1) * P], fc2[:, m, :],
                                           start=(m == 0), stop=(m == FF // P - 1))
                    mm.then_inc(fc2_done, 1)
                    meet(pe, "pe")

            def act_program(act):
                with act.Fori(0, B) as b:
                    act.wait_ge(xn_flipped, 1)
                    for k in range(KC):
                        ins = act.activation(hT[:, k, 0:S], T0[:, k * S:(k + 1) * S], ACT.Identity,
                                             bias=col("L3_xattn_ln_mlp_offset", k),
                                             scale=col("L3_xattn_ln_mlp_scale", k))
                    ins.then_inc(hT_ready, 1)
                    for m in range(FF // P):
                        if m % 2 == 0:
                            act.wait_ge(fc1_done, m // 2 + 1)
                        act.activation(hidden[:, m, :], banks[m // 2][:, m % 2 * S:(m % 2 + 1) * S], ACT.Gelu,
                                       bias=fc1_cols[:, m:m + 1]).then_inc(gelu_ready, 1)
                    meet(act, "act")

            def pool_program(pool):
                with pool.Fori(0, B) as b:
                    take_root(pool, var_ready, rstd_ready, 1)
                    meet(pool, "pool")

            def dve_program(dve):
                with dve.Fori(0, B) as b:
                    chain = Chain(dve, dve_chain)

                    def x_tile(t):
                        return x_tok[:, bass.ds(b * TQ + t, 1), :].rearrange("p a c -> p (a c)")

                    normalise(dve, chain, x_tile, xn, EPS, var_ready, rstd_ready, 1, xn_ready)
                    x_b = x_tok[:, bass.ds(b * TQ, TQ), :]
                    b_fc2 = row("L3_xattn_b_fc2").unsqueeze(1).to_broadcast([P, TQ, C])
                    chain.link(dve.tensor_tensor(xs[:, :, :], x_b, b_fc2, ALU.add))
                    dve.wait_ge(fc2_done, 1)
                    for t, bank_ in enumerate((O0, O1)):
                        ins = dve.tensor_tensor(x_tile(t), bank_[:, 0:C], xs[:, t, :], ALU.add)
                    ins.then_inc(batch_done, 1)
                    dve.wait_ge(batch_done, 1)
                    meet(dve, "dve")

            programs["pe"].append(pe_program)
            programs["act"].append(act_program)
            programs["pool"].append(pool_program)
            programs["dve"].append(dve_program)

        small_attention(0)
        if LAST_LAYER > 1:
            rwkv_block()
        if LAST_LAYER > 2:
            small_attention(2)
        if LAST_LAYER > 3:
            wide_attention(0)
            wide_attention(1)
            mlp()

        @block.sync
        def _(sp):
            def load(dst, name, group, src=None):
                sp.dma_start(dst, d[name] if src is None else src).then_inc(loaded[group], 16)

            def split_k(a):
                return a.rearrange("(k p) n -> p k n", p=P)

            load(ident[:, :], "ident", "const")
            load(head8[:, :], "head8", "const")
            load(head16[:, :], "head16", "const")
            load(cols[:, :], "cols", "const")
            load(gate[:, 0:1], "L0_xattn_gate", "const",
                 d["L0_xattn_gate"].rearrange("(o n) -> o n", o=1).to_broadcast([P, 1]))
            load(ctx_tok, "ctx", "ctx", d["ctx"].rearrange("(t p) c -> p t c", p=P))
            load(mask_bytes, "mask0", "ctx", d["mask0"].rearrange("(o n) -> o n", o=1).to_broadcast([P, N]))
            load(x_tok[:, :, :], "x", "x", d["x"].rearrange("(t p) c -> p t c", p=P))
            for n in ("L0_q", "L0_k", "L0_v", "L0_o"):
                load(w[n], n, "w0", split_k(d[n]))
            sp.wait_ge(loaded["w0"], 64)
            load(ctxT[:, :, :], "ctxT", "ctxT", split_k(d["ctxT"]))
            load(rows[:, :, :], "rows", "ctxT",
                 d["rows"].rearrange("(o r) n -> o r n", o=1).to_broadcast([P, len(ROWS), C]))
            if LAST_LAYER > 1:
                load_layer1(load, split_k, lambda: sp.wait_ge(w2_cleared, 1))
            if LAST_LAYER > 2:
                for n in ("L2_q", "L2_k", "L2_v", "L2_o"):
                    load(w[n], n, "w2", split_k(d[n]))
                load(mask2, "mask2", "w2", d["mask2"].rearrange("(t p) s -> p t s", p=P))
            for i in range(len(programs["pe"])):
                lead(sp)
                if i % 2 == 0 and i < 3 and LAST_LAYER > 3:
                    a = i // 2
                    for n, dst in zip("qkv", wide[a][:3]):
                        load(dst, f"w{n}{a + 1}", f"wide{a}", split_k(d[f"L3_xattn_w{n}{a + 1}"]))
                    load(wide[a][3], f"wo{a + 1}", f"wide{a}",
                         d[f"L3_xattn_wo{a + 1}"].rearrange("(h p) n -> p h n", p=P))
                if i == 3:
                    load(fc1, "fc1", "fc", split_k(d["L3_xattn_w_fc1"]))
                    load(fc2, "fc2", "fc", d["L3_xattn_w_fc2"].rearrange("(m p) n -> p m n", p=P))
            sp.dma_start(out.rearrange("(t p) c -> p t c", p=P), x_tok[:, :, :]).then_inc(stored, 16)
            sp.wait_ge(stored, 16)

        @block.tensor
        def _(pe):
            for program in programs["pe"]:
                program(pe)

        @block.vector
        def _(dve):
            for program in programs["dve"]:
                program(dve)

        @block.scalar
        def _(act):
            for program in programs["act"]:
                program(act)

        @block.gpsimd
        def _(pool):
            pool.memset(w2, 0.0).then_inc(w2_cleared, 1)
            for program in programs["pool"]:
                program(pool)


def kernel(**inputs):
    import concourse.bacc as bacc
    from concourse.bass_utils import run_bass_kernel_spmd

    a = {k: np.ascontiguousarray(v) for k, v in inputs.items()}

    def t(name):
        return np.ascontiguousarray(a[name].T)

    arrays = {
        "x": a["x"].reshape(N, C),
        "ctx": a["ctx_2048"].reshape(N, C),
        "ctxT": np.ascontiguousarray(a["ctx_2048"].reshape(N, C).T),
        "state0": np.ascontiguousarray(a["ctx_2048"][:, 2:2 + DIM1].reshape(B, KC, P, DIM1)
                                       .transpose(2, 0, 1, 3)).reshape(P, B, KC * DIM1),
        "mask0": a["mask_BxS2_bf1"].reshape(N).view(np.uint8),
        "mask2": a["mask_Bx1xSxS2_ff0"].reshape(N, S),
        "L0_xattn_gate": a["L0_xattn_gate"],
        "ident": np.eye(P, dtype=np.float32),
        "head8": np.repeat(np.eye(P // 8, dtype=np.float32), 8, axis=0),
        "head16": np.repeat(np.eye(P // 16, dtype=np.float32), 16, axis=0),
        "L0_q": t("L0_xattn_Wq"), "L0_k": t("L0_xattn_Wk"), "L0_v": t("L0_xattn_Wv"), "L0_o": t("L0_xattn_Wo"),
        "L1_r": t("L1_xattn_Wr"), "L1_k": t("L1_xattn_Wk"), "L1_v": t("L1_xattn_Wv"), "L1_g": t("L1_xattn_Wg"),
        "L1_o": t("L1_xattn_Wo"), "L1_fk": t("L1_xattn_fWk"), "L1_fr": t("L1_xattn_fWr"),
        "L1_fv": t("L1_xattn_fWv"),
        "L1_w1": a["L1_xattn_maa_w1"], "L1_w2": a["L1_xattn_maa_w2"].reshape(MIX * DMIX, C),
        "L1_dec1": a["L1_xattn_decay_w1"], "L1_dec2": a["L1_xattn_decay_w2"],
        "L2_q": a["L2_xattn_Wq"], "L2_v": a["L2_xattn_Wv"],
        "L2_k": np.repeat(a["L2_xattn_Wk"].reshape(C, KV2, 1, DIM2), HEADS2 // KV2, axis=2).reshape(C, C),
        "L2_o": a["L2_xattn_Wo"],
    }
    for n in ("wq1", "wk1", "wv1", "wo1", "wq2", "wk2", "wv2", "wo2", "w_fc1", "w_fc2"):
        arrays["L3_xattn_" + n] = a["L3_xattn_" + n]
    a["bk_of_q_heads"] = np.repeat(a["L2_xattn_bk"].reshape(KV2, 1, DIM2), HEADS2 // KV2, axis=1)
    arrays["cols"] = np.concatenate(
        [a[n].reshape(KC, P).T for n in COLS] + [a["L3_xattn_" + n].reshape(HEADS3, P).T for n in HEAD_COLS]
        + [a["L3_xattn_b_fc1"].reshape(FF // P, P).T], axis=1)
    arrays["rows"] = np.stack([np.resize(a[n], C) for n in ROWS])
    arrays = {k: np.ascontiguousarray(v) for k, v in arrays.items()}

    nc = bacc.Bacc("TRN2", target_bir_lowering=False, num_devices=1)
    dram = {k: nc.dram_tensor("in_" + k, v.shape, mybir.dt.from_np(v.dtype), kind="ExternalInput").ap()
            for k, v in arrays.items()}
    out = nc.dram_tensor("out", (N, C), F32, kind="ExternalOutput").ap()
    build(nc, dram, out)
    r = run_bass_kernel_spmd(nc, [{"in_" + k: v for k, v in arrays.items()}], core_ids=[0])
    return r.results[0]["out"].reshape(B, S, C)
```

```python
from contextlib import ExitStack

import numpy as np

import concourse.bass as bass
from concourse import mybir

ALU = mybir.AluOpType
ACT = mybir.ActivationFunctionType
AX_X = mybir.AxisListType.X
F32 = mybir.dt.float32
BF16 = mybir.dt.bfloat16
U8 = mybir.dt.uint8

P = 128
B, S, C = 4, 256, 256
N = B * S
TQ = S // P
KC = C // P
LAST_LAYER = 4

HEADS0, DIM0 = 16, 16
HEADS2, DIM2, KV2 = 32, 8, 8
HEADS1, DIM1, MIX, DMIX, DDEC = 32, 8, 5, 32, 64
HEADS3, DIM3, FF = 16, 128, 1024
EPS = 1e-5
EPS2 = 1e-6
BIG = 3.0e38

COLS = ["L0_xattn_ln_gamma", "L0_xattn_ln_beta", "L1_xattn_ln1_w", "L1_xattn_ln1_b", "L1_xattn_ln2_w",
        "L1_xattn_ln2_b", "L1_xattn_maa_x", "L1_xattn_maa_w", "L1_xattn_maa_k", "L1_xattn_maa_v",
        "L1_xattn_maa_r", "L1_xattn_maa_g", "L1_xattn_time_decay", "L1_xattn_faaaa", "L1_xattn_fmaa_k",
        "L1_xattn_fmaa_r", "L2_xattn_bq", "bk_of_q_heads", "L3_xattn_ln1_scale", "L3_xattn_ln1_offset",
        "L3_xattn_ln2_scale", "L3_xattn_ln2_offset", "L3_xattn_ln_mlp_scale", "L3_xattn_ln_mlp_offset"]
HEAD_COLS = ["bq1", "bk1", "bv1", "bias_k1", "bias_v1", "bq2", "bk2", "bv2", "bias_k2", "bias_v2"]
ROWS = ["L1_xattn_gn_w", "L1_xattn_gn_b", "L2_xattn_bo", "L2_xattn_gamma", "L2_xattn_beta",
        "L3_xattn_bo1", "L3_xattn_bo2", "L3_xattn_b_fc2", "L2_xattn_bv"]
N_HEAD_COLS = len(HEAD_COLS) * HEADS3
N_COLS = len(COLS) * KC + N_HEAD_COLS + FF // P


class Chain:

    def __init__(self, eng, sem):
        self.eng, self.sem, self.n = eng, sem, 0

    def link(self, ins):
        self.n += 1
        ins.then_inc(self.sem, 1)
        self.eng.wait_ge(self.sem, self.n)


def build(nc, d, out):
    with ExitStack() as ctx:
        def sb(name, shape, dt=F32):
            return ctx.enter_context(nc.sbuf_tensor(name, shape, dt))

        def bank(name):
            return ctx.enter_context(nc.psum_tensor(name, [P, 512], F32))

        def sem(name):
            return ctx.enter_context(nc.semaphore(name))

        J0, J1, S0, S1, T0, T1, O0, O1 = (bank(n) for n in ("J0", "J1", "S0", "S1", "T0", "T1", "O0", "O1"))

        def two(x):
            return x[:, :].rearrange("p (a n) -> p a n", a=2)

        ident = sb("ident", [P, P])
        head8 = sb("head8", [P, P // DIM1])
        head16 = sb("head16", [P, P // DIM0])
        cols = sb("cols", [P, N_COLS])
        rows = sb("rows", [P, len(ROWS), C])
        x_tok = sb("x_tok", [P, B * TQ, C])
        ctxT = sb("ctxT", [P, KC, N])
        weights_a = sb("weights_a", [P, 4 * 4096])
        early = sb("early", [P, 4 * 4096])
        km0 = sb("km0", [P, 16 * S])

        def col(name, k):
            i = COLS.index(name) * KC + k
            return cols[:, i:i + 1]

        def head_cols(name):
            i = len(COLS) * KC + HEAD_COLS.index(name) * HEADS3
            return cols[:, i:i + HEADS3]

        fc1_cols = cols[:, N_COLS - FF // P:N_COLS]

        def row(name):
            return rows[:, ROWS.index(name), :]

        taken = [0]

        def carve(n, pattern=None, **sizes):
            at = taken[0]
            taken[0] += n
            assert taken[0] <= 4 * 4096
            v = early[:, at:at + n]
            return v.rearrange(pattern, **sizes) if pattern else v

        km1 = carve(16 * S)
        km = [km0[:, :].rearrange("p (h n) -> p h n", h=16), km1.rearrange("p (h n) -> p h n", h=16)]
        w = {}
        WEIGHTS = ["L0_q", "L0_k", "L0_v", "L0_o", "L1_r", "L1_k", "L1_v", "L1_g", "L1_o", "L1_fk", "L1_fr",
                   "L1_fv", "L2_q", "L2_k", "L2_o"]
        for n in WEIGHTS:
            w[n] = carve(KC * C, "p (k n) -> p k n", k=KC)
        w["L2_v"] = carve(KC * KV2 * DIM2, "p (k n) -> p k n", k=KC)
        w1 = carve(KC * MIX * DMIX, "p (k n) -> p k n", k=KC)
        w2 = carve(4 * C, "p (f n) -> p f n", f=4)
        w2_last = carve(C)
        dec1 = carve(KC * DDEC, "p (k n) -> p k n", k=KC)
        dec2 = carve(C)
        mask2 = carve(B * TQ * S, "p (t n) -> p t n", t=B * TQ)

        ctx_tok = weights_a[:, 0:B * TQ * C].rearrange("p (t c) -> p t c", c=C)
        mask0 = weights_a[:, 2048:2048 + N]
        mask_bytes = weights_a[:, 3072:3072 + N // 4].bitcast(U8)

        def wide_weights(region):
            q, k, v, o = (region[:, i * 4096:(i + 1) * 4096] for i in range(4))
            return (q.rearrange("p (k n) -> p k n", k=KC), k.rearrange("p (k n) -> p k n", k=KC),
                    v.rearrange("p (k n) -> p k n", k=KC), o.rearrange("p (h n) -> p h n", h=HEADS3))

        wide = [wide_weights(weights_a[:, :]), wide_weights(early[:, :])]
        fc1 = weights_a[:, 0:KC * FF].rearrange("p (k n) -> p k n", k=KC)
        fc2 = weights_a[:, KC * FF:KC * FF + FF // P * C].rearrange("p (m n) -> p m n", m=FF // P)

        xs = sb("xs", [P, TQ, C])
        xn = sb("xn", [P, TQ, C])
        hT = sb("hT", [P, KC, S + 1])
        aT = sb("aT", [P, KC, S])
        QT = sb("QT", [P, KC, S])
        KT = sb("KT", [P, KC, S])
        V = sb("V", [P, TQ, C])
        masked = sb("masked", [P, 2, 512])
        probs = sb("probs", [P, 2, 514])
        PT = sb("PT", [P, 2, 512])
        On = sb("On", [P, TQ, C])
        OT = sb("OT", [P, KC, S])
        maxes = sb("maxes", [P, TQ, 32])
        sums = sb("sums", [P, TQ, 32])
        inv = sb("inv", [P, TQ, 32])
        stats = sb("stats", [P, TQ, 6])
        moments = sb("moments", [P, TQ, 2])
        rstd = sb("rstd", [P, 2, TQ, 1])
        gate = sb("gate", [P, 2])
        mask_b = sb("mask_b", [P, TQ, S])
        halves = sb("halves", [P, 1])
        QK = sb("QK", [P, 2, 2, 260])
        weightT = On[:, 0, 0:TQ * 17].rearrange("p (t h) -> p t h", t=TQ)
        w17, v17 = QT[0:17, 0, :], KT[0:17, 0, :]
        dm = masked[:, :, :].rearrange("p a n -> p (a n)")[:, 0:HEADS3 * 17]
        start_all = sb("start_all", [P, B, KC * DIM1])
        gn = QK[:, :, :, :].rearrange("p a b n -> p (a b n)")[:, 0:TQ * HEADS1 * 3]

        loaded = {n: sem(f"loaded_{n}") for n in
                  ("const", "x", "ctx", "ctxT", "w0", "w1", "w2", "wide0", "wide1", "fc")}
        arrived = sem("arrived")
        go = {n: sem(f"go_{n}") for n in ("pe", "act", "dve", "pool")}
        steps = {}
        v17_done, v17_ready, dm_ready = sem("v17_done"), sem("v17_ready"), sem("dm_ready")
        stored = sem("stored")
        halves_ready, mask_ready = sem("halves_ready"), sem("mask_ready")
        w2_cleared, select_ready = sem("w2_cleared"), sem("select_ready")
        neg_ready, gate_ready = sem("neg_ready"), sem("gate_ready")

        block = ctx.enter_context(nc.Block())
        programs = {"pe": [], "dve": [], "act": [], "pool": []}

        def normalise(dve, chain, src, dst, eps, rstd, var_ready, rstd_ready, turn, last_sem):
            for t in range(TQ):
                ins = dve.bn_stats(stats[:, t, :], src(t))
            chain.link(ins)
            for t in range(TQ):
                ins = dve.bn_aggr(moments[:, t, :], stats[:, t, :])
            chain.link(ins)
            dve.tensor_scalar(rstd[:, :, :], moments[:, :, 1:2], eps, None, ALU.add).then_inc(var_ready, 1)
            dve.wait_ge(rstd_ready, turn)
            for t in range(TQ):
                ins = dve.tensor_scalar(dst[:, t, :], src(t), moments[:, t, 0:1], rstd[:, t, :],
                                        ALU.subtract, ALU.mult)
            ins.then_inc(last_sem, 1)

        def take_root(pool, values, var_ready, rstd_ready, turn):
            pool.wait_ge(var_ready, turn)
            pool.tensor_tensor(values, values, halves[:, 0:1].to_broadcast(list(values.shape)), ALU.pow)\
                .then_inc(rstd_ready, 1)

        def step(name):
            if name not in steps:
                steps[name] = sem(name)
            return steps[name]

        def meet(eng, name):
            eng.drain().then_inc(arrived, 1)
            eng.wait_ge(go[name], 1)
            eng.sem_clear(go[name])

        def lead(sp, meetings):
            numbers = sorted(s.num for s in steps.values())
            assert numbers == list(range(numbers[0], numbers[-1] + 1))
            with sp.Fori(0, meetings):
                sp.wait_ge(arrived, len(go))
                sp.sem_clear(range(numbers[0], numbers[-1] + 1))
                sp.sem_clear(arrived)
                for s in go.values():
                    sp.sem_inc(s, 1)

        def flip(pe, bank_, src, done_sem):
            for k in range(KC):
                for t in range(TQ):
                    mm = pe.transpose(bank_[:, k * S + t * P:k * S + (t + 1) * P],
                                      src[:, t, k * P:(k + 1) * P], ident[:, :])
            mm.then_inc(done_sem, 1)

        def project(pe, bank_, weight, moving, n_out, done_sem):
            for o in range(n_out):
                for k in range(KC):
                    mm = pe.matmul(bank_[:, o * S:(o + 1) * S], weight(k, o), moving[:, k, :],
                                   start=(k == 0), stop=(k == KC - 1))
            if done_sem is not None:
                mm.then_inc(done_sem, 1)

        def project_tokens(pe, bank_, src, weight, n, done_sem):
            for t in range(TQ):
                for k in range(KC):
                    mm = pe.matmul(bank_[:, t * S:t * S + n], src[:, k, t * P:(t + 1) * P], weight(k),
                                   start=(k == 0), stop=(k == KC - 1))
            mm.then_inc(done_sem, 1)

        def x_of(b):
            return x_tok[:, bass.ds(b * TQ, TQ), :]

        def tile_of(src, b):
            return lambda t: src[:, bass.ds(b * TQ + t, 1), :].rearrange("p a c -> p (a c)")

        xn_ready, xs_ready = step("xn_ready"), step("xs_ready")
        x_flipped, a_flipped = step("x_flipped"), step("a_flipped")
        hT_ready, aT_ready, mask_b_ready = step("hT_ready"), step("aT_ready"), step("mask_b_ready")
        next_var_ready, next_rstd_ready = step("next_var_ready"), step("next_rstd_ready")
        own_rstd, next_rstd = rstd[:, 0], rstd[:, 1]

        def front_dve(layer, dve, chain, b):
            if layer == 2 or layer is None:
                return
            normalise(dve, chain, tile_of(ctx_tok if layer == 0 else x_tok, b), xn, EPS, next_rstd,
                      next_var_ready, next_rstd_ready, 1, xn_ready)

        def front_pool_first(layer, pool, b):
            if layer is None:
                return
            if layer in (0, 2):
                pool.tensor_copy(xs[:, :, :], x_of(b)).then_inc(xs_ready, 1)
            if layer != 2:
                take_root(pool, next_rstd.rearrange("p t o -> p (t o)"), next_var_ready, next_rstd_ready, 1)

        def front_pool_last(layer, pool, b):
            if layer == 0:
                pool.tensor_copy(mask_b[:, 0, :], mask0[:, bass.ds(b * S, S)]).then_inc(mask_b_ready, 1)
            if layer == 2:
                pool.tensor_copy(mask_b[:, :, :], mask2[:, bass.ds(b * TQ, TQ), :]).then_inc(mask_b_ready, 1)
            if layer in (2, 3, 4):
                pool.tensor_copy(aT[:, :, :], ctxT[:, :, bass.ds(b * S, S)]).then_inc(aT_ready, 1)

        def front_pe(layer, pe, bank_x, bank_a):
            if layer is None:
                return
            if layer in (0, 2):
                pe.wait_ge(xs_ready, 1)
                flip(pe, bank_x, xs, x_flipped)
            if layer == 0:
                pe.wait_ge(xn_ready, 1)
                flip(pe, bank_a, xn, a_flipped)
            if layer not in (0, 2):
                pe.wait_ge(xn_ready, 1)
                flip(pe, bank_x, xn, x_flipped)

        def front_act(layer, act, b, bank_x, bank_a):
            if layer is None:
                return
            if layer == 1:
                act.activation(hT[:, :, 0:1], ctxT[:, :, bass.ds(b * S + 1, 1)], ACT.Copy)
            act.wait_ge(x_flipped, 1)
            if layer in (0, 2):
                act.activation(hT[:, :, 0:S], two(bank_x), ACT.Copy).then_inc(hT_ready, 1)
            else:
                name, offset, scale = {1: ("L1_xattn_ln1", "_b", "_w"), 3: ("L3_xattn_ln1", "_offset", "_scale"),
                                       4: ("L3_xattn_ln2", "_offset", "_scale"),
                                       5: ("L3_xattn_ln_mlp", "_offset", "_scale")}[layer]
                at = 1 if layer == 1 else 0
                for k in range(KC):
                    ins = act.activation(hT[:, k, at:at + S], bank_x[:, k * S:(k + 1) * S], ACT.Identity,
                                         bias=col(name + offset, k), scale=col(name + scale, k))
                ins.then_inc(hT_ready, 1)
            if layer == 0:
                act.wait_ge(a_flipped, 1)
                for k in range(KC):
                    ins = act.activation(aT[:, k, :], bank_a[:, k * S:(k + 1) * S], ACT.Identity,
                                         bias=col("L0_xattn_ln_beta", k), scale=col("L0_xattn_ln_gamma", k))
                ins.then_inc(aT_ready, 1)

        def batches(eng, name, layer, last_layer, main):
            with eng.Fori(0, B - 1) as b:
                main(b, layer, b + 1)
                meet(eng, name)
            main(B - 1, None if last_layer else layer + 1, 0)
            meet(eng, name)

        def small_attention(layer):
            heads, dim = (HEADS0, DIM0) if layer == 0 else (HEADS2, DIM2)
            per_tile = P // dim
            head_of = head16 if layer == 0 else head8
            pairs = heads // 2
            items = pairs * TQ
            scale = float(dim) ** -0.5
            q_done, k_done, v_done = step("q_done"), step("k_done"), step("v_done")
            q_ready, k_ready, v_ready = step("q_ready"), step("k_ready"), step("v_ready")
            km_ready = step("km_ready")
            scores_done, max_ready = step("scores_done"), step("max_ready")
            probs_ready, probs_flipped = step("probs_ready"), step("probs_flipped")
            pt_ready, av_done = step("pt_ready"), step("av_done")
            on_ready, on_flipped, ot_ready = step("on_ready"), step("on_flipped"), step("ot_ready")
            out_done, batch_done = step("out_done"), step("batch_done")
            dve_chain = step("dve_chain")
            normed = step("normed")
            var_ready, rstd_ready = step("var_ready"), step("rstd_ready")
            S_, T_ = [S0, S1], [T0, T1]
            O_ = [O0, O1]
            wq, wk, wv, wo = (w[f"L{layer}_{n}"] for n in "qkvo")

            def pe_program(pe):
                pe.wait_ge(loaded["const"], 16 * 5)
                pe.wait_ge(loaded[f"w{layer}"], 16 * (4 if layer == 0 else 5))

                def main(b, following, b_next):
                    project(pe, J1, lambda k, o: wk[:, k, o * P:(o + 1) * P], aT, KC, k_done)
                    if layer == 0:
                        project_tokens(pe, O0, aT, lambda k: wv[:, k, :], C, v_done)
                    else:
                        project_tokens(pe, O0, aT, lambda k: wv[:, k, :], KV2 * DIM2, v_done)
                    project(pe, J0, lambda k, o: wq[:, k, o * P:(o + 1) * P], hT[:, :, 0:S], KC, q_done)

                    def scores(i):
                        pair, qt = i // TQ, i % TQ
                        half, h = pair * 2 // per_tile, pair * 2 % per_tile
                        if i == 0:
                            pe.wait_ge(q_ready, 1)
                        if qt == 0:
                            pe.wait_ge(km_ready, pair + 1)
                        if i >= 2:
                            pe.wait_ge(max_ready, i - 1)
                        pe.matmul(S_[i % 2][:, :], QT[:, half, qt * P:(qt + 1) * P],
                                  km[half][:, h:h + 2, :], start=True, stop=True).then_inc(scores_done, 1)

                    def turn(i):
                        pe.wait_ge(probs_ready, i + 1)
                        if i >= 2:
                            pe.wait_ge(pt_ready, i - 1)
                        for n in range(2 * TQ):
                            mm = pe.transpose(T_[i % 2][:, n * P:(n + 1) * P],
                                              probs[:, i % 2, n * P:(n + 1) * P], ident[:, :])
                        mm.then_inc(probs_flipped, 1)

                    def weigh(i):
                        pair, qt = i // TQ, i % TQ
                        pe.wait_ge(pt_ready, i + 1)
                        if i == 0:
                            pe.wait_ge(v_ready, 1)
                        for hh in range(2):
                            h = pair * 2 + hh
                            kv = h * dim if layer == 0 else h // (HEADS2 // KV2) * dim
                            for st in range(TQ):
                                mm = pe.matmul(O_[qt][:, h * dim:(h + 1) * dim],
                                               PT[:, i % 2, (hh * TQ + st) * P:(hh * TQ + st + 1) * P],
                                               V[:, st, kv:kv + dim], start=(st == 0), stop=(st == TQ - 1))
                        mm.then_inc(av_done, 1)

                    scores(0)
                    for i in range(items):
                        if i + 1 < items:
                            scores(i + 1)
                        turn(i)
                        if i >= 1:
                            weigh(i - 1)
                        if i == items // 2:
                            front_pe(following, pe, J0, J1)
                    weigh(items - 1)
                    pe.wait_ge(on_ready, 1)
                    pe.wait_ge(pt_ready, items)
                    flip(pe, T0, On, on_flipped)
                    pe.wait_ge(ot_ready, 1)
                    project_tokens(pe, O0, OT, lambda k: wo[:, k, :], C, out_done)

                if layer == 0:
                    front_pe(0, pe, J0, J1)
                    meet(pe, "pe")
                batches(pe, "pe", layer, layer == last_layer, main)

            def act_program(act):
                if layer == 0:
                    act.wait_ge(loaded["const"], 16 * 5)
                    act.activation(gate[:, 1:2], gate[:, 0:1], ACT.Tanh).then_inc(gate_ready, 1)

                def main(b, following, b_next):
                    act.wait_ge(k_done, 1)
                    for k in range(KC):
                        if layer == 0:
                            ins = act.activation(KT[:, k, :], J1[:, k * S:(k + 1) * S], ACT.Copy)
                        else:
                            ins = act.activation(KT[:, k, :], J1[:, k * S:(k + 1) * S], ACT.Identity,
                                                 bias=col("bk_of_q_heads", k))
                        ins.then_inc(k_ready, 1)
                    for i in range(items):
                        pair, qt = i // TQ, i % TQ
                        act.wait_ge(max_ready, i + 1)
                        if i >= 2:
                            act.wait_ge(probs_flipped, i - 1)
                        for hh in range(2):
                            h = pair * 2 + hh
                            ins = act.activation(probs[:, i % 2, hh * S:(hh + 1) * S],
                                                 masked[:, i % 2, hh * S:(hh + 1) * S], ACT.Exp,
                                                 bias=maxes[:, qt, h:h + 1], scale=-1.0,
                                                 accum_out=sums[:, qt, h:h + 1])
                        ins.then_inc(probs_ready, 1)
                        if i == items // 2 + 1:
                            act.wait_ge(q_done, 1)
                            act.wait_ge(v_done, 1)
                            front_act(following, act, b_next, J0, J1)
                    act.wait_ge(on_flipped, 1)
                    act.activation(OT[:, :, :], two(T0), ACT.Copy).then_inc(ot_ready, 1)

                if layer == 0:
                    front_act(0, act, 0, J0, J1)
                    act.wait_ge(loaded["ctxT"], 32)
                    meet(act, "act")
                batches(act, "act", layer, layer == last_layer, main)

            def pool_program(pool):
                if layer == 0:
                    pool.wait_ge(loaded["x"], 16)
                    pool.memset(halves[:, :], -0.5).then_inc(halves_ready, 1)
                    pool.wait_ge(halves_ready, 1)

                def main(b, following, b_next):
                    for pair in range(pairs):
                        half, h = pair * 2 // per_tile, pair * 2 % per_tile
                        if h == 0:
                            pool.wait_ge(k_ready, half + 1)
                        for hh in range(2):
                            ins = pool.tensor_scalar(km[half][:, h + hh, :], KT[:, half, :],
                                                     head_of[:, h + hh:h + hh + 1], 1.0, ALU.mult, ALU.mult)
                        ins.then_inc(km_ready, 1)
                    front_pool_first(following, pool, b_next)
                    if following == 1:
                        pass
                    else:
                        pool.wait_ge(max_ready, items)
                        front_pool_last(following, pool, b_next)
                    if layer == 2:
                        take_root(pool, own_rstd.rearrange("p t o -> p (t o)"), var_ready, rstd_ready, 1)

                if layer == 0:
                    front_pool_first(0, pool, 0)
                    pool.wait_ge(mask_ready, 2)
                    front_pool_last(0, pool, 0)
                    meet(pool, "pool")
                batches(pool, "pool", layer, layer == last_layer, main)

            def dve_program(dve):
                if layer == 0:
                    dve.wait_ge(loaded["ctx"], 32)
                    dve.tensor_scalar(mask0, mask_bytes, 1.0, -BIG, ALU.subtract, ALU.mult).then_inc(mask_ready, 1)
                    dve.wait_ge(mask_ready, 1)
                    dve.tensor_scalar(mask0, mask0, 2.0, None, ALU.mult).then_inc(mask_ready, 1)
                    dve.wait_ge(mask_ready, 2)
                    dve.wait_ge(gate_ready, 1)

                def main(b, following, b_next):
                    chain = Chain(dve, dve_chain)
                    dve.wait_ge(v_done, 1)
                    if layer == 0:
                        dve.tensor_copy(V[:, :, :], two(O0)).then_inc(v_ready, 1)
                    else:
                        n = KV2 * DIM2
                        dve.tensor_tensor(V[:, :, 0:n], two(O0)[:, :, 0:n],
                                          row("L2_xattn_bv")[:, 0:n].unsqueeze(1).to_broadcast([P, TQ, n]),
                                          ALU.add).then_inc(v_ready, 1)
                    dve.wait_ge(q_done, 1)
                    for k in range(KC):
                        if layer == 0:
                            ins = dve.tensor_scalar(QT[:, k, :], J0[:, k * S:(k + 1) * S], -scale, None, ALU.mult)
                        else:
                            ins = dve.tensor_scalar(QT[:, k, :], J0[:, k * S:(k + 1) * S], col("L2_xattn_bq", k),
                                                    -scale, ALU.add, ALU.mult)
                    ins.then_inc(q_ready, 1)

                    def add_mask(i):
                        pair, qt = i // TQ, i % TQ
                        dve.wait_ge(scores_done, i + 1)
                        if i >= 2:
                            dve.wait_ge(probs_ready, i - 1)
                        for hh in range(2):
                            h = pair * 2 + hh
                            ins = dve.tensor_tensor_reduce(
                                out=masked[:, i % 2, hh * S:(hh + 1) * S], in0=S_[i % 2][:, hh * S:(hh + 1) * S],
                                in1=mask_b[:, 0 if layer == 0 else qt, :], scale=1.0, scalar=BIG, op0=ALU.add, op1=ALU.min,
                                accum_out=maxes[:, qt, h:h + 1])
                        ins.then_inc(max_ready, 1)

                    def fetch_turned(i):
                        dve.wait_ge(probs_flipped, i + 1)
                        if i >= 2:
                            dve.wait_ge(av_done, i - 1)
                        dve.tensor_copy(PT[:, i % 2, :], T_[i % 2][:, :]).then_inc(pt_ready, 1)

                    for i in range(items):
                        add_mask(i)
                        if i >= 1:
                            fetch_turned(i - 1)
                        if i == items // 4:
                            front_dve(following, dve, chain, b_next)
                    fetch_turned(items - 1)
                    dve.wait_ge(probs_ready, items)
                    chain.link(dve.reciprocal(inv[:, :, 0:heads], sums[:, :, 0:heads]))
                    dve.wait_ge(av_done, items)
                    for qt in range(TQ):
                        ins = dve.tensor_tensor(On[:, qt, :].rearrange("p (h d) -> p h d", d=dim),
                                                O_[qt][:, 0:C].rearrange("p (h d) -> p h d", d=dim),
                                                inv[:, qt, 0:heads].unsqueeze(2).to_broadcast([P, heads, dim]),
                                                ALU.mult)
                    ins.then_inc(on_ready, 1)
                    dve.wait_ge(out_done, 1)
                    x_b = x_of(b)
                    if layer == 0:
                        dve.scalar_tensor_tensor(
                            out=x_b.rearrange("p t c -> p (t c)"), in0=O0[:, :], scalar=gate[:, 1:2],
                            in1=x_b.rearrange("p t c -> p (t c)"), op0=ALU.mult, op1=ALU.add)\
                            .then_inc(batch_done, 1)
                    else:
                        bo = row("L2_xattn_bo").unsqueeze(1).to_broadcast([P, TQ, C])
                        gamma = row("L2_xattn_gamma").unsqueeze(1).to_broadcast([P, TQ, C])
                        beta = row("L2_xattn_beta").unsqueeze(1).to_broadcast([P, TQ, C])
                        added = masked[:, 0, :].rearrange("p (t c) -> p t c", t=TQ)
                        result = masked[:, 1, :].rearrange("p (t c) -> p t c", t=TQ)
                        chain.link(dve.tensor_tensor(added, two(O0), x_b, ALU.add))
                        chain.link(dve.tensor_tensor(added, added, bo, ALU.add))
                        normalise(dve, chain, lambda t: added[:, t, :], result, EPS2, own_rstd,
                                  var_ready, rstd_ready, 1, normed)
                        dve.wait_ge(normed, 1)
                        chain.link(dve.tensor_tensor(result, result, gamma, ALU.mult))
                        dve.tensor_tensor(x_b, result, beta, ALU.add).then_inc(batch_done, 1)
                    dve.wait_ge(batch_done, 1)

                if layer == 0:
                    front_dve(0, dve, Chain(dve, dve_chain), 0)
                    meet(dve, "dve")
                batches(dve, "dve", layer, layer == last_layer, main)

            programs["pe"].append(pe_program)
            programs["act"].append(act_program)
            programs["pool"].append(pool_program)
            programs["dve"].append(dve_program)

        def rwkv_block():
            sx_ready = step("sx_ready")
            xxx_ready, lora_done, lora_ready = step("xxx_ready"), step("lora_done"), step("lora_ready")
            mix_done, mix_ready, xf_ready = step("mix_done"), step("mix_ready"), step("xf_ready")
            dec1_done, dec1_ready, dec2_done = step("dec1_done"), step("dec1_ready"), step("dec2_done")
            exp_ready, decay_ready = step("exp_ready"), step("decay_ready")
            k_done, v_done, r_done, g_done = (step(f"{n}_done") for n in "kvrg")
            k_ready, v_ready, r_ready, g_ready = (step(f"{n}_ready") for n in "kvrg")
            spread_done, kv_ready, start_ready = step("spread_done"), step("kv_ready"), step("start_ready")
            start_here, split = step("start_here"), step("split")
            vT_done, vT_ready, v_parts_ready = step("vT_done"), step("vT_ready"), step("v_parts_ready")
            state_ready, read_ready, y_done = step("state_ready"), step("read_ready"), step("y_done")
            rk_ready, ruk_ready, bonus_done = step("rk_ready"), step("ruk_ready"), step("bonus_done")
            yg_ready, yg_flipped, ygT_ready = step("yg_ready"), step("yg_flipped"), step("ygT_ready")
            out_done, x_ready = step("out_done"), step("x_ready")
            xc_flipped, xc_ready, sxc_ready = step("xc_flipped"), step("xc_ready"), step("sxc_ready")
            xk2_ready, xr2_ready = step("xk2_ready"), step("xr2_ready")
            fk_done, fr_done, relu_ready = step("fk_done"), step("fr_done"), step("relu_ready")
            kk_ready, rr_ready, fv_done = step("kk_ready"), step("rr_ready"), step("fv_done")
            var_ready, rstd_ready, xc_normed = step("var_ready"), step("rstd_ready"), step("xc_normed")
            batch_done, dve_chain = step("batch_done"), step("dve_chain")

            def scratch(half, at, n=KC * S):
                return [km0[:, :], km1][half][:, at:at + n]

            def pair(v):
                return v.rearrange("p (a n) -> p a n", a=2)

            xf = [pair(scratch(0, i * 512)) for i in range(MIX)]
            rT, kT, wT = (pair(scratch(0, 512 * i)) for i in (5, 6, 7))
            kv = [pair(scratch(1, 512 * i)) for i in (0, 1)]
            read = [pair(scratch(1, 512 * i)) for i in (2, 3)]
            state = [scratch(1, 2048 + 514 * i, 514).rearrange("p (a n) -> p a n", a=2) for i in (0, 1)]
            silu_g = scratch(1, 3076).rearrange("p (t c) -> p t c", t=TQ)
            start = scratch(1, 3588, KC * DIM1).rearrange("p (a j) -> p a j", a=2)
            sx, xxx = QT, KT
            mixed = [masked[:, i, :].rearrange("p (a n) -> p a n", a=2) for i in (0, 1)]
            lora = PT[:, 0, 0:S]
            lora_last = PT[0:DMIX, 0, S:2 * S]
            decay_in = PT[0:DDEC, 1, 0:S]
            ruk = pair(PT[:, 1, :])
            v_tok = V
            yv = probs[:, 0, 0:512]
            tmp = probs[:, 1, 0:512]
            xc = tmp.rearrange("p (t c) -> p t c", t=TQ)
            yv3, tmp3 = (v.rearrange("p (h j) -> p h j", j=DIM1) for v in (yv, tmp))
            mean, var = gn[:, 0:TQ * HEADS1], gn[:, TQ * HEADS1:2 * TQ * HEADS1]
            bonus = gn[:, 2 * TQ * HEADS1:3 * TQ * HEADS1]
            mix_banks = [S0, S1, T1, O0, O1]
            spread_banks = [T0, J1]
            heads_tile = P // DIM1

            select = mask_b[:, :, :].rearrange("p t n -> p (t n)").bitcast(BF16)
            rest = aT[:, :, :].rearrange("p k n -> p (k n)")
            halves_of_on = On[:, :, :].rearrange("p t n -> p (t n)").bitcast(BF16)
            v_parts = [halves_of_on[:, 0:512], halves_of_on[:, 512:1024],
                       OT[:, :, :].rearrange("p k n -> p (k n)").bitcast(BF16)[:, 0:512]]

            def pe_program(pe):
                pe.wait_ge(loaded["w1"], 16 * 17)
                pe.wait_ge(select_ready, 1)

                def main(b, following, b_next):
                    pe.wait_ge(xxx_ready, 1)
                    for k in range(KC):
                        pe.matmul(J0[:, 0:S], w1[:, k, 0:P], xxx[:, k, :], start=(k == 0), stop=(k == KC - 1))
                    for k in range(KC):
                        mm = pe.matmul(J0[0:DMIX, S:2 * S], w1[:, k, P:P + DMIX], xxx[:, k, :],
                                       start=(k == 0), stop=(k == KC - 1))
                    mm.then_inc(lora_done, 1)
                    pe.wait_ge(lora_ready, 1)
                    for f in range(MIX):
                        for o in range(KC):
                            if f < 4:
                                mm = pe.matmul(mix_banks[f][:, o * S:(o + 1) * S], w2[:, f, o * P:(o + 1) * P], lora,
                                               start=True, stop=True)
                            else:
                                mm = pe.matmul(mix_banks[f][:, o * S:(o + 1) * S],
                                               w2_last[0:DMIX, o * P:(o + 1) * P], lora_last, start=True, stop=True)
                        mm.then_inc(mix_done, 1)
                    pe.wait_ge(xf_ready, 1)
                    for k in range(KC):
                        mm = pe.matmul(J1[0:DDEC, 0:S], dec1[:, k, :], xf[0][:, k, :], start=(k == 0), stop=(k == KC - 1))
                    mm.then_inc(dec1_done, 1)
                    pe.wait_ge(xf_ready, 2)
                    project(pe, S0, lambda k, o: w["L1_k"][:, k, o * P:(o + 1) * P], xf[1], KC, k_done)
                    pe.wait_ge(dec1_ready, 1)
                    for o in range(KC):
                        mm = pe.matmul(J0[:, o * S:(o + 1) * S], dec2[0:DDEC, o * P:(o + 1) * P], decay_in,
                                       start=True, stop=True)
                    mm.then_inc(dec2_done, 1)
                    pe.wait_ge(xf_ready, 3)
                    project_tokens(pe, S1, xf[2], lambda k: w["L1_v"][:, k, :], C, v_done)

                    def spread(j):
                        if j >= 2:
                            pe.wait_ge(kv_ready, j - 1)
                        for n, part in enumerate(v_parts):
                            mm = pe.matmul(spread_banks[j % 2][:, :], select[:, j * P:(j + 1) * P], part,
                                           start=(n == 0), stop=(n == len(v_parts) - 1))
                        mm.then_inc(spread_done, 1)

                    project(pe, J1, lambda k, o: w["L1_v"][:, k, o * P:(o + 1) * P], xf[2], KC, vT_done)
                    pe.wait_ge(xf_ready, 4)
                    project(pe, T1, lambda k, o: w["L1_r"][:, k, o * P:(o + 1) * P], xf[3], KC, r_done)
                    pe.wait_ge(xf_ready, 5)
                    project_tokens(pe, O0, xf[4], lambda k: w["L1_g"][:, k, :], C, g_done)
                    pe.wait_ge(v_parts_ready, 1)
                    spread(0)
                    spread(1)

                    def gather(j):
                        pe.wait_ge(read_ready, j + 1)
                        for t in range(TQ):
                            for half in range(KC):
                                at = t * C + half * P
                                y = O1[:, at:at + P].rearrange("p (h j) -> p h j", j=DIM1)[:, :, j]
                                mm = pe.matmul(y, read[j % 2][:, half, t * P:(t + 1) * P], head8[:, :],
                                               start=True, stop=True)
                        mm.then_inc(y_done, 1)

                    for j in range(DIM1):
                        if j + 2 < DIM1:
                            spread(j + 2)
                        if j == 1:
                            pe.wait_ge(ruk_ready, 1)
                            pe.wait_ge(k_ready, 1)
                            for t in range(TQ):
                                for half in range(KC):
                                    at = t * HEADS1 + half * heads_tile
                                    mm = pe.matmul(S0[:, at:at + heads_tile], ruk[:, half, t * P:(t + 1) * P],
                                                   head8[:, :], start=True, stop=True)
                            mm.then_inc(bonus_done, 1)
                        gather(j)
                    pe.wait_ge(yg_ready, 1)
                    flip(pe, T0, yv.rearrange("p (t c) -> p t c", t=TQ), yg_flipped)
                    pe.wait_ge(ygT_ready, 1)
                    project_tokens(pe, J0, OT, lambda k: w["L1_o"][:, k, :], C, out_done)
                    pe.wait_ge(xc_normed, 1)
                    flip(pe, T1, xc, xc_flipped)
                    pe.wait_ge(xk2_ready, 1)
                    project(pe, S0, lambda k, o: w["L1_fk"][:, k, o * P:(o + 1) * P], xf[0], KC, fk_done)
                    pe.wait_ge(xr2_ready, 1)
                    project_tokens(pe, S1, xf[1], lambda k: w["L1_fr"][:, k, :], C, fr_done)
                    front_pe(following, pe, J1, None)
                    pe.wait_ge(kk_ready, 1)
                    project_tokens(pe, O0, xf[3], lambda k: w["L1_fv"][:, k, :], C, fv_done)

                batches(pe, "pe", 1, last_layer == 1, main)

            def act_program(act):
                def main(b, following, b_next):
                    act.wait_ge(lora_done, 1)
                    act.activation(lora, J0[:, 0:S], ACT.Tanh)
                    act.activation(lora_last, J0[0:DMIX, S:2 * S], ACT.Tanh).then_inc(lora_ready, 1)
                    act.wait_ge(dec1_done, 1)
                    act.activation(decay_in, J1[0:DDEC, 0:S], ACT.Tanh).then_inc(dec1_ready, 1)
                    act.wait_ge(k_done, 1)
                    act.activation(kT, two(S0), ACT.Copy).then_inc(k_ready, 1)
                    act.wait_ge(dec2_done, 1)
                    for k in range(KC):
                        ins = act.activation(wT[:, k, :], J0[:, k * S:(k + 1) * S], ACT.Exp,
                                             bias=col("L1_xattn_time_decay", k))
                    ins.then_inc(exp_ready, 1)
                    act.wait_ge(exp_ready, 1)
                    act.activation(wT, wT, ACT.Exp, scale=-1.0).then_inc(decay_ready, 1)
                    act.wait_ge(v_done, 1)
                    act.activation(v_tok[:, :, :], two(S1), ACT.Copy).then_inc(v_ready, 1)
                    act.wait_ge(vT_done, 1)
                    act.activation(rest, J1[:, :], ACT.Copy)
                    act.activation(v_parts[0], J1[:, :], ACT.Copy).then_inc(vT_ready, 1)
                    act.wait_ge(r_done, 1)
                    act.activation(rT, two(T1), ACT.Copy).then_inc(r_ready, 1)
                    act.wait_ge(start_here, 1)
                    for j in range(DIM1):
                        if j >= 2:
                            act.wait_ge(read_ready, j - 1)
                        act.activation(state[j % 2][:, :, 0:1], start[:, :, j:j + 1], ACT.Copy)\
                            .then_inc(start_ready, 1)
                    act.wait_ge(g_done, 1)
                    act.activation(silu_g, two(O0), ACT.Silu).then_inc(g_ready, 1)
                    act.wait_ge(yg_flipped, 1)
                    act.activation(OT[:, :, :], two(T0), ACT.Copy).then_inc(ygT_ready, 1)
                    act.wait_ge(xf_ready, MIX)
                    act.activation(hT[:, :, 0:1], ctxT[:, :, bass.ds(b * S, 1)], ACT.Copy)
                    act.wait_ge(xc_flipped, 1)
                    for k in range(KC):
                        ins = act.activation(hT[:, k, 1:S + 1], T1[:, k * S:(k + 1) * S], ACT.Identity,
                                             bias=col("L1_xattn_ln2_b", k), scale=col("L1_xattn_ln2_w", k))
                    ins.then_inc(xc_ready, 1)
                    act.wait_ge(fk_done, 1)
                    act.activation(xf[2], two(S0), ACT.Relu).then_inc(relu_ready, 1)
                    act.wait_ge(relu_ready, 1)
                    act.activation(xf[3], xf[2], ACT.Square).then_inc(kk_ready, 1)
                    act.wait_ge(fr_done, 1)
                    act.activation(silu_g, two(S1), ACT.Sigmoid).then_inc(rr_ready, 1)
                    act.wait_ge(xr2_ready, 1)
                    front_act(following, act, b_next, J1, None)

                batches(act, "act", 1, last_layer == 1, main)

            def pool_program(pool):
                pool.wait_ge(loaded["w1"], 16 * 17)
                pool.wait_ge(loaded["ctxT"], 32)
                for j in range(DIM1):
                    ins = pool.tensor_copy(
                        select[:, j * P:(j + 1) * P].rearrange("p (h i) -> p h i", i=DIM1),
                        ident[:, j:P:DIM1].unsqueeze(2).to_broadcast([P, heads_tile, DIM1]))
                ins.then_inc(select_ready, 1)

                def main(b, following, b_next):
                    pool.tensor_copy(start.rearrange("p a j -> p (a j)"),
                                     start_all[:, bass.ds(b, 1), :].rearrange("p o n -> p (o n)"))\
                        .then_inc(start_here, 1)
                    for f in range(MIX):
                        pool.wait_ge(mix_ready, f + 1)
                        pool.tensor_tensor(xf[f], mixed[f % 2], hT[:, :, 1:S + 1], ALU.add).then_inc(xf_ready, 1)
                    pool.wait_ge(vT_ready, 1)
                    pool.tensor_tensor(rest, rest, v_parts[0], ALU.subtract).then_inc(split, 1)
                    pool.wait_ge(split, 1)
                    pool.tensor_copy(v_parts[1], rest).then_inc(split, 1)
                    pool.wait_ge(split, 2)
                    pool.tensor_tensor(rest, rest, v_parts[1], ALU.subtract).then_inc(split, 1)
                    pool.wait_ge(split, 3)
                    pool.tensor_copy(v_parts[2], rest).then_inc(v_parts_ready, 1)
                    front_pool_first(following, pool, b_next)
                    take_root(pool, var, var_ready, rstd_ready, 1)
                    if following == 2:
                        pool.wait_ge(loaded["w2"], 16 * 5)
                        pool.tensor_scalar(mask2[:, :, :], mask2[:, :, :], -1.0, 0.0, ALU.mult, ALU.add)\
                            .then_inc(neg_ready, 1)
                        pool.wait_ge(neg_ready, 1)
                        pool.wait_ge(spread_done, DIM1)
                    front_pool_last(following, pool, b_next)
                    take_root(pool, own_rstd.rearrange("p t o -> p (t o)"), var_ready, rstd_ready, 2)

                batches(pool, "pool", 1, last_layer == 1, main)

            def dve_program(dve):
                dve.wait_ge(loaded["ctxT"], 32)

                def main(b, following, b_next):
                    chain = Chain(dve, dve_chain)
                    x_b = x_of(b)
                    dve.tensor_tensor(sx[:, :, :], hT[:, :, 0:S], hT[:, :, 1:S + 1], ALU.subtract).then_inc(sx_ready, 1)
                    dve.wait_ge(sx_ready, 1)
                    for k in range(KC):
                        ins = dve.scalar_tensor_tensor(out=xxx[:, k, :], in0=sx[:, k, :], scalar=col("L1_xattn_maa_x", k),
                                                       in1=hT[:, k, 1:S + 1], op0=ALU.mult, op1=ALU.add)
                    ins.then_inc(xxx_ready, 1)
                    for f, n in enumerate("wkvrg"):
                        dve.wait_ge(mix_done, f + 1)
                        if f >= 2:
                            dve.wait_ge(xf_ready, f - 1)
                        for k in range(KC):
                            ins = dve.scalar_tensor_tensor(out=mixed[f % 2][:, k, :],
                                                           in0=mix_banks[f][:, k * S:(k + 1) * S],
                                                           scalar=col("L1_xattn_maa_" + n, k), in1=sx[:, k, :],
                                                           op0=ALU.add, op1=ALU.mult)
                        ins.then_inc(mix_ready, 1)

                    def times_k(j):
                        dve.wait_ge(spread_done, j + 1)
                        if j >= 2:
                            dve.wait_ge(state_ready, j - 1)
                        dve.tensor_tensor(kv[j % 2], kT, two(spread_banks[j % 2]), ALU.mult).then_inc(kv_ready, 1)

                    dve.wait_ge(k_ready, 1)
                    times_k(0)
                    dve.wait_ge(r_ready, 1)
                    dve.wait_ge(decay_ready, 1)
                    for k in range(KC):
                        ins = dve.scalar_tensor_tensor(out=ruk[:, k, :], in0=rT[:, k, :], scalar=col("L1_xattn_faaaa", k),
                                                       in1=kT[:, k, :], op0=ALU.mult, op1=ALU.mult)
                    ins.then_inc(ruk_ready, 1)
                    for j in range(DIM1):
                        dve.wait_ge(kv_ready, j + 1)
                        dve.wait_ge(start_ready, j + 1)
                        if j >= 2:
                            dve.wait_ge(read_ready, j - 1)
                        for half in range(KC):
                            ins = dve.tensor_tensor_scan(state[j % 2][:, half, 1:S + 1], wT[:, half, :],
                                                         kv[j % 2][:, half, :], start[:, half, j:j + 1],
                                                         ALU.mult, ALU.add)
                        ins.then_inc(state_ready, 1)
                        if j + 1 < DIM1:
                            times_k(j + 1)
                        dve.wait_ge(state_ready, j + 1)
                        if j >= 2:
                            dve.wait_ge(y_done, j - 1)
                        dve.tensor_tensor(read[j % 2], rT, state[j % 2][:, :, 0:S], ALU.mult).then_inc(read_ready, 1)
                    front_dve(following, dve, chain, b_next)
                    dve.wait_ge(bonus_done, 1)
                    dve.wait_ge(v_ready, 1)
                    chain.link(dve.tensor_tensor(tmp3, v_tok[:, :, :].rearrange("p t (h j) -> p (t h) j", j=DIM1),
                                                 S0[:, 0:TQ * HEADS1].unsqueeze(2).to_broadcast([P, TQ * HEADS1, DIM1]),
                                                 ALU.mult))
                    dve.wait_ge(y_done, DIM1)
                    chain.link(dve.tensor_tensor(yv, O1[:, :], tmp, ALU.add))
                    chain.link(dve.tensor_reduce(mean, yv3, AX_X, ALU.add))
                    chain.link(dve.tensor_scalar(mean, mean, 1.0 / DIM1, None, ALU.mult))
                    wide_mean = mean.unsqueeze(2).to_broadcast([P, TQ * HEADS1, DIM1])
                    chain.link(dve.tensor_tensor(yv3, yv3, wide_mean, ALU.subtract))
                    chain.link(dve.tensor_tensor(tmp, yv, yv, ALU.mult))
                    chain.link(dve.tensor_reduce(var, tmp3, AX_X, ALU.add))
                    dve.tensor_scalar(var, var, 1.0 / DIM1, EPS, ALU.mult, ALU.add).then_inc(var_ready, 1)
                    dve.wait_ge(rstd_ready, 1)
                    wide_rstd = var.unsqueeze(2).to_broadcast([P, TQ * HEADS1, DIM1])
                    chain.link(dve.tensor_tensor(yv3, yv3, wide_rstd, ALU.mult))

                    def both(n):
                        return row(n).unsqueeze(1).to_broadcast([P, TQ, C])

                    y_t = yv.rearrange("p (t c) -> p t c", t=TQ)
                    chain.link(dve.tensor_tensor(y_t, y_t, both("L1_xattn_gn_w"), ALU.mult))
                    chain.link(dve.tensor_tensor(y_t, y_t, both("L1_xattn_gn_b"), ALU.add))
                    dve.wait_ge(g_ready, 1)
                    dve.tensor_tensor(y_t, y_t, silu_g, ALU.mult).then_inc(yg_ready, 1)
                    dve.wait_ge(out_done, 1)
                    dve.tensor_tensor(x_b, two(J0), x_b, ALU.add).then_inc(x_ready, 1)
                    dve.wait_ge(x_ready, 1)
                    normalise(dve, chain, tile_of(x_tok, b), xc, EPS, own_rstd, var_ready, rstd_ready, 2, xc_normed)
                    dve.wait_ge(xc_ready, 1)
                    dve.tensor_tensor(sx[:, :, :], hT[:, :, 0:S], hT[:, :, 1:S + 1], ALU.subtract).then_inc(sxc_ready, 1)
                    dve.wait_ge(sxc_ready, 1)
                    for n, dst, ready in (("k", xf[0], xk2_ready), ("r", xf[1], xr2_ready)):
                        for k in range(KC):
                            ins = dve.scalar_tensor_tensor(out=dst[:, k, :], in0=sx[:, k, :],
                                                           scalar=col("L1_xattn_fmaa_" + n, k),
                                                           in1=hT[:, k, 1:S + 1], op0=ALU.mult, op1=ALU.add)
                        ins.then_inc(ready, 1)
                    dve.wait_ge(fv_done, 1)
                    dve.wait_ge(rr_ready, 1)
                    chain.link(dve.tensor_tensor(silu_g, two(O0), silu_g, ALU.mult))
                    dve.tensor_tensor(x_b, silu_g, x_b, ALU.add).then_inc(batch_done, 1)
                    dve.wait_ge(batch_done, 1)

                batches(dve, "dve", 1, last_layer == 1, main)

            programs["pe"].append(pe_program)
            programs["act"].append(act_program)
            programs["pool"].append(pool_program)
            programs["dve"].append(dve_program)

        def load_layer1(load, split_k, wait_cleared):
            for n in ("r", "k", "v", "g", "o", "fk", "fr", "fv"):
                load(w["L1_" + n], "L1_" + n, "w1", split_k(d["L1_" + n]))
            load(w1, "L1_w1", "w1", split_k(d["L1_w1"]))
            load(w2_last[0:DMIX, :], "L1_w2", "w1", d["L1_w2"][4 * DMIX:MIX * DMIX, :])
            load(dec1, "L1_dec1", "w1", split_k(d["L1_dec1"]))
            load(dec2[0:DDEC, :], "L1_dec2", "w1")
            load(start_all[:, :, :], "state0", "w1")
            wait_cleared()
            for f in range(4):
                load(w2[f * DMIX:(f + 1) * DMIX, f, :], "L1_w2", "w1", d["L1_w2"][f * DMIX:(f + 1) * DMIX, :])
        def wide_attention(a):
            T = S + 1
            qk_done, v_done, q_ready, k_ready, v_ready = (step(n) for n in
                                                          ("qk_done", "v_done", "q_ready", "k_ready", "v_ready"))
            logits_done, max_ready, exp_ready, probs_ready = (step(n) for n in
                                                              ("logits_done", "max_ready", "exp_ready", "probs_ready"))
            probs_flipped, pt_ready, av_done, av_ready = (step(n) for n in
                                                          ("probs_flipped", "pt_ready", "av_done", "av_ready"))
            last_ready, last_flipped, w17_ready = (step(n) for n in
                                                   ("last_ready", "last_flipped", "w17_ready"))
            out_done, batch_done, dve_chain = step("out_done"), step("batch_done"), step("dve_chain")
            wq, wk, wv, wo = wide[a]
            scale = float(DIM3) ** -0.5
            V_ = [V, OT]
            avT = km0[:, :].rearrange("p (h n) -> p h n", h=HEADS3)
            P_ = [probs[:, i, :].rearrange("p (q n) -> p q n", q=TQ) for i in (0, 1)]
            L_ = [[S0, S1], [O0, O1]]

            def pe_program(pe):
                pe.wait_ge(loaded[f"wide{a}"], 16 * 4)
                pe.wait_ge(dm_ready, 3 * a + 3)
                for h in range(HEADS3):
                    mm = pe.matmul(J0[0:17, 0:C], dm[:, h * 17:(h + 1) * 17], wo[:, h, :],
                                   start=(h == 0), stop=(h == HEADS3 - 1))
                mm.then_inc(v17_done, 1)
                pe.wait_ge(v17_ready, a + 1)

                def main(b, following, b_next):
                    def project_head(h):
                        if h >= 1:
                            pe.wait_ge(q_ready, h)
                            pe.wait_ge(k_ready, h)
                        for o, (wt, src) in enumerate(((wq, hT), (wk, aT))):
                            for k in range(KC):
                                mm = pe.matmul(J0[:, o * S:(o + 1) * S], wt[:, k, h * P:(h + 1) * P], src[:, k, 0:S],
                                               start=(k == 0), stop=(k == KC - 1))
                        mm.then_inc(qk_done, 1)
                        if h % 2 == 0:
                            if h >= 2:
                                pe.wait_ge(v_ready, h // 2)
                            project_tokens(pe, J1, aT, lambda k: wv[:, k, h * P:(h + 2) * P], 2 * P, v_done)

                    def logits(h):
                        pe.wait_ge(q_ready, h + 1)
                        pe.wait_ge(k_ready, h + 1)
                        if h >= 2:
                            pe.wait_ge(exp_ready, h - 1)
                        for qt in range(TQ):
                            mm = pe.matmul(L_[h % 2][qt][:, 0:T], QK[:, h % 2, 0, qt * P:(qt + 1) * P],
                                           QK[:, h % 2, 1, 0:T], start=True, stop=True)
                        mm.then_inc(logits_done, 1)

                    def turn(h):
                        pe.wait_ge(probs_ready, h + 1)
                        if h >= 1:
                            pe.wait_ge(pt_ready, h)
                        for st in range(TQ):
                            for qt in range(TQ):
                                mm = pe.transpose(T0[:, st * S + qt * P:st * S + (qt + 1) * P],
                                                  P_[h % 2][:, qt, st * P:(st + 1) * P], ident[:, :])
                        mm.then_inc(probs_flipped, 1)

                    def weigh(h):
                        pe.wait_ge(pt_ready, h + 1)
                        pe.wait_ge(v_ready, h // 2 + 1)
                        if h >= 1:
                            pe.wait_ge(av_ready, h)
                        for st in range(TQ):
                            mm = pe.matmul(T1[:, 0:S], V_[h // 2 % 2][:, st, h % 2 * P:(h % 2 + 1) * P],
                                           PT[:, h % 2, st * S:(st + 1) * S], start=(st == 0), stop=(st == TQ - 1))
                        mm.then_inc(av_done, 1)

                    project_head(0)
                    project_head(1)
                    logits(0)
                    for h in range(HEADS3):
                        if h + 1 < HEADS3:
                            logits(h + 1)
                        turn(h)
                        if h + 2 < HEADS3:
                            project_head(h + 2)
                        weigh(h)
                    pe.wait_ge(v_ready, HEADS3 // 2)
                    front_pe(following, pe, J1, None)
                    pe.wait_ge(last_ready, HEADS3)
                    pe.wait_ge(pt_ready, HEADS3)
                    for qt in range(TQ):
                        mm = pe.transpose(T0[0:17, qt * P:(qt + 1) * P], weightT[:, qt, :], ident[:, :])
                    mm.then_inc(last_flipped, 1)
                    pe.wait_ge(w17_ready, 1)
                    pe.wait_ge(av_ready, HEADS3)
                    for qt in range(TQ):
                        for h in range(HEADS3):
                            pe.matmul(J0[:, qt * C:(qt + 1) * C], avT[:, h, qt * P:(qt + 1) * P], wo[:, h, :],
                                      start=(h == 0), stop=False)
                        mm = pe.matmul(J0[:, qt * C:(qt + 1) * C], w17[:, qt * P:(qt + 1) * P], v17,
                                       start=False, stop=True)
                    mm.then_inc(out_done, 1)

                batches(pe, "pe", 3 + a, last_layer == 3 + a, main)

            def act_program(act):
                act.wait_ge(v17_done, a + 1)
                act.activation(v17, J0[0:17, 0:C], ACT.Copy).then_inc(v17_ready, 1)

                def main(b, following, b_next):
                    def fetch_k(h):
                        act.wait_ge(qk_done, h + 1)
                        if h >= 2:
                            act.wait_ge(logits_done, h - 1)
                        act.wait_ge(q_ready, h + 1)
                        act.activation(QK[:, h % 2, 1, S:T], head_cols(f"bias_k{a + 1}")[:, h:h + 1], ACT.Copy)
                        act.activation(QK[:, h % 2, 1, 0:S], J0[:, S:2 * S], ACT.Identity,
                                       bias=head_cols(f"bk{a + 1}")[:, h:h + 1]).then_inc(k_ready, 1)

                    def exponents(h):
                        if h >= 2:
                            act.wait_ge(probs_flipped, h - 1)
                            act.wait_ge(last_ready, h - 1)
                        act.wait_ge(max_ready, h + 1)
                        for qt in range(TQ):
                            ins = act.activation(P_[h % 2][:, qt, 0:T], L_[h % 2][qt][:, 0:T], ACT.Exp,
                                                 bias=maxes[:, qt, h:h + 1], accum_out=sums[:, qt, h:h + 1])
                        ins.then_inc(exp_ready, 1)

                    def fetch_turned(h):
                        act.wait_ge(probs_flipped, h + 1)
                        if h >= 2:
                            act.wait_ge(av_done, h - 1)
                        act.activation(PT[:, h % 2, :], T0[:, :], ACT.Copy).then_inc(pt_ready, 1)

                    fetch_k(0)
                    fetch_k(1)
                    exponents(0)
                    for h in range(HEADS3):
                        if h + 1 < HEADS3:
                            exponents(h + 1)
                        fetch_turned(h)
                        if h + 2 < HEADS3:
                            fetch_k(h + 2)
                    act.wait_ge(last_flipped, 1)
                    act.activation(w17, T0[0:17, 0:S], ACT.Copy).then_inc(w17_ready, 1)
                    act.wait_ge(qk_done, HEADS3)
                    front_act(following, act, b_next, J1, None)

                batches(act, "act", 3 + a, last_layer == 3 + a, main)

            def pool_program(pool):
                pool.memset(dm, 0.0).then_inc(dm_ready, 1)
                pool.wait_ge(dm_ready, 3 * a + 1)
                pool.tensor_tensor(dm[:, 0:HEADS3 * 17:18], head_cols(f"bias_v{a + 1}"), head_cols(f"bv{a + 1}"),
                                   ALU.subtract).then_inc(dm_ready, 1)
                pool.tensor_copy(dm.rearrange("p (h n) -> p h n", n=17)[:, :, 16],
                                 head_cols(f"bv{a + 1}")).then_inc(dm_ready, 1)

                def main(b, following, b_next):
                    pool.memset(weightT[:, :, 16:17], 1.0)
                    for h in range(HEADS3):
                        pool.wait_ge(probs_ready, h + 1)
                        pool.tensor_copy(weightT[:, :, h:h + 1], P_[h % 2][:, :, S:T]).then_inc(last_ready, 1)
                        if h == 6:
                            front_pool_first(following, pool, b_next)
                    pool.wait_ge(qk_done, HEADS3)
                    pool.wait_ge(v_done, HEADS3 // 2)
                    front_pool_last(following, pool, b_next)

                batches(pool, "pool", 3 + a, last_layer == 3 + a, main)

            def dve_program(dve):
                dve.wait_ge(v17_ready, a + 1)

                def main(b, following, b_next):
                    chain = Chain(dve, dve_chain)

                    def fetch_qv(h):
                        dve.wait_ge(qk_done, h + 1)
                        if h >= 2:
                            dve.wait_ge(logits_done, h - 1)
                        dve.tensor_scalar(QK[:, h % 2, 0, 0:S], J0[:, 0:S], head_cols(f"bq{a + 1}")[:, h:h + 1],
                                          scale, ALU.add, ALU.mult).then_inc(q_ready, 1)
                        if h % 2 == 0:
                            dve.wait_ge(v_done, h // 2 + 1)
                            if h >= 4:
                                dve.wait_ge(av_done, h - 2)
                            dve.tensor_copy(V_[h // 2 % 2][:, :, :], two(J1)).then_inc(v_ready, 1)

                    def maxima(h):
                        dve.wait_ge(logits_done, h + 1)
                        for qt in range(TQ):
                            ins = dve.tensor_reduce(maxes[:, qt, h:h + 1], L_[h % 2][qt][:, 0:T], AX_X, ALU.max,
                                                    negate=True)
                        ins.then_inc(max_ready, 1)

                    def divide(h):
                        dve.wait_ge(exp_ready, h + 1)
                        chain.link(dve.reciprocal(inv[:, :, h:h + 1], sums[:, :, h:h + 1]))
                        for qt in range(TQ):
                            ins = dve.tensor_scalar(P_[h % 2][:, qt, :], P_[h % 2][:, qt, :], inv[:, qt, h:h + 1],
                                                    None, ALU.mult)
                        ins.then_inc(probs_ready, 1)

                    def fetch_av(h):
                        dve.wait_ge(av_done, h + 1)
                        dve.tensor_copy(avT[:, h, :], T1[:, 0:S]).then_inc(av_ready, 1)

                    fetch_qv(0)
                    fetch_qv(1)
                    maxima(0)
                    divide(0)
                    for h in range(HEADS3):
                        if h + 1 < HEADS3:
                            maxima(h + 1)
                        if h + 2 < HEADS3:
                            fetch_qv(h + 2)
                        if h + 1 < HEADS3:
                            divide(h + 1)
                        fetch_av(h)
                        if h == 5:
                            front_dve(following, dve, chain, b_next)
                    dve.wait_ge(out_done, 1)
                    x_b = x_of(b)
                    bo = row(f"L3_xattn_bo{a + 1}").unsqueeze(1).to_broadcast([P, TQ, C])
                    chain.link(dve.tensor_tensor(xs[:, :, :], two(J0), bo, ALU.add))
                    dve.tensor_tensor(x_b, x_b, xs[:, :, :], ALU.add).then_inc(batch_done, 1)
                    dve.wait_ge(batch_done, 1)

                batches(dve, "dve", 3 + a, last_layer == 3 + a, main)

            programs["pe"].append(pe_program)
            programs["act"].append(act_program)
            programs["pool"].append(pool_program)
            programs["dve"].append(dve_program)

        def mlp():
            fc1_done = step("fc1_done")
            gelu_ready, fc2_done, batch_done = (step(n) for n in ("gelu_ready", "fc2_done", "batch_done"))
            dve_chain = step("dve_chain")
            hidden = km0[:, 0:FF // P * S].rearrange("p (m n) -> p m n", n=S)
            banks = [J0, J1, S0, S1]

            def pe_program(pe):
                pe.wait_ge(loaded["fc"], 16 * 2)

                def main(b, following, b_next):
                    for i, bank_ in enumerate(banks):
                        project(pe, bank_, lambda k, o: fc1[:, k, (2 * i + o) * P:(2 * i + o + 1) * P],
                                hT[:, :, 0:S], 2, fc1_done)
                    front_pe(following, pe, T0, None)
                    for m in range(FF // P):
                        pe.wait_ge(gelu_ready, m + 1)
                        for t, bank_ in enumerate((O0, O1)):
                            mm = pe.matmul(bank_[:, 0:C], hidden[:, m, t * P:(t + 1) * P], fc2[:, m, :],
                                           start=(m == 0), stop=(m == FF // P - 1))
                    mm.then_inc(fc2_done, 1)

                batches(pe, "pe", 5, True, main)

            def act_program(act):
                def main(b, following, b_next):
                    for m in range(FF // P):
                        if m % 2 == 0:
                            act.wait_ge(fc1_done, m // 2 + 1)
                        act.activation(hidden[:, m, :], banks[m // 2][:, m % 2 * S:(m % 2 + 1) * S], ACT.Gelu,
                                       bias=fc1_cols[:, m:m + 1]).then_inc(gelu_ready, 1)
                    front_act(following, act, b_next, T0, None)

                batches(act, "act", 5, True, main)

            def pool_program(pool):
                def main(b, following, b_next):
                    front_pool_first(following, pool, b_next)

                batches(pool, "pool", 5, True, main)

            def dve_program(dve):
                def main(b, following, b_next):
                    chain = Chain(dve, dve_chain)
                    front_dve(following, dve, chain, b_next)
                    b_fc2 = row("L3_xattn_b_fc2").unsqueeze(1).to_broadcast([P, TQ, C])
                    chain.link(dve.tensor_tensor(xs[:, :, :], x_of(b), b_fc2, ALU.add))
                    dve.wait_ge(fc2_done, 1)
                    for t, bank_ in enumerate((O0, O1)):
                        ins = dve.tensor_tensor(tile_of(x_tok, b)(t), bank_[:, 0:C], xs[:, t, :], ALU.add)
                    ins.then_inc(batch_done, 1)
                    dve.wait_ge(batch_done, 1)

                batches(dve, "dve", 5, True, main)

            programs["pe"].append(pe_program)
            programs["act"].append(act_program)
            programs["pool"].append(pool_program)
            programs["dve"].append(dve_program)

        last_layer = LAST_LAYER - 1 if LAST_LAYER < 4 else 5
        small_attention(0)
        if LAST_LAYER > 1:
            rwkv_block()
        if LAST_LAYER > 2:
            small_attention(2)
        if LAST_LAYER > 3:
            wide_attention(0)
            wide_attention(1)
            mlp()

        @block.sync
        def _(sp):
            def load(dst, name, group, src=None):
                sp.dma_start(dst, d[name] if src is None else src).then_inc(loaded[group], 16)

            def split_k(a):
                return a.rearrange("(k p) n -> p k n", p=P)

            load(ident[:, :], "ident", "const")
            load(head8[:, :], "head8", "const")
            load(head16[:, :], "head16", "const")
            load(cols[:, :], "cols", "const")
            load(gate[:, 0:1], "L0_xattn_gate", "const",
                 d["L0_xattn_gate"].rearrange("(o n) -> o n", o=1).to_broadcast([P, 1]))
            load(ctx_tok, "ctx", "ctx", d["ctx"].rearrange("(t p) c -> p t c", p=P))
            load(mask_bytes, "mask0", "ctx", d["mask0"].rearrange("(o n) -> o n", o=1).to_broadcast([P, N]))
            load(x_tok[:, :, :], "x", "x", d["x"].rearrange("(t p) c -> p t c", p=P))
            for n in ("L0_q", "L0_k", "L0_v", "L0_o"):
                load(w[n], n, "w0", split_k(d[n]))
            sp.wait_ge(loaded["w0"], 64)
            load(ctxT[:, :, :], "ctxT", "ctxT", split_k(d["ctxT"]))
            load(rows[:, :, :], "rows", "ctxT",
                 d["rows"].rearrange("(o r) n -> o r n", o=1).to_broadcast([P, len(ROWS), C]))
            if LAST_LAYER > 1:
                load_layer1(load, split_k, lambda: sp.wait_ge(w2_cleared, 1))
            if LAST_LAYER > 2:
                for n in ("L2_q", "L2_k", "L2_v", "L2_o"):
                    load(w[n], n, "w2", split_k(d[n]))
                load(mask2, "mask2", "w2", d["mask2"].rearrange("(t p) s -> p t s", p=P))
            for i in range(len(programs["pe"])):
                lead(sp, B + 1 if i == 0 else B)
                if i % 2 == 0 and i < 3 and LAST_LAYER > 3:
                    a = i // 2
                    for n, dst in zip("qkv", wide[a][:3]):
                        load(dst, f"w{n}{a + 1}", f"wide{a}", split_k(d[f"L3_xattn_w{n}{a + 1}"]))
                    load(wide[a][3], f"wo{a + 1}", f"wide{a}",
                         d[f"L3_xattn_wo{a + 1}"].rearrange("(h p) n -> p h n", p=P))
                if i == 3:
                    load(fc1, "fc1", "fc", split_k(d["L3_xattn_w_fc1"]))
                    load(fc2, "fc2", "fc", d["L3_xattn_w_fc2"].rearrange("(m p) n -> p m n", p=P))
            sp.dma_start(out.rearrange("(t p) c -> p t c", p=P), x_tok[:, :, :]).then_inc(stored, 16)
            sp.wait_ge(stored, 16)

        @block.tensor
        def _(pe):
            for program in programs["pe"]:
                program(pe)

        @block.vector
        def _(dve):
            for program in programs["dve"]:
                program(dve)

        @block.scalar
        def _(act):
            for program in programs["act"]:
                program(act)

        @block.gpsimd
        def _(pool):
            pool.memset(w2, 0.0).then_inc(w2_cleared, 1)
            for program in programs["pool"]:
                program(pool)


def kernel(**inputs):
    import concourse.bacc as bacc
    from concourse.bass_utils import run_bass_kernel_spmd

    a = {k: np.ascontiguousarray(v) for k, v in inputs.items()}

    def t(name):
        return np.ascontiguousarray(a[name].T)

    arrays = {
        "x": a["x"].reshape(N, C),
        "ctx": a["ctx_2048"].reshape(N, C),
        "ctxT": np.ascontiguousarray(a["ctx_2048"].reshape(N, C).T),
        "state0": np.ascontiguousarray(a["ctx_2048"][:, 2:2 + DIM1].reshape(B, KC, P, DIM1)
                                       .transpose(2, 0, 1, 3)).reshape(P, B, KC * DIM1),
        "mask0": a["mask_BxS2_bf1"].reshape(N).view(np.uint8),
        "mask2": a["mask_Bx1xSxS2_ff0"].reshape(N, S),
        "L0_xattn_gate": a["L0_xattn_gate"],
        "ident": np.eye(P, dtype=np.float32),
        "head8": np.repeat(np.eye(P // 8, dtype=np.float32), 8, axis=0),
        "head16": np.repeat(np.eye(P // 16, dtype=np.float32), 16, axis=0),
        "L0_q": t("L0_xattn_Wq"), "L0_k": t("L0_xattn_Wk"), "L0_v": t("L0_xattn_Wv"), "L0_o": t("L0_xattn_Wo"),
        "L1_r": t("L1_xattn_Wr"), "L1_k": t("L1_xattn_Wk"), "L1_v": t("L1_xattn_Wv"), "L1_g": t("L1_xattn_Wg"),
        "L1_o": t("L1_xattn_Wo"), "L1_fk": t("L1_xattn_fWk"), "L1_fr": t("L1_xattn_fWr"),
        "L1_fv": t("L1_xattn_fWv"),
        "L1_w1": a["L1_xattn_maa_w1"], "L1_w2": a["L1_xattn_maa_w2"].reshape(MIX * DMIX, C),
        "L1_dec1": a["L1_xattn_decay_w1"], "L1_dec2": a["L1_xattn_decay_w2"],
        "L2_q": a["L2_xattn_Wq"], "L2_v": a["L2_xattn_Wv"],
        "L2_k": np.repeat(a["L2_xattn_Wk"].reshape(C, KV2, 1, DIM2), HEADS2 // KV2, axis=2).reshape(C, C),
        "L2_o": a["L2_xattn_Wo"],
    }
    for n in ("wq1", "wk1", "wv1", "wo1", "wq2", "wk2", "wv2", "wo2", "w_fc1", "w_fc2"):
        arrays["L3_xattn_" + n] = a["L3_xattn_" + n]
    a["bk_of_q_heads"] = np.repeat(a["L2_xattn_bk"].reshape(KV2, 1, DIM2), HEADS2 // KV2, axis=1)
    arrays["cols"] = np.concatenate(
        [a[n].reshape(KC, P).T for n in COLS] + [a["L3_xattn_" + n].reshape(HEADS3, P).T for n in HEAD_COLS]
        + [a["L3_xattn_b_fc1"].reshape(FF // P, P).T], axis=1)
    arrays["rows"] = np.stack([np.resize(a[n], C) for n in ROWS])
    arrays = {k: np.ascontiguousarray(v) for k, v in arrays.items()}

    nc = bacc.Bacc("TRN2", target_bir_lowering=False, num_devices=1)
    dram = {k: nc.dram_tensor("in_" + k, v.shape, mybir.dt.from_np(v.dtype), kind="ExternalInput").ap()
            for k, v in arrays.items()}
    out = nc.dram_tensor("out", (N, C), F32, kind="ExternalOutput").ap()
    build(nc, dram, out)
    r = run_bass_kernel_spmd(nc, [{"in_" + k: v for k, v in arrays.items()}], core_ids=[0])
    return r.results[0]["out"].reshape(B, S, C)
```

```python
from contextlib import ExitStack

import numpy as np

import concourse.bass as bass
from concourse import mybir

ALU = mybir.AluOpType
ACT = mybir.ActivationFunctionType
AX_X = mybir.AxisListType.X
F32 = mybir.dt.float32
BF16 = mybir.dt.bfloat16
U8 = mybir.dt.uint8

P = 128
B, S, C = 4, 256, 256
N = B * S
TQ = S // P
KC = C // P

HEADS0, DIM0 = 16, 16
HEADS2, DIM2, KV2 = 32, 8, 8
HEADS1, DIM1, MIX, DMIX, DDEC = 32, 8, 5, 32, 64
HEADS3, DIM3, FF = 16, 128, 1024
EPS = 1e-5
EPS2 = 1e-6
BIG = 3.0e38

COLS = ["L0_xattn_ln_gamma", "L0_xattn_ln_beta", "L1_xattn_ln1_w", "L1_xattn_ln1_b", "L1_xattn_ln2_w",
        "L1_xattn_ln2_b", "L1_xattn_maa_x", "L1_xattn_maa_w", "L1_xattn_maa_k", "L1_xattn_maa_v",
        "L1_xattn_maa_r", "L1_xattn_maa_g", "L1_xattn_time_decay", "L1_xattn_faaaa", "L1_xattn_fmaa_k",
        "L1_xattn_fmaa_r", "L2_xattn_bq", "bk_of_q_heads", "L3_xattn_ln1_scale", "L3_xattn_ln1_offset",
        "L3_xattn_ln2_scale", "L3_xattn_ln2_offset", "L3_xattn_ln_mlp_scale", "L3_xattn_ln_mlp_offset"]
HEAD_COLS = ["bq1", "bk1", "bv1", "bias_k1", "bias_v1", "bq2", "bk2", "bv2", "bias_k2", "bias_v2"]
ROWS = ["L1_xattn_gn_w", "L1_xattn_gn_b", "L2_xattn_bo", "L2_xattn_gamma", "L2_xattn_beta",
        "L3_xattn_bo1", "L3_xattn_bo2", "L3_xattn_b_fc2", "L2_xattn_bv"]
N_HEAD_COLS = len(HEAD_COLS) * HEADS3
N_COLS = len(COLS) * KC + N_HEAD_COLS + FF // P


class Chain:

    def __init__(self, eng, sem):
        self.eng, self.sem, self.n = eng, sem, 0

    def link(self, ins):
        self.n += 1
        ins.then_inc(self.sem, 1)
        self.eng.wait_ge(self.sem, self.n)


def build(nc, d, out):
    with ExitStack() as ctx:
        def sb(name, shape, dt=F32):
            return ctx.enter_context(nc.sbuf_tensor(name, shape, dt))

        def bank(name):
            return ctx.enter_context(nc.psum_tensor(name, [P, 512], F32))

        def sem(name):
            return ctx.enter_context(nc.semaphore(name))

        J0, J1, S0, S1, T0, T1, O0, O1 = (bank(n) for n in ("J0", "J1", "S0", "S1", "T0", "T1", "O0", "O1"))

        def two(x):
            return x[:, :].rearrange("p (a n) -> p a n", a=2)

        ident = sb("ident", [P, P])
        head8 = sb("head8", [P, P // DIM1])
        head16 = sb("head16", [P, P // DIM0])
        cols = sb("cols", [P, N_COLS])
        rows = sb("rows", [P, len(ROWS), C])
        x_tok = sb("x_tok", [P, B * TQ, C])
        ctxT = sb("ctxT", [P, KC, N])
        weights_a = sb("weights_a", [P, 4 * 4096])
        early = sb("early", [P, 4 * 4096])
        km0 = sb("km0", [P, 16 * S])

        def col(name, k):
            i = COLS.index(name) * KC + k
            return cols[:, i:i + 1]

        def head_cols(name):
            i = len(COLS) * KC + HEAD_COLS.index(name) * HEADS3
            return cols[:, i:i + HEADS3]

        fc1_cols = cols[:, N_COLS - FF // P:N_COLS]

        def row(name):
            return rows[:, ROWS.index(name), :]

        taken = [0]

        def carve(n, pattern=None, **sizes):
            at = taken[0]
            taken[0] += n
            assert taken[0] <= 4 * 4096
            v = early[:, at:at + n]
            return v.rearrange(pattern, **sizes) if pattern else v

        km1 = carve(16 * S)
        km = [km0[:, :].rearrange("p (h n) -> p h n", h=16), km1.rearrange("p (h n) -> p h n", h=16)]
        w = {}
        WEIGHTS = ["L0_q", "L0_k", "L0_v", "L0_o", "L1_r", "L1_k", "L1_v", "L1_g", "L1_o", "L1_fk", "L1_fr",
                   "L1_fv", "L2_q", "L2_k", "L2_o"]
        for n in WEIGHTS:
            w[n] = carve(KC * C, "p (k n) -> p k n", k=KC)
        w["L2_v"] = carve(KC * KV2 * DIM2, "p (k n) -> p k n", k=KC)
        w1 = carve(KC * MIX * DMIX, "p (k n) -> p k n", k=KC)
        w2 = carve(4 * C, "p (f n) -> p f n", f=4)
        w2_last = carve(C)
        dec1 = carve(KC * DDEC, "p (k n) -> p k n", k=KC)
        dec2 = carve(C)
        mask2 = carve(B * TQ * S, "p (t n) -> p t n", t=B * TQ)

        ctx_tok = weights_a[:, 0:B * TQ * C].rearrange("p (t c) -> p t c", c=C)
        mask0 = weights_a[:, 2048:2048 + N]
        mask_bytes = weights_a[:, 3072:3072 + N // 4].bitcast(U8)

        def wide_weights(region):
            q, k, v, o = (region[:, i * 4096:(i + 1) * 4096] for i in range(4))
            return (q.rearrange("p (k n) -> p k n", k=KC), k.rearrange("p (k n) -> p k n", k=KC),
                    v.rearrange("p (k n) -> p k n", k=KC), o.rearrange("p (h n) -> p h n", h=HEADS3))

        wide = [wide_weights(weights_a[:, :]), wide_weights(early[:, :])]
        fc1 = weights_a[:, 0:KC * FF].rearrange("p (k n) -> p k n", k=KC)
        fc2 = weights_a[:, KC * FF:KC * FF + FF // P * C].rearrange("p (m n) -> p m n", m=FF // P)

        xs = sb("xs", [P, TQ, C])
        xn = sb("xn", [P, TQ, C])
        hT = sb("hT", [P, KC, S + 1])
        aT = sb("aT", [P, KC, S])
        QT = sb("QT", [P, KC, S])
        KT = sb("KT", [P, KC, S])
        V = sb("V", [P, TQ, C])
        masked = sb("masked", [P, 2, 512])
        probs = sb("probs", [P, 2, 514])
        PT = sb("PT", [P, 2, 512])
        On = sb("On", [P, TQ, C])
        OT = sb("OT", [P, KC, S])
        maxes = sb("maxes", [P, TQ, 32])
        sums = sb("sums", [P, TQ, 32])
        inv = sb("inv", [P, TQ, 32])
        stats = sb("stats", [P, TQ, 6])
        moments = sb("moments", [P, TQ, 2])
        rstd = sb("rstd", [P, 2, TQ, 1])
        gate = sb("gate", [P, 2])
        mask_b = sb("mask_b", [P, TQ, S])
        halves = sb("halves", [P, 1])
        QK = sb("QK", [P, 2, 2, 260])
        weightT = On[:, 0, 0:TQ * 17].rearrange("p (t h) -> p t h", t=TQ)
        w17, v17 = QT[0:17, 0, :], KT[0:17, 0, :]
        dm = mask_b[:, :, :].rearrange("p a n -> p (a n)")[:, 0:HEADS3 * 17]
        start_all = sb("start_all", [P, B, KC * DIM1])
        gn = QK[:, :, :, :].rearrange("p a b n -> p (a b n)")[:, 0:TQ * HEADS1 * 3]

        loaded = {n: sem(f"loaded_{n}") for n in
                  ("ident", "const", "x_first", "x", "ctx_first", "ctx",
                   "mask0", "ctxT", "w0", "w1", "w2", "wide0", "wide1", "fc")}
        arrived = sem("arrived")
        go = {n: sem(f"go_{n}") for n in ("pe", "act", "dve", "pool")}
        steps = {}
        v17_done, dm_ready = sem("v17_done"), sem("dm_ready")
        stored = sem("stored")
        halves_ready, mask_ready = sem("halves_ready"), sem("mask_ready")
        w2_cleared, select_ready = sem("w2_cleared"), sem("select_ready")
        neg_ready, gate_ready = sem("neg_ready"), sem("gate_ready")

        block = ctx.enter_context(nc.Block())
        programs = {"pe": [], "dve": [], "act": [], "pool": []}

        def take_stats(dve, chain, src):
            for t in range(TQ):
                ins = dve.bn_stats(stats[:, t, :], src(t))
            chain.link(ins)

        def take_variance(dve, chain, eps, rstd, var_ready):
            for t in range(TQ):
                ins = dve.bn_aggr(moments[:, t, :], stats[:, t, :])
            chain.link(ins)
            dve.tensor_scalar(rstd[:, :, :], moments[:, :, 1:2], eps, None, ALU.add).then_inc(var_ready, 1)

        def measure(dve, chain, src, eps, rstd, var_ready):
            take_stats(dve, chain, src)
            take_variance(dve, chain, eps, rstd, var_ready)

        def centre(dve, src, dst, rstd, rstd_ready, turn, last_sem):
            dve.wait_ge(rstd_ready, turn)
            for t in range(TQ):
                ins = dve.tensor_scalar(dst[:, t, :], src(t), moments[:, t, 0:1], rstd[:, t, :],
                                        ALU.subtract, ALU.mult)
            ins.then_inc(last_sem, 1)

        def take_root(pool, values, var_ready, rstd_ready, turn):
            pool.wait_ge(var_ready, turn)
            pool.tensor_tensor(values, values, halves[:, 0:1].to_broadcast(list(values.shape)), ALU.pow)\
                .then_inc(rstd_ready, 1)

        def step(name):
            if name not in steps:
                steps[name] = sem(name)
            return steps[name]

        def meet(eng, name):
            eng.drain().then_inc(arrived, 1)
            eng.wait_ge(go[name], 1)
            eng.sem_clear(go[name])

        def lead(sp, meetings):
            numbers = sorted(s.num for s in steps.values())
            assert numbers == list(range(numbers[0], numbers[-1] + 1))
            with sp.Fori(0, meetings):
                sp.wait_ge(arrived, len(go))
                sp.sem_clear(range(numbers[0], numbers[-1] + 1))
                sp.sem_clear(arrived)
                for s in go.values():
                    sp.sem_inc(s, 1)

        def flip(pe, bank_, src, done_sem):
            for k in range(KC):
                for t in range(TQ):
                    mm = pe.transpose(bank_[:, k * S + t * P:k * S + (t + 1) * P],
                                      src[:, t, k * P:(k + 1) * P], ident[:, :])
            mm.then_inc(done_sem, 1)

        def project(pe, bank_, weight, moving, n_out, done_sem):
            for o in range(n_out):
                for k in range(KC):
                    mm = pe.matmul(bank_[:, o * S:(o + 1) * S], weight(k, o), moving[:, k, :],
                                   start=(k == 0), stop=(k == KC - 1))
            if done_sem is not None:
                mm.then_inc(done_sem, 1)

        def project_tokens(pe, bank_, src, weight, n, done_sem):
            for t in range(TQ):
                for k in range(KC):
                    mm = pe.matmul(bank_[:, t * S:t * S + n], src[:, k, t * P:(t + 1) * P], weight(k),
                                   start=(k == 0), stop=(k == KC - 1))
            mm.then_inc(done_sem, 1)

        def x_of(b):
            return x_tok[:, bass.ds(b * TQ, TQ), :]

        def tile_of(src, b):
            return lambda t: src[:, bass.ds(b * TQ + t, 1), :].rearrange("p a c -> p (a c)")

        xn_ready, xs_ready = step("xn_ready"), step("xs_ready")
        x_flipped, a_flipped = step("x_flipped"), step("a_flipped")
        hT_ready, aT_ready = step("hT_ready"), step("aT_ready")
        next_var_ready, next_rstd_ready = step("next_var_ready"), step("next_rstd_ready")
        own_rstd, next_rstd = rstd[:, 0], rstd[:, 1]

        def front_dve_stats(layer, dve, chain, b):
            if layer in (0, 1, 3, 4, 5):
                take_stats(dve, chain, tile_of(ctx_tok if layer == 0 else x_tok, b))

        def front_dve_variance(layer, dve, chain):
            if layer in (0, 1, 3, 4, 5):
                take_variance(dve, chain, EPS, next_rstd, next_var_ready)

        def front_dve_first(layer, dve, chain, b):
            front_dve_stats(layer, dve, chain, b)
            front_dve_variance(layer, dve, chain)

        def front_dve_last(layer, dve, b):
            if layer in (0, 1, 3, 4, 5):
                centre(dve, tile_of(ctx_tok if layer == 0 else x_tok, b), xn, next_rstd, next_rstd_ready, 1,
                       xn_ready)

        def front_pool_first(layer, pool, b):
            if layer is None:
                return
            if layer in (0, 2):
                pool.tensor_copy(xs[:, :, :], x_of(b)).then_inc(xs_ready, 1)
            if layer != 2:
                take_root(pool, next_rstd.rearrange("p t o -> p (t o)"), next_var_ready, next_rstd_ready, 1)

        def front_pool_last(layer, pool, b):
            if layer == 0:
                pool.tensor_copy(mask_b[:, 0, :], mask0[:, bass.ds(b * S, S)])
            if layer == 2:
                pool.tensor_copy(mask_b[:, :, :], mask2[:, bass.ds(b * TQ, TQ), :])

        def front_pool_ctx(layer, pool, b):
            if layer in (2, 3, 4):
                pool.tensor_copy(aT[:, :, :], ctxT[:, :, bass.ds(b * S, S)]).then_inc(aT_ready, 1)

        def front_pe(layer, pe, bank_x, bank_a):
            if layer is None:
                return
            if layer in (0, 2):
                pe.wait_ge(xs_ready, 1)
                flip(pe, bank_x, xs, x_flipped)
            if layer == 0:
                pe.wait_ge(xn_ready, 1)
                flip(pe, bank_a, xn, a_flipped)
            if layer not in (0, 2):
                pe.wait_ge(xn_ready, 1)
                flip(pe, bank_x, xn, x_flipped)

        def front_act(layer, act, b, bank_x, bank_a):
            if layer is None:
                return
            if layer == 1:
                act.activation(hT[:, :, 0:1], ctxT[:, :, bass.ds(b * S + 1, 1)], ACT.Copy)
            act.wait_ge(x_flipped, 1)
            if layer in (0, 2):
                act.activation(hT[:, :, 0:S], two(bank_x), ACT.Copy).then_inc(hT_ready, 1)
            else:
                name, offset, scale = {1: ("L1_xattn_ln1", "_b", "_w"), 3: ("L3_xattn_ln1", "_offset", "_scale"),
                                       4: ("L3_xattn_ln2", "_offset", "_scale"),
                                       5: ("L3_xattn_ln_mlp", "_offset", "_scale")}[layer]
                at = 1 if layer == 1 else 0
                for k in range(KC):
                    ins = act.activation(hT[:, k, at:at + S], bank_x[:, k * S:(k + 1) * S], ACT.Identity,
                                         bias=col(name + offset, k), scale=col(name + scale, k))
                ins.then_inc(hT_ready, 1)
            if layer == 0:
                act.wait_ge(a_flipped, 1)
                for k in range(KC):
                    ins = act.activation(aT[:, k, :], bank_a[:, k * S:(k + 1) * S], ACT.Identity,
                                         bias=col("L0_xattn_ln_beta", k), scale=col("L0_xattn_ln_gamma", k))
                ins.then_inc(aT_ready, 1)

        def batches(eng, name, layer, main):
            with eng.Fori(0, B - 1) as b:
                main(b, layer, b + 1)
                meet(eng, name)
            main(B - 1, None if layer == 5 else layer + 1, 0)
            meet(eng, name)

        SMALL = {0: (HEADS0, DIM0, head16), 2: (HEADS2, DIM2, head8)}
        q_done, k_done, v_done = step("q_done"), step("k_done"), step("v_done")
        k_ready, km_ready, scores_done = step("k_ready"), step("km_ready"), step("scores_done")

        def start_pe_keys_queries(layer, pe):
            wq, wk = w[f"L{layer}_q"], w[f"L{layer}_k"]
            pe.wait_ge(hT_ready, 1)
            pe.wait_ge(aT_ready, 1)
            project(pe, J1, lambda k, o: wk[:, k, o * P:(o + 1) * P], aT, KC, k_done)
            project(pe, J0, lambda k, o: wq[:, k, o * P:(o + 1) * P], hT[:, :, 0:S], KC, q_done)

        def start_pe_values(layer, pe):
            pe.wait_ge(k_ready, KC)
            project_tokens(pe, J1, aT, lambda k: w[f"L{layer}_v"][:, k, :], C if layer == 0 else KV2 * DIM2, v_done)

        def start_act_keys(layer, act):
            act.wait_ge(k_done, 1)
            for k in range(KC):
                if layer == 0:
                    ins = act.activation(KT[:, k, :], J1[:, k * S:(k + 1) * S], ACT.Copy)
                else:
                    ins = act.activation(KT[:, k, :], J1[:, k * S:(k + 1) * S], ACT.Identity,
                                         bias=col("bk_of_q_heads", k))
                ins.then_inc(k_ready, 1)

        def start_pool_keys(layer, pool, first, last, in_use, in_this_run=True):
            heads, dim, head_of = SMALL[layer]
            per_tile = P // dim
            for pair in range(first, last):
                half, h = pair * 2 // per_tile, pair * 2 % per_tile
                if in_this_run:
                    pool.wait_ge(k_ready, half + 1)
                if in_use:
                    pool.wait_ge(scores_done, (pair + 1) * TQ)
                for hh in range(2):
                    ins = pool.tensor_scalar(km[half][:, h + hh, :], KT[:, half, :],
                                             head_of[:, h + hh:h + hh + 1], 1.0, ALU.mult, ALU.mult)
                ins.then_inc(km_ready, 1)

        def start_dve_queries(layer, dve):
            scale = float(SMALL[layer][1]) ** -0.5
            dve.wait_ge(q_done, 1)
            for k in range(KC):
                if layer == 0:
                    dve.tensor_scalar(QT[:, k, :], J0[:, k * S:(k + 1) * S], -scale, None, ALU.mult)
                else:
                    dve.tensor_scalar(QT[:, k, :], J0[:, k * S:(k + 1) * S], col("L2_xattn_bq", k),
                                      -scale, ALU.add, ALU.mult)

        def start_dve_values(layer, dve):
            dve.wait_ge(v_done, 1)
            if layer == 0:
                dve.tensor_copy(V[:, :, :], two(J1))
            else:
                n = KV2 * DIM2
                dve.tensor_tensor(V[:, :, 0:n], two(J1)[:, :, 0:n],
                                  row("L2_xattn_bv")[:, 0:n].unsqueeze(1).to_broadcast([P, TQ, n]), ALU.add)

        T = S + 1
        qk_done, q_ready, v_ready = step("qk_done"), step("q_ready"), step("v_ready")
        logits_done = step("logits_done")

        def project_qk(pe, a, g, h):
            wq, wk = wide[a][:2]
            if g >= 1:
                pe.wait_ge(q_ready, g)
                pe.wait_ge(k_ready, g)
            for o, (wt, src) in enumerate(((wq, hT), (wk, aT))):
                for k in range(KC):
                    mm = pe.matmul(J0[:, o * S:(o + 1) * S], wt[:, k, h * P:(h + 1) * P], src[:, k, 0:S],
                                   start=(k == 0), stop=(k == KC - 1))
            mm.then_inc(qk_done, 1)

        def project_values(pe, a, g, h):
            wv = wide[a][2]
            t = h % 2
            if t == 0 and g >= 2:
                pe.wait_ge(v_ready, g // 2)
            for k in range(KC):
                mm = pe.matmul(J1[:, t * S:(t + 1) * S], aT[:, k, t * P:(t + 1) * P],
                               wv[:, k, (h - t) * P:(h - t + 2) * P], start=(k == 0), stop=(k == KC - 1))
            if t == 1:
                mm.then_inc(v_done, 1)

        def project_head(pe, a, g, h):
            project_qk(pe, a, g, h)
            project_values(pe, a, g, h)

        def fetch_k(act, a, g, h):
            act.wait_ge(qk_done, g + 1)
            act.wait_ge(q_ready, g + 1)
            act.activation(QK[:, h % 2, 1, S:T], head_cols(f"bias_k{a + 1}")[:, h:h + 1], ACT.Copy)
            act.activation(QK[:, h % 2, 1, 0:S], J0[:, S:2 * S], ACT.Identity,
                           bias=head_cols(f"bk{a + 1}")[:, h:h + 1]).then_inc(k_ready, 1)

        def fetch_qv(dve, a, g, h):
            scale = float(DIM3) ** -0.5
            dve.wait_ge(qk_done, g + 1)
            dve.tensor_scalar(QK[:, h % 2, 0, 0:S], J0[:, 0:S], head_cols(f"bq{a + 1}")[:, h:h + 1],
                              scale, ALU.add, ALU.mult).then_inc(q_ready, 1)
            if h % 2 == 1:
                dve.wait_ge(v_done, g // 2 + 1)
                dve.tensor_copy((V, OT)[h // 2 % 2][:, :, :], two(J1)).then_inc(v_ready, 1)

        def bias_rows_pool(pool, a):
            pool.memset(dm, 0.0).then_inc(dm_ready, 1)
            pool.wait_ge(dm_ready, 3 * a + 1)
            pool.tensor_tensor(dm[:, 0:HEADS3 * 17:18], head_cols(f"bias_v{a + 1}"), head_cols(f"bv{a + 1}"),
                               ALU.subtract).then_inc(dm_ready, 1)
            pool.tensor_copy(dm.rearrange("p (h n) -> p h n", n=17)[:, :, 16],
                             head_cols(f"bv{a + 1}")).then_inc(dm_ready, 1)

        def bias_rows_pe(pe, a):
            pe.wait_ge(loaded[f"wide{a}"], 16 * 4)
            pe.wait_ge(dm_ready, 3 * a + 3)
            for h in range(HEADS3):
                mm = pe.matmul(S0[0:17, 0:C], dm[:, h * 17:(h + 1) * 17], wide[a][3][:, h, :],
                               start=(h == 0), stop=(h == HEADS3 - 1))
            mm.then_inc(v17_done, 1)

        def bias_rows_act(act, a):
            act.wait_ge(v17_done, a + 1)
            act.activation(v17, S0[0:17, 0:C], ACT.Copy)

        def small_attention(layer):
            heads, dim, _ = SMALL[layer]
            per_tile = P // dim
            pairs = heads // 2
            items = pairs * TQ
            max_ready = step("max_ready")
            probs_ready, probs_flipped = step("probs_ready"), step("probs_flipped")
            pt_ready, av_done = step("pt_ready"), step("av_done")
            on_ready, on_flipped, ot_ready = step("on_ready"), step("on_flipped"), step("ot_ready")
            out_done, x_added = step("out_done"), step("x_added")
            dve_chain = step("dve_chain")
            normed, scaled, pool_step = step("normed"), step("scaled"), step("pool_step")
            var_ready, rstd_ready = step("var_ready"), step("rstd_ready")
            S_, T_ = [S0, S1], [T0, T1]
            O_ = [O0, O1]
            wo = w[f"L{layer}_o"]

            TAIL = 4
            NEXT = 5 if layer == 0 else 11
            FRONT = items // 2
            MOVE = items * 5 // 8

            PAIRS_LEFT = pairs * 3 // 4

            def runs(eng, name, main):
                if layer == 0:
                    first_run[name](eng)
                    meet(eng, name)
                main(0, None, layer, 1)
                meet(eng, name)
                with eng.Fori(1, B - 1) as b:
                    main(b, b - 1, layer, b + 1)
                    meet(eng, name)
                main(B - 1, B - 2, layer + 1, 0)
                meet(eng, name)

            def first_pe(pe):
                front_pe(0, pe, J0, J1)
                start_pe_keys_queries(0, pe)
                start_pe_values(0, pe)

            def first_act(act):
                front_act(0, act, 0, J0, J1)
                start_act_keys(0, act)
                act.wait_ge(loaded["ctxT"], 32)

            def first_pool(pool):
                pool.wait_ge(loaded["x_first"], 16)
                front_pool_first(0, pool, 0)
                pool.wait_ge(loaded["const"], 16 * 4)
                start_pool_keys(0, pool, 0, pairs - PAIRS_LEFT, False)
                pool.wait_ge(mask_ready, 2)
                front_pool_last(0, pool, 0)
                pool.wait_ge(loaded["x"], 16)

            def first_dve(dve):
                front_dve_first(0, dve, Chain(dve, dve_chain), 0)
                front_dve_last(0, dve, 0)
                dve.wait_ge(loaded["mask0"], 16)
                dve.tensor_scalar(mask0, mask_bytes, 1.0, -BIG, ALU.subtract, ALU.mult).then_inc(mask_ready, 1)
                dve.wait_ge(mask_ready, 1)
                dve.tensor_scalar(mask0, mask0, 2.0, None, ALU.mult).then_inc(mask_ready, 1)
                dve.wait_ge(mask_ready, 2)
                start_dve_queries(0, dve)
                start_dve_values(0, dve)
                dve.wait_ge(gate_ready, 1)
                dve.wait_ge(loaded["ctx"], 16)
                dve.wait_ge(loaded["x"], 16)

            first_run = {"pe": first_pe, "act": first_act, "pool": first_pool, "dve": first_dve}

            def pe_program(pe):
                if layer == 0:
                    pe.wait_ge(loaded["ident"], 16)
                    pe.wait_ge(loaded["w0"], 16 * 4)

                def main(b, b_before, following, b_next):
                    def scores(i):
                        pair, qt = i // TQ, i % TQ
                        half, h = pair * 2 // per_tile, pair * 2 % per_tile
                        if layer == 0 and b_before is None and qt == 0 and pair >= pairs - PAIRS_LEFT:
                            pe.wait_ge(km_ready, pair - (pairs - PAIRS_LEFT) + 1)
                        if i >= 2:
                            pe.wait_ge(max_ready, i - 1)
                        pe.matmul(S_[i % 2][:, :], QT[:, half, qt * P:(qt + 1) * P],
                                  km[half][:, h:h + 2, :], start=True, stop=True).then_inc(scores_done, 1)

                    def turn(i):
                        pe.wait_ge(probs_ready, i + 1)
                        if i >= 2:
                            pe.wait_ge(pt_ready, i - 1)
                        for n in range(2 * TQ):
                            mm = pe.transpose(T_[i % 2][:, n * P:(n + 1) * P],
                                              probs[:, i % 2, n * P:(n + 1) * P], ident[:, :])
                        mm.then_inc(probs_flipped, 1)

                    def weigh(i):
                        pair, qt = i // TQ, i % TQ
                        pe.wait_ge(pt_ready, i + 1)
                        for hh in range(2):
                            h = pair * 2 + hh
                            kv = h * dim if layer == 0 else h // (HEADS2 // KV2) * dim
                            for st in range(TQ):
                                mm = pe.matmul(O_[qt][:, h * dim:(h + 1) * dim],
                                               PT[:, i % 2, (hh * TQ + st) * P:(hh * TQ + st + 1) * P],
                                               V[:, st, kv:kv + dim], start=(st == 0), stop=(st == TQ - 1))
                        mm.then_inc(av_done, 1)

                    def project_out(nth):
                        pe.wait_ge(ot_ready, nth)
                        project_tokens(pe, J1, OT, lambda k: wo[:, k, :], C, out_done)

                    scores(0)
                    for i in range(items):
                        if i + 1 < items:
                            scores(i + 1)
                        if i == 0 and b_before is not None:
                            flip(pe, J0, On, on_flipped)
                        if i == items - 1 and following == layer:
                            start_pe_values(layer, pe)
                        turn(i)
                        if i >= 1:
                            weigh(i - 1)
                        if i == TAIL - 2 and b_before is not None:
                            project_out(1)
                        if i == FRONT:
                            if b_before is not None:
                                pe.wait_ge(x_added, 1)
                            front_pe(following, pe, J0, J1)
                        if i == MOVE and following == layer:
                            start_pe_keys_queries(layer, pe)
                    weigh(items - 1)
                    if following != layer:
                        pe.wait_ge(on_ready, 1)
                        pe.wait_ge(hT_ready, 1)
                        flip(pe, J0, On, on_flipped)
                        project_out(2)
                    if following == 3:
                        pe.wait_ge(max_ready, items)
                        bias_rows_pe(pe, 0)
                        pe.wait_ge(hT_ready, 1)
                        pe.wait_ge(aT_ready, 1)
                        pe.wait_ge(x_added, 2)
                        project_head(pe, 0, 0, 0)
                        project_head(pe, 0, 1, 1)

                runs(pe, "pe", main)

            def act_program(act):
                if layer == 0:
                    act.wait_ge(loaded["const"], 16 * 4)
                    act.activation(gate[:, 1:2], gate[:, 0:1], ACT.Tanh).then_inc(gate_ready, 1)

                def main(b, b_before, following, b_next):
                    def fetch_out(nth):
                        act.wait_ge(on_flipped, nth)
                        if nth > 1:
                            act.wait_ge(out_done, nth - 1)
                        act.activation(OT[:, :, :], two(J0), ACT.Copy).then_inc(ot_ready, 1)

                    for i in range(items):
                        pair, qt = i // TQ, i % TQ
                        act.wait_ge(max_ready, i + 1)
                        if i >= 2:
                            act.wait_ge(probs_flipped, i - 1)
                        for hh in range(2):
                            h = pair * 2 + hh
                            ins = act.activation(probs[:, i % 2, hh * S:(hh + 1) * S],
                                                 masked[:, i % 2, hh * S:(hh + 1) * S], ACT.Exp,
                                                 bias=maxes[:, qt, h:h + 1], scale=-1.0,
                                                 accum_out=sums[:, qt, h:h + 1])
                        ins.then_inc(probs_ready, 1)
                        if i == 1 and b_before is not None:
                            fetch_out(1)
                        if i == FRONT + 1:
                            front_act(following, act, b_next, J0, J1)
                        if i == MOVE + 1 and following == layer:
                            if layer == 0 and b_before is None:
                                act.wait_ge(km_ready, PAIRS_LEFT)
                            start_act_keys(layer, act)
                    if following != layer:
                        fetch_out(2)
                    if following == 3:
                        bias_rows_act(act, 0)
                        fetch_k(act, 0, 0, 0)
                        fetch_k(act, 0, 1, 1)

                runs(act, "act", main)

            def pool_program(pool):
                if layer == 0:
                    pool.memset(halves[:, :], -0.5).then_inc(halves_ready, 1)
                    pool.wait_ge(halves_ready, 1)

                def root(nth):
                    if layer == 2:
                        take_root(pool, own_rstd.rearrange("p t o -> p (t o)"), var_ready, rstd_ready, nth)

                def scale_out(b, nth):
                    if layer == 2:
                        gamma = row("L2_xattn_gamma").unsqueeze(1).to_broadcast([P, TQ, C])
                        beta = row("L2_xattn_beta").unsqueeze(1).to_broadcast([P, TQ, C])
                        pool.wait_ge(normed, nth)
                        pool.tensor_tensor(xn[:, :, :], xn[:, :, :], gamma, ALU.mult).then_inc(pool_step, 1)
                        pool.wait_ge(pool_step, nth)
                        pool.tensor_tensor(x_of(b), xn[:, :, :], beta, ALU.add).then_inc(scaled, 1)

                def main(b, b_before, following, b_next):
                    if layer == 0 and b_before is None:
                        start_pool_keys(layer, pool, pairs - PAIRS_LEFT, pairs, False, False)
                    if b_before is not None:
                        root(1)
                        scale_out(b_before, 1)
                    front_pool_first(following, pool, b_next)
                    front_pool_ctx(following, pool, b_next)
                    if following == layer:
                        start_pool_keys(layer, pool, 0, pairs, True)
                        pool.wait_ge(max_ready, items)
                        front_pool_last(following, pool, b_next)
                    else:
                        if following == 3:
                            pool.wait_ge(max_ready, items)
                            bias_rows_pool(pool, 0)
                        root(2)
                        scale_out(b, 2)

                runs(pool, "pool", main)

            def dve_program(dve):
                if layer == 0:
                    dve.wait_ge(loaded["ctx_first"], 16)

                def main(b, b_before, following, b_next):
                    chain = Chain(dve, dve_chain)

                    def add_mask(i):
                        pair, qt = i // TQ, i % TQ
                        dve.wait_ge(scores_done, i + 1)
                        if i >= 2:
                            dve.wait_ge(probs_ready, i - 1)
                        for hh in range(2):
                            h = pair * 2 + hh
                            ins = dve.tensor_tensor_reduce(
                                out=masked[:, i % 2, hh * S:(hh + 1) * S], in0=S_[i % 2][:, hh * S:(hh + 1) * S],
                                in1=mask_b[:, 0 if layer == 0 else qt, :], scale=1.0, scalar=BIG,
                                op0=ALU.add, op1=ALU.min, accum_out=maxes[:, qt, h:h + 1])
                        ins.then_inc(max_ready, 1)

                    def fetch_turned(i):
                        dve.wait_ge(probs_flipped, i + 1)
                        if i >= 2:
                            dve.wait_ge(av_done, i - 1)
                        dve.tensor_copy(PT[:, i % 2, :], T_[i % 2][:, :]).then_inc(pt_ready, 1)

                    def add_out(b, nth):
                        dve.wait_ge(out_done, nth)
                        x_b = x_of(b)
                        if layer == 0:
                            dve.scalar_tensor_tensor(
                                out=x_b.rearrange("p t c -> p (t c)"), in0=J1[:, :], scalar=gate[:, 1:2],
                                in1=x_b.rearrange("p t c -> p (t c)"), op0=ALU.mult, op1=ALU.add)\
                                .then_inc(x_added, 1)
                            return
                        dve.tensor_tensor(xn[:, :, :], two(J1), x_b, ALU.add).then_inc(x_added, 1)
                        dve.wait_ge(x_added, nth)

                    def add_bias():
                        if layer == 2:
                            bo = row("L2_xattn_bo").unsqueeze(1).to_broadcast([P, TQ, C])
                            chain.link(dve.tensor_tensor(xn[:, :, :], xn[:, :, :], bo, ALU.add))

                    def out_stats():
                        if layer == 2:
                            take_stats(dve, chain, lambda t: xn[:, t, :])

                    def out_variance():
                        if layer == 2:
                            take_variance(dve, chain, EPS2, own_rstd, var_ready)

                    def centre_out(nth):
                        if layer == 2:
                            centre(dve, lambda t: xn[:, t, :], xn, own_rstd, rstd_ready, nth, normed)

                    for i in range(items):
                        add_mask(i)
                        if i >= 1:
                            fetch_turned(i - 1)
                        if b_before is not None:
                            if i == TAIL:
                                add_out(b_before, 1)
                            if i == TAIL + 1:
                                add_bias()
                            if i == TAIL + 2:
                                out_stats()
                            if i == TAIL + 3:
                                out_variance()
                            if i == TAIL + 4:
                                centre_out(1)
                        if i == NEXT:
                            front_dve_stats(following, dve, chain, b_next)
                        if i == NEXT + 1:
                            front_dve_variance(following, dve, chain)
                        if i == NEXT + 2:
                            if layer == 2 and following != 2:
                                dve.wait_ge(scaled, 1)
                            front_dve_last(following, dve, b_next)
                    fetch_turned(items - 1)
                    dve.wait_ge(probs_ready, items)
                    chain.link(dve.reciprocal(inv[:, :, 0:heads], sums[:, :, 0:heads]))
                    if following == layer:
                        dve.wait_ge(scores_done, items)
                        start_dve_queries(layer, dve)
                    if b_before is not None:
                        dve.wait_ge(on_flipped, 1)
                    dve.wait_ge(av_done, items)
                    for qt in range(TQ):
                        ins = dve.tensor_tensor(On[:, qt, :].rearrange("p (h d) -> p h d", d=dim),
                                                O_[qt][:, 0:C].rearrange("p (h d) -> p h d", d=dim),
                                                inv[:, qt, 0:heads].unsqueeze(2).to_broadcast([P, heads, dim]),
                                                ALU.mult)
                    ins.then_inc(on_ready, 1)
                    if following == layer:
                        start_dve_values(layer, dve)
                    else:
                        if layer == 2:
                            dve.wait_ge(x_flipped, 1)
                        add_out(b, 2)
                        add_bias()
                        out_stats()
                        out_variance()
                        centre_out(2)
                    if following == 3:
                        fetch_qv(dve, 0, 0, 0)
                        fetch_qv(dve, 0, 1, 1)

                runs(dve, "dve", main)

            programs["pe"].append(pe_program)
            programs["act"].append(act_program)
            programs["pool"].append(pool_program)
            programs["dve"].append(dve_program)

        def rwkv_block():
            sx_ready = step("sx_ready")
            xxx_ready, lora_done, lora_ready = step("xxx_ready"), step("lora_done"), step("lora_ready")
            mix_done, mix_ready, xf_ready = step("mix_done"), step("mix_ready"), step("xf_ready")
            dec1_done, dec1_ready, dec2_done = step("dec1_done"), step("dec1_ready"), step("dec2_done")
            exp_ready, decay_ready = step("exp_ready"), step("decay_ready")
            k_done, v_done, r_done, g_done = (step(f"rwkv_{n}_done") for n in "kvrg")
            k_ready, v_ready, r_ready, g_ready = (step(f"rwkv_{n}_ready") for n in "kvrg")
            spread_done, kv_ready, start_ready = step("spread_done"), step("kv_ready"), step("start_ready")
            start_here, split, rest_ready = step("start_here"), step("split"), step("rest_ready")
            vT_done, v_parts_ready = step("vT_done"), step("v_parts_ready")
            state_ready, read_ready, y_done = step("state_ready"), step("read_ready"), step("y_done")
            ruk_ready, bonus_done, bonus_ready = step("ruk_ready"), step("bonus_done"), step("bonus_ready")
            bonus_times_v = step("bonus_times_v")
            yg_ready, yg_flipped, ygT_ready = step("yg_ready"), step("yg_flipped"), step("ygT_ready")
            out_done, x_ready = step("out_done"), step("x_ready")
            xc_flipped, xc_ready, sxc_ready = step("xc_flipped"), step("xc_ready"), step("sxc_ready")
            xk2_ready, xr2_ready = step("xk2_ready"), step("xr2_ready")
            fk_done, fr_done, relu_ready = step("fk_done"), step("fr_done"), step("relu_ready")
            kk_ready, rr_ready, fv_done = step("kk_ready"), step("rr_ready"), step("fv_done")
            fv_read, tail_step, tail_done = step("fv_read"), step("tail_step"), step("tail_done")
            gvar_ready, groot_ready = step("gvar_ready"), step("groot_ready")
            var_ready, rstd_ready, xc_normed = step("var_ready"), step("rstd_ready"), step("xc_normed")
            dve_chain = step("dve_chain")

            xv_ready, xg_ready, gates_ready = step("xv_ready"), step("xg_ready"), step("gates_ready")
            ORDER = [2, 0, 1, 3, 4]

            def scratch(half, at, n=KC * S):
                return [km0[:, :], km1][half][:, at:at + n]

            def pair(v):
                return v.rearrange("p (a n) -> p a n", a=2)

            xf = [pair(scratch(0, i * 512)) for i in range(MIX)]
            rT, kT, wT = (pair(scratch(0, 512 * i)) for i in (5, 6, 7))
            kv = [pair(scratch(1, 512 * i)) for i in (0, 1)]
            read = [pair(scratch(1, 512 * i)) for i in (2, 3)]
            state = [scratch(1, 2048 + 514 * i, 514).rearrange("p (a n) -> p a n", a=2) for i in (0, 1)]
            silu_g = scratch(1, 3076).rearrange("p (t c) -> p t c", t=TQ)

            def late(i, n=KC * S):
                return weights_a[:, i * 520:i * 520 + n]

            xcT = pair(late(0, KC * (S + 1)))
            sxc, xk2, xr2, relu, kk, rr, ygT = (pair(late(i)) for i in range(1, 8))
            xc = late(8).rearrange("p (t c) -> p t c", t=TQ)
            start = scratch(1, 3588, KC * DIM1).rearrange("p (a j) -> p a j", a=2)
            sx, xxx = QT, KT
            mixed = [masked[:, i, :].rearrange("p (a n) -> p a n", a=2) for i in (0, 1)]
            lora = PT[:, 0, 0:S]
            lora_last = PT[0:DMIX, 0, S:2 * S]
            decay_in = PT[0:DDEC, 1, 0:S]
            ruk = pair(PT[:, 1, :])
            v_tok = V
            yv = probs[:, 0, 0:512]
            tmp = probs[:, 1, 0:512]
            yv3, tmp3 = (v.rearrange("p (h j) -> p h j", j=DIM1) for v in (yv, tmp))
            bonus = gn[:, 0:TQ * HEADS1]
            mean, var = gn[:, 0:TQ * HEADS1], gn[:, TQ * HEADS1:2 * TQ * HEADS1]
            root = gn[:, 2 * TQ * HEADS1:3 * TQ * HEADS1]
            mix_banks = [S0, S1, T1, O0, O1]
            gated_w, gated_b = xf[4], xf[0]
            spread_banks = [T0, J1]
            heads_tile = P // DIM1

            select = mask_b[:, :, :].rearrange("p t n -> p (t n)").bitcast(BF16)
            rest = aT[:, :, :].rearrange("p k n -> p (k n)")
            halves_of_on = On[:, :, :].rearrange("p t n -> p (t n)").bitcast(BF16)
            v_parts = [halves_of_on[:, 0:512], halves_of_on[:, 512:1024],
                       OT[:, :, :].rearrange("p k n -> p (k n)").bitcast(BF16)[:, 0:512]]

            def runs(eng, name, main):
                main(0, None, 1, 1)
                meet(eng, name)
                with eng.Fori(1, B - 1) as b:
                    main(b, b - 1, 1, b + 1)
                    meet(eng, name)
                main(B - 1, B - 2, 2, 0)
                meet(eng, name)

            def pe_program(pe):
                pe.wait_ge(loaded["w1"], 16 * 17)

                def flip_out():
                    flip(pe, T0, yv.rearrange("p (t c) -> p t c", t=TQ), yg_flipped)

                def project_out(turn):
                    pe.wait_ge(ygT_ready, turn)
                    project_tokens(pe, T0, ygT, lambda k: w["L1_o"][:, k, :], C, out_done)

                def flip_xc(turn):
                    pe.wait_ge(xc_normed, turn)
                    flip(pe, T0, xc, xc_flipped)

                def project_fk(turn):
                    pe.wait_ge(xk2_ready, turn)
                    pe.wait_ge(r_ready, 1)
                    if turn > 1:
                        pe.wait_ge(fv_read, turn - 1)
                    project(pe, T1, lambda k, o: w["L1_fk"][:, k, o * P:(o + 1) * P], xk2, KC, fk_done)

                def project_fr(turn):
                    pe.wait_ge(xr2_ready, turn)
                    pe.wait_ge(g_ready, 1)
                    if turn > 1:
                        pe.wait_ge(rr_ready, turn - 1)
                    project_tokens(pe, O0, xr2, lambda k: w["L1_fr"][:, k, :], C, fr_done)

                def project_fv(turn):
                    pe.wait_ge(kk_ready, turn)
                    project_tokens(pe, T1, kk, lambda k: w["L1_fv"][:, k, :], C, fv_done)

                def main(b, b_before, following, b_next):
                    if b_before is not None:
                        flip_out()
                    pe.wait_ge(xxx_ready, 1)
                    for k in range(KC):
                        pe.matmul(J0[:, 0:S], w1[:, k, 0:P], xxx[:, k, :], start=(k == 0), stop=(k == KC - 1))
                    for k in range(KC):
                        mm = pe.matmul(J0[0:DMIX, S:2 * S], w1[:, k, P:P + DMIX], xxx[:, k, :],
                                       start=(k == 0), stop=(k == KC - 1))
                    mm.then_inc(lora_done, 1)
                    if b_before is not None:
                        project_out(1)
                    pe.wait_ge(lora_ready, 1)
                    for f in ORDER:
                        for o in range(KC):
                            if f < 4:
                                mm = pe.matmul(mix_banks[f][:, o * S:(o + 1) * S], w2[:, f, o * P:(o + 1) * P], lora,
                                               start=True, stop=True)
                            else:
                                mm = pe.matmul(mix_banks[f][:, o * S:(o + 1) * S],
                                               w2_last[0:DMIX, o * P:(o + 1) * P], lora_last, start=True, stop=True)
                        mm.then_inc(mix_done, 1)
                    def spread(j):
                        if j >= 2:
                            pe.wait_ge(kv_ready, j - 1)
                        for n, part in enumerate(v_parts):
                            mm = pe.matmul(spread_banks[j % 2][:, :], select[:, j * P:(j + 1) * P], part,
                                           start=(n == 0), stop=(n == len(v_parts) - 1))
                        mm.then_inc(spread_done, 1)

                    pe.wait_ge(xv_ready, 1)
                    project(pe, J1, lambda k, o: w["L1_v"][:, k, o * P:(o + 1) * P], xf[2], KC, vT_done)
                    if b_before is not None:
                        flip_xc(1)
                    pe.wait_ge(xf_ready, 1)
                    for k in range(KC):
                        mm = pe.matmul(J0[0:DDEC, 0:S], dec1[:, k, :], xf[0][:, k, :], start=(k == 0), stop=(k == KC - 1))
                    mm.then_inc(dec1_done, 1)
                    pe.wait_ge(xf_ready, 2)
                    project(pe, S0, lambda k, o: w["L1_k"][:, k, o * P:(o + 1) * P], xf[1], KC, k_done)
                    pe.wait_ge(dec1_ready, 1)
                    for o in range(KC):
                        mm = pe.matmul(J0[:, o * S:(o + 1) * S], dec2[0:DDEC, o * P:(o + 1) * P], decay_in,
                                       start=True, stop=True)
                    mm.then_inc(dec2_done, 1)
                    pe.wait_ge(xf_ready, 3)
                    project(pe, T1, lambda k, o: w["L1_r"][:, k, o * P:(o + 1) * P], xf[3], KC, r_done)
                    if b_before is None:
                        pe.wait_ge(select_ready, 1)
                    pe.wait_ge(v_parts_ready, 1)
                    spread(0)
                    spread(1)
                    project_tokens(pe, S1, xf[2], lambda k: w["L1_v"][:, k, :], C, v_done)
                    pe.wait_ge(xg_ready, 1)
                    project_tokens(pe, O0, xf[4], lambda k: w["L1_g"][:, k, :], C, g_done)

                    def gather(j):
                        pe.wait_ge(read_ready, j + 1)
                        for t in range(TQ):
                            for half in range(KC):
                                at = t * C + half * P
                                y = O1[:, at:at + P].rearrange("p (h j) -> p h j", j=DIM1)[:, :, j]
                                mm = pe.matmul(y, read[j % 2][:, half, t * P:(t + 1) * P], head8[:, :],
                                               start=True, stop=True)
                        mm.then_inc(y_done, 1)

                    for j in range(DIM1):
                        if j + 2 < DIM1:
                            spread(j + 2)
                        if j == 1:
                            pe.wait_ge(ruk_ready, 1)
                            pe.wait_ge(k_ready, 1)
                            for t in range(TQ):
                                for half in range(KC):
                                    at = t * HEADS1 + half * heads_tile
                                    mm = pe.matmul(S0[:, at:at + heads_tile], ruk[:, half, t * P:(t + 1) * P],
                                                   head8[:, :], start=True, stop=True)
                            mm.then_inc(bonus_done, 1)
                        gather(j)
                        if b_before is not None:
                            if j == 0:
                                project_fk(1)
                            if j == 2:
                                project_fr(1)
                            if j == 4:
                                project_fv(1)
                        if j == 5:
                            pe.wait_ge(v_ready, 1)
                            front_pe(following, pe, S1, None)
                    if following == 2:
                        pe.wait_ge(loaded["w2"], 16 * 5)
                        start_pe_keys_queries(2, pe)
                        start_pe_values(2, pe)
                        pe.wait_ge(yg_ready, 1)
                        flip_out()
                        project_out(2)
                        flip_xc(2)
                        project_fk(2)
                        project_fr(2)
                        project_fv(2)

                runs(pe, "pe", main)

            def act_program(act):
                def fetch_out(turn):
                    act.wait_ge(yg_flipped, turn)
                    act.activation(ygT, two(T0), ACT.Copy).then_inc(ygT_ready, 1)

                def fetch_xc(b, turn):
                    if turn > 1:
                        act.wait_ge(xr2_ready, turn - 1)
                    act.activation(xcT[:, :, 0:1], ctxT[:, :, bass.ds(b * S, 1)], ACT.Copy)
                    act.wait_ge(xc_flipped, turn)
                    for k in range(KC):
                        ins = act.activation(xcT[:, k, 1:S + 1], T0[:, k * S:(k + 1) * S], ACT.Identity,
                                             bias=col("L1_xattn_ln2_b", k), scale=col("L1_xattn_ln2_w", k))
                    ins.then_inc(xc_ready, 1)

                def square_relu(turn):
                    act.wait_ge(fk_done, turn)
                    if turn > 1:
                        act.wait_ge(tail_done, turn - 1)
                    act.activation(relu, two(T1), ACT.Relu).then_inc(relu_ready, 1)
                    act.wait_ge(relu_ready, turn)
                    act.activation(kk, relu, ACT.Square).then_inc(kk_ready, 1)

                def sigmoid_r(turn):
                    act.wait_ge(fr_done, turn)
                    if turn > 1:
                        act.wait_ge(tail_done, turn - 1)
                    act.activation(rr, two(O0), ACT.Sigmoid).then_inc(rr_ready, 1)

                def fetch_fv(turn):
                    act.wait_ge(fv_done, turn)
                    act.wait_ge(kk_ready, turn)
                    act.activation(relu, two(T1), ACT.Copy).then_inc(fv_read, 1)

                def main(b, b_before, following, b_next):
                    if b_before is not None:
                        fetch_out(1)
                    act.wait_ge(lora_done, 1)
                    act.activation(lora, J0[:, 0:S], ACT.Tanh)
                    act.activation(lora_last, J0[0:DMIX, S:2 * S], ACT.Tanh).then_inc(lora_ready, 1)
                    act.wait_ge(vT_done, 1)
                    act.activation(v_parts[0], J1[:, :], ACT.Copy).then_inc(split, 1)
                    act.wait_ge(dec1_done, 1)
                    act.activation(decay_in, J0[0:DDEC, 0:S], ACT.Tanh).then_inc(dec1_ready, 1)
                    act.wait_ge(rest_ready, 1)
                    act.activation(v_parts[1], rest, ACT.Copy).then_inc(split, 1)
                    if b_before is not None:
                        fetch_xc(b_before, 1)
                    act.wait_ge(k_done, 1)
                    act.activation(kT, two(S0), ACT.Copy).then_inc(k_ready, 1)
                    act.wait_ge(rest_ready, 2)
                    act.activation(v_parts[2], rest, ACT.Copy).then_inc(v_parts_ready, 1)
                    act.wait_ge(dec2_done, 1)
                    for k in range(KC):
                        ins = act.activation(wT[:, k, :], J0[:, k * S:(k + 1) * S], ACT.Exp,
                                             bias=col("L1_xattn_time_decay", k))
                    ins.then_inc(exp_ready, 1)
                    act.wait_ge(exp_ready, 1)
                    act.activation(wT, wT, ACT.Exp, scale=-1.0).then_inc(decay_ready, 1)
                    act.wait_ge(r_done, 1)
                    act.activation(rT, two(T1), ACT.Copy).then_inc(r_ready, 1)
                    act.wait_ge(start_here, 1)

                    def first_state(j):
                        if j >= 2:
                            act.wait_ge(read_ready, j - 1)
                        act.activation(state[j % 2][:, :, 0:1], start[:, :, j:j + 1], ACT.Copy)\
                            .then_inc(start_ready, 1)

                    first_state(0)
                    first_state(1)
                    act.wait_ge(v_done, 1)
                    act.activation(v_tok[:, :, :], two(S1), ACT.Copy).then_inc(v_ready, 1)
                    first_state(2)
                    act.wait_ge(g_done, 1)
                    act.activation(silu_g, two(O0), ACT.Silu).then_inc(g_ready, 1)
                    for j in range(3, DIM1):
                        first_state(j)
                        if j == 3:
                            act.wait_ge(bonus_done, 1)
                            act.activation(bonus, S0[:, 0:TQ * HEADS1], ACT.Copy).then_inc(bonus_ready, 1)
                        if b_before is not None:
                            if j == 3:
                                square_relu(1)
                            if j == 4:
                                sigmoid_r(1)
                            if j == 6:
                                fetch_fv(1)
                    act.wait_ge(xf_ready, 3)
                    act.wait_ge(xg_ready, 1)
                    front_act(following, act, b_next, S1, None)
                    if following == 2:
                        act.wait_ge(lora_done, 1)
                        start_act_keys(2, act)
                    act.wait_ge(gvar_ready, 1)
                    act.activation(root, var, ACT.Sqrt).then_inc(groot_ready, 1)
                    if following == 2:
                        fetch_out(2)
                        fetch_xc(b, 2)
                        square_relu(2)
                        sigmoid_r(2)
                        fetch_fv(2)

                runs(act, "act", main)

            def pool_program(pool):
                pool.wait_ge(loaded["w1"], 16 * 17)
                pool.wait_ge(loaded["ctxT"], 32)
                for j in range(DIM1):
                    ins = pool.tensor_copy(
                        select[:, j * P:(j + 1) * P].rearrange("p (h i) -> p h i", i=DIM1),
                        ident[:, j:P:DIM1].unsqueeze(2).to_broadcast([P, heads_tile, DIM1]))
                ins.then_inc(select_ready, 1)

                def root_of_tail(turn):
                    take_root(pool, own_rstd.rearrange("p t o -> p (t o)"), var_ready, rstd_ready, turn)

                def finish_tail(b, turn):
                    pool.wait_ge(rr_ready, turn)
                    pool.wait_ge(fv_read, turn)
                    pool.tensor_tensor(relu, relu, rr, ALU.mult).then_inc(tail_step, 1)
                    pool.wait_ge(tail_step, turn)
                    pool.tensor_tensor(x_of(b), x_of(b), relu, ALU.add).then_inc(tail_done, 1)

                def main(b, b_before, following, b_next):
                    pool.tensor_copy(start.rearrange("p a j -> p (a j)"),
                                     start_all[:, bass.ds(b, 1), :].rearrange("p o n -> p (o n)"))\
                        .then_inc(start_here, 1)
                    front_pool_first(following, pool, b_next)
                    if b_before is not None:
                        root_of_tail(1)
                    for n, f in enumerate(ORDER[1:4]):
                        pool.wait_ge(mix_ready, n + 1)
                        pool.tensor_tensor(xf[f], mixed[(n + 1) % 2], hT[:, :, 1:S + 1], ALU.add)\
                            .then_inc(xf_ready, 1)
                    pool.wait_ge(g_ready, 1)
                    pool.tensor_tensor(gated_w, silu_g, row("L1_xattn_gn_w").unsqueeze(1).to_broadcast([P, TQ, C]),
                                       ALU.mult)
                    pool.tensor_tensor(gated_b, silu_g, row("L1_xattn_gn_b").unsqueeze(1).to_broadcast([P, TQ, C]),
                                       ALU.mult).then_inc(gates_ready, 1)
                    pool.wait_ge(v_ready, 1)
                    pool.wait_ge(bonus_ready, 1)
                    pool.tensor_tensor(tmp3, v_tok[:, :, :].rearrange("p t (h j) -> p (t h) j", j=DIM1),
                                       bonus.unsqueeze(2).to_broadcast([P, TQ * HEADS1, DIM1]), ALU.mult)\
                        .then_inc(bonus_times_v, 1)
                    if b_before is not None:
                        finish_tail(b_before, 1)
                    if following == 2:
                        pool.wait_ge(loaded["w2"], 16 * 5)
                        pool.tensor_scalar(mask2[:, :, :], mask2[:, :, :], -1.0, 0.0, ALU.mult, ALU.add)\
                            .then_inc(neg_ready, 1)
                        pool.wait_ge(neg_ready, 1)
                        pool.wait_ge(spread_done, DIM1)
                    front_pool_last(following, pool, b_next)
                    front_pool_ctx(following, pool, b_next)
                    if following == 2:
                        pool.wait_ge(yg_ready, 1)
                        start_pool_keys(2, pool, 0, HEADS2 // 8, False)
                        root_of_tail(2)
                        start_pool_keys(2, pool, HEADS2 // 8, HEADS2 // 2, False)
                        finish_tail(b, 2)

                runs(pool, "pool", main)

            def dve_program(dve):
                dve.wait_ge(loaded["ctxT"], 32)

                def main(b, b_before, following, b_next):
                    chain = Chain(dve, dve_chain)

                    def add_out(b, turn):
                        dve.wait_ge(out_done, turn)
                        dve.tensor_tensor(x_of(b), two(T0), x_of(b), ALU.add).then_inc(x_ready, 1)
                        dve.wait_ge(x_ready, turn)
                        measure(dve, chain, tile_of(x_tok, b), EPS, own_rstd, var_ready)

                    def normalise_xc(b, turn):
                        if turn > 1:
                            dve.wait_ge(xc_flipped, turn - 1)
                        centre(dve, tile_of(x_tok, b), xc, own_rstd, rstd_ready, turn, xc_normed)

                    def mix_channels(turn):
                        dve.wait_ge(xc_ready, turn)
                        if turn > 1:
                            dve.wait_ge(fr_done, turn - 1)
                        dve.tensor_tensor(sxc, xcT[:, :, 0:S], xcT[:, :, 1:S + 1], ALU.subtract)\
                            .then_inc(sxc_ready, 1)
                        dve.wait_ge(sxc_ready, turn)
                        for n, dst, ready in (("k", xk2, xk2_ready), ("r", xr2, xr2_ready)):
                            for k in range(KC):
                                ins = dve.scalar_tensor_tensor(out=dst[:, k, :], in0=sxc[:, k, :],
                                                               scalar=col("L1_xattn_fmaa_" + n, k),
                                                               in1=xcT[:, k, 1:S + 1], op0=ALU.mult, op1=ALU.add)
                            ins.then_inc(ready, 1)

                    dve.tensor_tensor(sx[:, :, :], hT[:, :, 0:S], hT[:, :, 1:S + 1], ALU.subtract).then_inc(sx_ready, 1)
                    dve.wait_ge(sx_ready, 1)
                    for k in range(KC):
                        ins = dve.scalar_tensor_tensor(out=xxx[:, k, :], in0=sx[:, k, :], scalar=col("L1_xattn_maa_x", k),
                                                       in1=hT[:, k, 1:S + 1], op0=ALU.mult, op1=ALU.add)
                    ins.then_inc(xxx_ready, 1)
                    front_dve_first(following, dve, chain, b_next)
                    front_dve_last(following, dve, b_next)
                    if b_before is not None:
                        add_out(b_before, 1)

                    def mix(n, f):
                        dve.wait_ge(mix_done, n + 1)
                        if n == 2:
                            dve.wait_ge(xv_ready, 1)
                        if n >= 3:
                            dve.wait_ge(xf_ready, n - 2)
                        for k in range(KC):
                            ins = dve.scalar_tensor_tensor(out=mixed[n % 2][:, k, :],
                                                           in0=mix_banks[f][:, k * S:(k + 1) * S],
                                                           scalar=col("L1_xattn_maa_" + "wkvrg"[f], k),
                                                           in1=sx[:, k, :], op0=ALU.add, op1=ALU.mult)
                        if n in (1, 2, 3):
                            ins.then_inc(mix_ready, 1)
                        else:
                            chain.link(ins)
                            dve.tensor_tensor(xf[f], mixed[n % 2], hT[:, :, 1:S + 1], ALU.add)\
                                .then_inc(xv_ready if n == 0 else xg_ready, 1)

                    mix(0, ORDER[0])
                    mix(1, ORDER[1])
                    if b_before is not None:
                        normalise_xc(b_before, 1)
                    mix(2, ORDER[2])
                    dve.wait_ge(split, 1)
                    dve.tensor_tensor(rest, J1[:, :], v_parts[0], ALU.subtract).then_inc(rest_ready, 1)
                    mix(3, ORDER[3])
                    dve.wait_ge(split, 2)
                    dve.tensor_tensor(rest, rest, v_parts[1], ALU.subtract).then_inc(rest_ready, 1)
                    mix(4, ORDER[4])
                    if b_before is not None:
                        mix_channels(1)

                    def times_k(j):
                        dve.wait_ge(spread_done, j + 1)
                        if j >= 2:
                            dve.wait_ge(state_ready, j - 1)
                        dve.tensor_tensor(kv[j % 2], kT, two(spread_banks[j % 2]), ALU.mult).then_inc(kv_ready, 1)

                    dve.wait_ge(k_ready, 1)
                    times_k(0)
                    dve.wait_ge(r_ready, 1)
                    dve.wait_ge(decay_ready, 1)
                    for k in range(KC):
                        ins = dve.scalar_tensor_tensor(out=ruk[:, k, :], in0=rT[:, k, :], scalar=col("L1_xattn_faaaa", k),
                                                       in1=kT[:, k, :], op0=ALU.mult, op1=ALU.mult)
                    ins.then_inc(ruk_ready, 1)
                    for j in range(DIM1):
                        dve.wait_ge(kv_ready, j + 1)
                        dve.wait_ge(start_ready, j + 1)
                        if j >= 2:
                            dve.wait_ge(read_ready, j - 1)
                        for half in range(KC):
                            ins = dve.tensor_tensor_scan(state[j % 2][:, half, 1:S + 1], wT[:, half, :],
                                                         kv[j % 2][:, half, :], start[:, half, j:j + 1],
                                                         ALU.mult, ALU.add)
                        ins.then_inc(state_ready, 1)
                        if j + 1 < DIM1:
                            times_k(j + 1)
                        dve.wait_ge(state_ready, j + 1)
                        if j >= 2:
                            dve.wait_ge(y_done, j - 1)
                        dve.tensor_tensor(read[j % 2], rT, state[j % 2][:, :, 0:S], ALU.mult).then_inc(read_ready, 1)
                    dve.wait_ge(bonus_times_v, 1)
                    dve.wait_ge(y_done, DIM1)
                    chain.link(dve.tensor_tensor(yv, O1[:, :], tmp, ALU.add))
                    chain.link(dve.tensor_reduce(mean, yv3, AX_X, ALU.add))
                    wide_mean = mean.unsqueeze(2).to_broadcast([P, TQ * HEADS1, DIM1])
                    chain.link(dve.scalar_tensor_tensor(out=yv3, in0=wide_mean, scalar=-1.0 / DIM1, in1=yv3,
                                                        op0=ALU.mult, op1=ALU.add))
                    chain.link(dve.tensor_tensor(tmp, yv, yv, ALU.mult))
                    chain.link(dve.tensor_reduce(var, tmp3, AX_X, ALU.add))
                    dve.tensor_scalar(var, var, 1.0 / DIM1, EPS, ALU.mult, ALU.add).then_inc(gvar_ready, 1)
                    dve.wait_ge(groot_ready, 1)
                    chain.link(dve.reciprocal(root, root))
                    chain.link(dve.tensor_tensor(mean, root, root, ALU.mult))
                    chain.link(dve.tensor_tensor(mean, mean, var, ALU.mult))
                    chain.link(dve.tensor_scalar(mean, mean, -0.5, 1.5, ALU.mult, ALU.add))
                    chain.link(dve.tensor_tensor(root, root, mean, ALU.mult))
                    wide_rstd = root.unsqueeze(2).to_broadcast([P, TQ * HEADS1, DIM1])
                    chain.link(dve.tensor_tensor(yv3, yv3, wide_rstd, ALU.mult))
                    y_t = yv.rearrange("p (t c) -> p t c", t=TQ)
                    dve.wait_ge(gates_ready, 1)
                    chain.link(dve.tensor_tensor(y_t, y_t, gated_w, ALU.mult))
                    dve.tensor_tensor(y_t, y_t, gated_b, ALU.add).then_inc(yg_ready, 1)
                    if following == 2:
                        dve.wait_ge(xg_ready, 1)
                        start_dve_queries(2, dve)
                        start_dve_values(2, dve)
                        add_out(b, 2)
                        normalise_xc(b, 2)
                        mix_channels(2)

                runs(dve, "dve", main)

            programs["pe"].append(pe_program)
            programs["act"].append(act_program)
            programs["pool"].append(pool_program)
            programs["dve"].append(dve_program)

        def load_layer1(load, split_k, wait_cleared):
            for n in ("r", "k", "v", "g", "o", "fk", "fr", "fv"):
                load(w["L1_" + n], "L1_" + n, "w1", split_k(d["L1_" + n]))
            load(w1, "L1_w1", "w1", split_k(d["L1_w1"]))
            load(w2_last[0:DMIX, :], "L1_w2", "w1", d["L1_w2"][4 * DMIX:MIX * DMIX, :])
            load(dec1, "L1_dec1", "w1", split_k(d["L1_dec1"]))
            load(dec2[0:DDEC, :], "L1_dec2", "w1")
            load(start_all[:, :, :], "state0", "w1")
            wait_cleared()
            for f in range(4):
                load(w2[f * DMIX:(f + 1) * DMIX, f, :], "L1_w2", "w1", d["L1_w2"][f * DMIX:(f + 1) * DMIX, :])
        def wide_attention(a):
            max_ready, exp_ready, probs_ready = step("max_ready"), step("exp_ready"), step("probs_ready")
            probs_flipped, pt_ready, av_done, av_ready = (step(n) for n in
                                                          ("probs_flipped", "pt_ready", "av_done", "av_ready"))
            last_ready, last_flipped, w17_ready = (step(n) for n in
                                                   ("last_ready", "last_flipped", "w17_ready"))
            out_done, dve_chain = step("out_done"), step("dve_chain")
            wo = wide[a][3]
            V_ = [V, OT]
            avT = km0[:, :].rearrange("p (h n) -> p h n", h=HEADS3)
            P_ = [probs[:, i, :].rearrange("p (q n) -> p q n", q=TQ) for i in (0, 1)]
            L_ = [[S0, S1], [O0, O1]]
            O_ = [O0, O1]
            AHEAD = 2

            def pe_program(pe):
                def main(b, following, b_next):
                    ahead = following in (3, 4)

                    def logits(h):
                        if h >= AHEAD:
                            pe.wait_ge(q_ready, h - AHEAD + 1)
                            pe.wait_ge(k_ready, h - AHEAD + 1)
                            pe.wait_ge(exp_ready, h - 1)
                        for qt in range(TQ):
                            mm = pe.matmul(L_[h % 2][qt][:, 0:T], QK[:, h % 2, 0, qt * P:(qt + 1) * P],
                                           QK[:, h % 2, 1, 0:T], start=True, stop=True)
                        mm.then_inc(logits_done, 1)

                    def turn(h):
                        pe.wait_ge(probs_ready, h + 1)
                        if h >= 1:
                            pe.wait_ge(pt_ready, h)
                        for st in range(TQ):
                            for qt in range(TQ):
                                mm = pe.transpose(T0[:, st * S + qt * P:st * S + (qt + 1) * P],
                                                  P_[h % 2][:, qt, st * P:(st + 1) * P], ident[:, :])
                        mm.then_inc(probs_flipped, 1)

                    def weigh(h):
                        pe.wait_ge(pt_ready, h + 1)
                        if h >= AHEAD:
                            pe.wait_ge(v_ready, h // 2)
                        if h >= 1:
                            pe.wait_ge(av_ready, h)
                        for st in range(TQ):
                            mm = pe.matmul(T1[:, 0:S], V_[h // 2 % 2][:, st, h % 2 * P:(h % 2 + 1) * P],
                                           PT[:, h % 2, st * S:(st + 1) * S], start=(st == 0), stop=(st == TQ - 1))
                        mm.then_inc(av_done, 1)

                    def out_of_heads(qt, heads):
                        for h in heads:
                            pe.matmul(O_[qt][:, 0:C], avT[:, h, qt * P:(qt + 1) * P], wo[:, h, :],
                                      start=(h == 0), stop=False)

                    logits(0)
                    for h in range(HEADS3):
                        if h + 1 < HEADS3:
                            logits(h + 1)
                        if h == 0:
                            project_qk(pe, a, 0, AHEAD)
                        if h == HEADS3 - AHEAD:
                            pe.wait_ge(v_ready, HEADS3 // 2 - 1)
                            front_pe(following, pe, J1, None)
                        turn(h)
                        if h == 0:
                            project_values(pe, a, 0, AHEAD)
                        elif h + AHEAD < HEADS3:
                            project_head(pe, a, h, h + AHEAD)
                        if h == HEADS3 - 1:
                            pe.wait_ge(exp_ready, HEADS3)
                            pe.wait_ge(av_ready, HEADS3 - 1)
                            out_of_heads(0, range(HEADS3 - 1))
                        weigh(h)
                        if h == HEADS3 - AHEAD and ahead:
                            pe.wait_ge(loaded[f"wide{following - 3}"], 16 * 4)
                            pe.wait_ge(hT_ready, 1)
                            pe.wait_ge(aT_ready, 1)
                            project_head(pe, following - 3, HEADS3 - 2, 0)
                    pe.wait_ge(last_ready, HEADS3)
                    pe.wait_ge(pt_ready, HEADS3)
                    for qt in range(TQ):
                        mm = pe.transpose(T0[0:17, qt * P:(qt + 1) * P], weightT[:, qt, :], ident[:, :])
                    mm.then_inc(last_flipped, 1)
                    out_of_heads(1, range(HEADS3 - 1))
                    pe.wait_ge(av_ready, HEADS3)
                    for qt in range(TQ):
                        out_of_heads(qt, [HEADS3 - 1])
                    pe.wait_ge(w17_ready, 1)
                    for qt in range(TQ):
                        mm = pe.matmul(O_[qt][:, 0:C], w17[:, qt * P:(qt + 1) * P], v17, start=False, stop=True)
                    mm.then_inc(out_done, 1)
                    if ahead:
                        project_head(pe, following - 3, HEADS3 - 1, 1)
                    if ahead and following != 3 + a:
                        bias_rows_pe(pe, following - 3)

                batches(pe, "pe", 3 + a, main)

            def act_program(act):
                def main(b, following, b_next):
                    ahead = following in (3, 4)

                    def exponents(h):
                        if h >= 2:
                            act.wait_ge(probs_flipped, h - 1)
                            act.wait_ge(last_ready, h - 1)
                        act.wait_ge(max_ready, h + 1)
                        for qt in range(TQ):
                            ins = act.activation(P_[h % 2][:, qt, 0:T], L_[h % 2][qt][:, 0:T], ACT.Exp,
                                                 bias=maxes[:, qt, h:h + 1], accum_out=sums[:, qt, h:h + 1])
                        ins.then_inc(exp_ready, 1)

                    def fetch_turned(h):
                        act.wait_ge(probs_flipped, h + 1)
                        if h >= 2:
                            act.wait_ge(av_done, h - 1)
                        act.activation(PT[:, h % 2, :], T0[:, :], ACT.Copy).then_inc(pt_ready, 1)

                    exponents(0)
                    for h in range(HEADS3):
                        fetch_turned(h)
                        if h == HEADS3 - AHEAD:
                            front_act(following, act, b_next, J1, None)
                        if h + 1 < HEADS3:
                            exponents(h + 1)
                        if h + AHEAD < HEADS3:
                            act.wait_ge(logits_done, h + 1)
                            fetch_k(act, a, h, h + AHEAD)
                        if h == HEADS3 - AHEAD:
                            if ahead:
                                fetch_k(act, following - 3, HEADS3 - 2, 0)
                    act.wait_ge(last_flipped, 1)
                    act.activation(w17, T0[0:17, 0:S], ACT.Copy).then_inc(w17_ready, 1)
                    if ahead:
                        fetch_k(act, following - 3, HEADS3 - 1, 1)
                    if ahead and following != 3 + a:
                        act.wait_ge(out_done, 1)
                        bias_rows_act(act, following - 3)

                batches(act, "act", 3 + a, main)

            def pool_program(pool):
                def main(b, following, b_next):
                    ahead = following in (3, 4)
                    pool.memset(weightT[:, :, 16:17], 1.0)
                    for h in range(HEADS3):
                        pool.wait_ge(probs_ready, h + 1)
                        pool.tensor_copy(weightT[:, :, h:h + 1], P_[h % 2][:, :, S:T]).then_inc(last_ready, 1)
                        if h == 6:
                            front_pool_first(following, pool, b_next)
                        if h == HEADS3 - AHEAD:
                            pool.wait_ge(qk_done, HEADS3 - AHEAD)
                            pool.wait_ge(v_done, HEADS3 // 2 - 1)
                            front_pool_ctx(following, pool, b_next)
                    if ahead and following != 3 + a:
                        bias_rows_pool(pool, following - 3)

                batches(pool, "pool", 3 + a, main)

            def dve_program(dve):
                def main(b, following, b_next):
                    chain = Chain(dve, dve_chain)
                    ahead = following in (3, 4)

                    def maxima(h):
                        dve.wait_ge(logits_done, h + 1)
                        for qt in range(TQ):
                            ins = dve.tensor_reduce(maxes[:, qt, h:h + 1], L_[h % 2][qt][:, 0:T], AX_X, ALU.max,
                                                    negate=True)
                        ins.then_inc(max_ready, 1)

                    def divide(h):
                        dve.wait_ge(exp_ready, h + 1)
                        chain.link(dve.reciprocal(inv[:, :, h:h + 1], sums[:, :, h:h + 1]))
                        for qt in range(TQ):
                            ins = dve.tensor_scalar(P_[h % 2][:, qt, :], P_[h % 2][:, qt, :], inv[:, qt, h:h + 1],
                                                    None, ALU.mult)
                        ins.then_inc(probs_ready, 1)

                    def fetch_av(h):
                        dve.wait_ge(av_done, h + 1)
                        dve.tensor_copy(avT[:, h, :], T1[:, 0:S]).then_inc(av_ready, 1)

                    def fetch_ahead(h):
                        dve.wait_ge(logits_done, h + 1)
                        if h % 2 == 1 and h >= 2:
                            dve.wait_ge(av_done, h - 1)
                        fetch_qv(dve, a, h, h + AHEAD)

                    maxima(0)
                    divide(0)
                    for h in range(HEADS3):
                        if h + 1 < HEADS3:
                            maxima(h + 1)
                        if h + AHEAD < HEADS3:
                            fetch_ahead(h)
                        if h + 1 < HEADS3:
                            divide(h + 1)
                        fetch_av(h)
                        if h == 4:
                            front_dve_stats(following, dve, chain, b_next)
                        if h == 5:
                            front_dve_variance(following, dve, chain)
                        if h == 6:
                            front_dve_last(following, dve, b_next)
                        if h == HEADS3 - AHEAD and ahead:
                            fetch_qv(dve, following - 3, HEADS3 - 2, 0)
                    dve.wait_ge(out_done, 1)
                    bo = row(f"L3_xattn_bo{a + 1}")
                    for qt in range(TQ):
                        ins = dve.tensor_tensor(xs[:, qt, :], O_[qt][:, 0:C], bo, ALU.add)
                    chain.link(ins)
                    dve.tensor_tensor(x_of(b), x_of(b), xs[:, :, :], ALU.add)
                    if ahead:
                        fetch_qv(dve, following - 3, HEADS3 - 1, 1)

                batches(dve, "dve", 3 + a, main)

            programs["pe"].append(pe_program)
            programs["act"].append(act_program)
            programs["pool"].append(pool_program)
            programs["dve"].append(dve_program)

        def mlp():
            fc1_done = step("fc1_done")
            gelu_ready, fc2_done, batch_done = (step(n) for n in ("gelu_ready", "fc2_done", "batch_done"))
            dve_chain = step("dve_chain")
            hidden = km0[:, 0:FF // P * S].rearrange("p (m n) -> p m n", n=S)
            banks = [J0, J1, S0, S1]

            def pe_program(pe):
                pe.wait_ge(loaded["fc"], 16 * 2)

                def main(b, following, b_next):
                    for i, bank_ in enumerate(banks):
                        project(pe, bank_, lambda k, o: fc1[:, k, (2 * i + o) * P:(2 * i + o + 1) * P],
                                hT[:, :, 0:S], 2, fc1_done)
                    front_pe(following, pe, T0, None)
                    for m in range(FF // P):
                        pe.wait_ge(gelu_ready, m + 1)
                        for t, bank_ in enumerate((O0, O1)):
                            mm = pe.matmul(bank_[:, 0:C], hidden[:, m, t * P:(t + 1) * P], fc2[:, m, :],
                                           start=(m == 0), stop=(m == FF // P - 1))
                    mm.then_inc(fc2_done, 1)

                batches(pe, "pe", 5, main)

            def act_program(act):
                def main(b, following, b_next):
                    for m in range(FF // P):
                        if m % 2 == 0:
                            act.wait_ge(fc1_done, m // 2 + 1)
                        act.activation(hidden[:, m, :], banks[m // 2][:, m % 2 * S:(m % 2 + 1) * S], ACT.Gelu,
                                       bias=fc1_cols[:, m:m + 1]).then_inc(gelu_ready, 1)
                    front_act(following, act, b_next, T0, None)

                batches(act, "act", 5, main)

            def pool_program(pool):
                def main(b, following, b_next):
                    front_pool_first(following, pool, b_next)

                batches(pool, "pool", 5, main)

            def dve_program(dve):
                def main(b, following, b_next):
                    chain = Chain(dve, dve_chain)
                    front_dve_first(following, dve, chain, b_next)
                    front_dve_last(following, dve, b_next)
                    b_fc2 = row("L3_xattn_b_fc2").unsqueeze(1).to_broadcast([P, TQ, C])
                    chain.link(dve.tensor_tensor(xs[:, :, :], x_of(b), b_fc2, ALU.add))
                    dve.wait_ge(fc2_done, 1)
                    for t, bank_ in enumerate((O0, O1)):
                        ins = dve.tensor_tensor(tile_of(x_tok, b)(t), bank_[:, 0:C], xs[:, t, :], ALU.add)
                    ins.then_inc(batch_done, 1)
                    dve.wait_ge(batch_done, 1)

                batches(dve, "dve", 5, main)

            programs["pe"].append(pe_program)
            programs["act"].append(act_program)
            programs["pool"].append(pool_program)
            programs["dve"].append(dve_program)

        small_attention(0)
        rwkv_block()
        small_attention(2)
        wide_attention(0)
        wide_attention(1)
        mlp()

        @block.sync
        def _(sp):
            def load(dst, name, group, src=None):
                sp.dma_start(dst, d[name] if src is None else src).then_inc(loaded[group], 16)

            def split_k(a):
                return a.rearrange("(k p) n -> p k n", p=P)

            def tiles(name, first, last):
                return d[name].rearrange("(t p) c -> p t c", p=P)[:, first:last, :]

            load(ctx_tok[:, 0:TQ, :], "ctx", "ctx_first", tiles("ctx", 0, TQ))
            load(x_tok[:, 0:TQ, :], "x", "x_first", tiles("x", 0, TQ))
            load(ident[:, :], "ident", "ident")
            load(mask_bytes, "mask0", "mask0", d["mask0"].rearrange("(o n) -> o n", o=1).to_broadcast([P, N]))
            for n in ("L0_k", "L0_q", "L0_v", "L0_o"):
                load(w[n], n, "w0", split_k(d[n]))
            load(cols[:, :], "cols", "const")
            load(head16[:, :], "head16", "const")
            load(head8[:, :], "head8", "const")
            load(gate[:, 0:1], "L0_xattn_gate", "const",
                 d["L0_xattn_gate"].rearrange("(o n) -> o n", o=1).to_broadcast([P, 1]))
            load(ctx_tok[:, TQ:, :], "ctx", "ctx", tiles("ctx", TQ, B * TQ))
            load(x_tok[:, TQ:, :], "x", "x", tiles("x", TQ, B * TQ))
            sp.wait_ge(loaded["w0"], 64)
            load(ctxT[:, :, :], "ctxT", "ctxT", split_k(d["ctxT"]))
            load(rows[:, :, :], "rows", "ctxT",
                 d["rows"].rearrange("(o r) n -> o r n", o=1).to_broadcast([P, len(ROWS), C]))
            load_layer1(load, split_k, lambda: sp.wait_ge(w2_cleared, 1))
            for n in ("L2_q", "L2_k", "L2_v", "L2_o"):
                load(w[n], n, "w2", split_k(d[n]))
            load(mask2, "mask2", "w2", d["mask2"].rearrange("(t p) s -> p t s", p=P))
            def store(first, last):
                sp.dma_start(out.rearrange("(t p) c -> p t c", p=P)[:, first:last, :], x_tok[:, first:last, :])\
                    .then_inc(stored, 16)

            for i in range(len(programs["pe"]) - 1):
                lead(sp, B + 1 if i == 0 else B)
                if i in (1, 2):
                    a = i - 1
                    for n, dst in zip("qkv", wide[a][:3]):
                        load(dst, f"w{n}{a + 1}", f"wide{a}", split_k(d[f"L3_xattn_w{n}{a + 1}"]))
                    load(wide[a][3], f"wo{a + 1}", f"wide{a}",
                         d[f"L3_xattn_wo{a + 1}"].rearrange("(h p) n -> p h n", p=P))
                if i == 3:
                    load(fc1, "fc1", "fc", split_k(d["L3_xattn_w_fc1"]))
                    load(fc2, "fc2", "fc", d["L3_xattn_w_fc2"].rearrange("(m p) n -> p m n", p=P))
            lead(sp, B - 1)
            store(0, (B - 1) * TQ)
            lead(sp, 1)
            store((B - 1) * TQ, B * TQ)
            sp.wait_ge(stored, 16 * 2)

        @block.tensor
        def _(pe):
            for program in programs["pe"]:
                program(pe)

        @block.vector
        def _(dve):
            for program in programs["dve"]:
                program(dve)

        @block.scalar
        def _(act):
            for program in programs["act"]:
                program(act)

        @block.gpsimd
        def _(pool):
            pool.memset(w2, 0.0).then_inc(w2_cleared, 1)
            for program in programs["pool"]:
                program(pool)


def kernel(**inputs):
    import concourse.bacc as bacc
    from concourse.bass_utils import run_bass_kernel_spmd

    a = {k: np.ascontiguousarray(v) for k, v in inputs.items()}

    def t(name):
        return np.ascontiguousarray(a[name].T)

    arrays = {
        "x": a["x"].reshape(N, C),
        "ctx": a["ctx_2048"].reshape(N, C),
        "ctxT": np.ascontiguousarray(a["ctx_2048"].reshape(N, C).T),
        "state0": np.ascontiguousarray(a["ctx_2048"][:, 2:2 + DIM1].reshape(B, KC, P, DIM1)
                                       .transpose(2, 0, 1, 3)).reshape(P, B, KC * DIM1),
        "mask0": a["mask_BxS2_bf1"].reshape(N).view(np.uint8),
        "mask2": a["mask_Bx1xSxS2_ff0"].reshape(N, S),
        "L0_xattn_gate": a["L0_xattn_gate"],
        "ident": np.eye(P, dtype=np.float32),
        "head8": np.repeat(np.eye(P // 8, dtype=np.float32), 8, axis=0),
        "head16": np.repeat(np.eye(P // 16, dtype=np.float32), 16, axis=0),
        "L0_q": t("L0_xattn_Wq"), "L0_k": t("L0_xattn_Wk"), "L0_v": t("L0_xattn_Wv"), "L0_o": t("L0_xattn_Wo"),
        "L1_r": t("L1_xattn_Wr"), "L1_k": t("L1_xattn_Wk"), "L1_v": t("L1_xattn_Wv"), "L1_g": t("L1_xattn_Wg"),
        "L1_o": t("L1_xattn_Wo"), "L1_fk": t("L1_xattn_fWk"), "L1_fr": t("L1_xattn_fWr"),
        "L1_fv": t("L1_xattn_fWv"),
        "L1_w1": a["L1_xattn_maa_w1"], "L1_w2": a["L1_xattn_maa_w2"].reshape(MIX * DMIX, C),
        "L1_dec1": a["L1_xattn_decay_w1"], "L1_dec2": a["L1_xattn_decay_w2"],
        "L2_q": a["L2_xattn_Wq"], "L2_v": a["L2_xattn_Wv"],
        "L2_k": np.repeat(a["L2_xattn_Wk"].reshape(C, KV2, 1, DIM2), HEADS2 // KV2, axis=2).reshape(C, C),
        "L2_o": a["L2_xattn_Wo"],
    }
    for n in ("wq1", "wk1", "wv1", "wo1", "wq2", "wk2", "wv2", "wo2", "w_fc1", "w_fc2"):
        arrays["L3_xattn_" + n] = a["L3_xattn_" + n]
    a["bk_of_q_heads"] = np.repeat(a["L2_xattn_bk"].reshape(KV2, 1, DIM2), HEADS2 // KV2, axis=1)
    arrays["cols"] = np.concatenate(
        [a[n].reshape(KC, P).T for n in COLS] + [a["L3_xattn_" + n].reshape(HEADS3, P).T for n in HEAD_COLS]
        + [a["L3_xattn_b_fc1"].reshape(FF // P, P).T], axis=1)
    arrays["rows"] = np.stack([np.resize(a[n], C) for n in ROWS])
    arrays = {k: np.ascontiguousarray(v) for k, v in arrays.items()}

    nc = bacc.Bacc("TRN2", target_bir_lowering=False, num_devices=1)
    dram = {k: nc.dram_tensor("in_" + k, v.shape, mybir.dt.from_np(v.dtype), kind="ExternalInput").ap()
            for k, v in arrays.items()}
    out = nc.dram_tensor("out", (N, C), F32, kind="ExternalOutput").ap()
    build(nc, dram, out)
    r = run_bass_kernel_spmd(nc, [{"in_" + k: v for k, v in arrays.items()}], core_ids=[0])
    return r.results[0]["out"].reshape(B, S, C)
```
